# Optimizing a Trainium2 kernel written in Bass

```python
import numpy as np
import jax
import jax.numpy as jnp

def _softmax(x, axis=-1):
    return jax.nn.softmax(x, axis=axis)

def _gelu(x):
    return jax.nn.gelu(x, approximate=True)

def _silu(x):
    return jax.nn.silu(x)

def _sigmoid(x):
    return jax.nn.sigmoid(x)

def _layernorm(x, axis=-1, eps=1e-05):
    m = jnp.mean(x, axis=axis, keepdims=True)
    v = jnp.var(x, axis=axis, keepdims=True)
    return (x - m) / jnp.sqrt(v + eps)

def _scatter_add(tgt, idx, src, axis=0):
    return tgt.at[idx].add(src)

def _segment_sum(src, seg, n):
    return jax.ops.segment_sum(src, seg, n)
kernel_name = 'mk_flamingo_gated_d2_seqx_r8_8fa4c2'

def setup_inputs(seed: int=0):
    np.random.seed(seed)
    _w = jnp.asarray

    def _rec_inputs():
        import jax
        import jax.numpy as jnp
        _rk = jax.random.key(seed)
        x = -0.0005207 + 1.001 * jax.random.normal(jax.random.fold_in(_rk, 1), (4, 256, 128), jnp.float32)
        _lenS = 256 - jax.random.randint(jax.random.fold_in(_rk, 7), (4,), 0, max(1, 256 // 4) + 1, jnp.int32)
        _lenS2 = 1601 - jax.random.randint(jax.random.fold_in(_rk, 8), (4,), 0, max(1, 1601 // 4) + 1, jnp.int32)
        _ctx_1024P = jax.random.normal(jax.random.fold_in(_rk, 11), (4, 16, 128), jnp.float32)
        _ctx_1024c = jax.random.dirichlet(jax.random.fold_in(_rk, 511), 0.3 * jnp.ones((16,), jnp.float32), (4, 1601))
        _ctx_1024t = jnp.einsum('bsk,bkd->bsd', _ctx_1024c, _ctx_1024P)
        _ctx_1024t = _ctx_1024t * jax.lax.rsqrt(jnp.mean(jnp.square(_ctx_1024t)) + 1e-12) * 0.953939
        ctx_1024 = -1.39393e-06 + 0.999914 * (_ctx_1024t + 0.3 * jax.random.normal(jax.random.fold_in(_rk, 611), (4, 1601, 128), jnp.float32))
        itok_BxSx64_0_2047 = jax.random.randint(jax.random.fold_in(_rk, 12), (4, 256, 64), 0, 256, jnp.int32)
        _g = jax.random.normal(jax.random.fold_in(_rk, 9001), (2, 2), jnp.float32)
        _g = jnp.sign(_g) * jnp.maximum(jnp.abs(_g), 1.0) + (_g == 0) * 1.0
        g_xattn = _g[0]
        g_ffn = _g[1]
        return (x, ctx_1024, itok_BxSx64_0_2047, g_xattn, g_ffn)
    x, ctx_1024, itok_BxSx64_0_2047, g_xattn, g_ffn = _rec_inputs()

    def _L0_xattn_setup():
        import jax, jax.numpy as jnp
        import numpy as np
        B, NQ, NKV, K = (2, 128, 256, 64)
        D, H, LAT = (128, 16, 128)
        HD = D // H
        SCALE = 1.0 / np.sqrt(HD)
        key = jax.random.key(seed)
        ks = jax.random.split(key, 7)
        s = lambda fan_in: 1.0 / np.sqrt(fan_in)
        return {'x_q': jax.random.normal(ks[0], (B, NQ, D), jnp.float32), 'x_kv': jax.random.normal(ks[1], (B, NKV, D), jnp.float32), 'indices': jax.random.randint(ks[2], (B, NQ, K), 0, NKV), 'W_q': jax.random.normal(ks[3], (D, D), jnp.float32) * s(D), 'W_kv_down': jax.random.normal(ks[4], (LAT, D), jnp.float32) * s(D), 'W_kv_up': jax.random.normal(ks[5], (2 * D, LAT), jnp.float32) * s(LAT), 'W_out': jax.random.normal(ks[6], (D, D), jnp.float32) * s(D)}
    _L0_xattn_all = _L0_xattn_setup()
    _L0_xattn_in = {k: v for k, v in _L0_xattn_all.items() if k in ('W_q', 'W_kv_down', 'W_kv_up', 'W_out')}
    del _L0_xattn_all

    def _L0_ffn_setup():
        import jax, jax.numpy as jnp
        import numpy as np
        B, S, D_MODEL, D_FF = (4, 256, 128, 512)

        def _quantum_transform(hidden, theta, w_real, w_imag):
            imag = w_imag * jnp.sin(theta + hidden * 0.1)
            quantum_phase = jnp.cos(theta) * w_real + jnp.sin(theta) * w_imag
            return hidden + quantum_phase * imag * 0.1
        key = jax.random.key(seed)
        ks = jax.random.split(key, 8)
        return {'x': jax.random.normal(ks[0], (B, S, D_MODEL), dtype=jnp.float32), 'W1': jax.random.normal(ks[1], (D_MODEL, D_FF), dtype=jnp.float32) * (1.0 / np.sqrt(D_MODEL)), 'b1': jnp.zeros((D_FF,), dtype=jnp.float32), 'quantum_phases': jax.random.normal(ks[2], (D_FF,), dtype=jnp.float32) * (2.0 * np.pi), 'quantum_weights_real': jax.random.normal(ks[3], (D_FF,), dtype=jnp.float32) * 0.1, 'quantum_weights_imag': jax.random.normal(ks[4], (D_FF,), dtype=jnp.float32) * 0.1, 'W2': jax.random.normal(ks[5], (D_FF, D_MODEL), dtype=jnp.float32) * (1.0 / np.sqrt(D_FF)), 'b2': jnp.zeros((D_MODEL,), dtype=jnp.float32)}
    _L0_ffn_all = _L0_ffn_setup()
    _L0_ffn_in = {k: v for k, v in _L0_ffn_all.items() if k in ('W1', 'b1', 'quantum_phases', 'quantum_weights_real', 'quantum_weights_imag', 'W2', 'b2')}
    del _L0_ffn_all

    def _L1_xattn_setup():
        import jax, jax.numpy as jnp
        import numpy as np
        N_HEAD, MODEL_DIM, KEY_DIM, VALUE_DIM = (16, 128, 64, 64)
        B, S = (4, 256)
        EPS = 1e-05
        TEMP = float(np.sqrt(KEY_DIM))
        key = jax.random.key(seed)
        ks = jax.random.split(key, 12)
        d = {'query': jax.random.normal(ks[0], (B, S, MODEL_DIM), jnp.float32), 'key': jax.random.normal(ks[1], (B, S, MODEL_DIM), jnp.float32), 'value': jax.random.normal(ks[2], (B, S, MODEL_DIM), jnp.float32), 'Wq': jax.random.normal(ks[3], (MODEL_DIM, N_HEAD * KEY_DIM), jnp.float32) * np.sqrt(2.0 / (MODEL_DIM + KEY_DIM)), 'bq': jnp.zeros((N_HEAD * KEY_DIM,), jnp.float32), 'Wk': jax.random.normal(ks[4], (MODEL_DIM, N_HEAD * KEY_DIM), jnp.float32) * np.sqrt(2.0 / (MODEL_DIM + KEY_DIM)), 'bk': jnp.zeros((N_HEAD * KEY_DIM,), jnp.float32), 'Wv': jax.random.normal(ks[5], (MODEL_DIM, N_HEAD * VALUE_DIM), jnp.float32) * np.sqrt(2.0 / (MODEL_DIM + VALUE_DIM)), 'bv': jnp.zeros((N_HEAD * VALUE_DIM,), jnp.float32), 'Wo': jax.random.normal(ks[6], (N_HEAD * VALUE_DIM, MODEL_DIM), jnp.float32) * np.sqrt(2.0 / (N_HEAD * VALUE_DIM + MODEL_DIM)), 'bo': jnp.zeros((MODEL_DIM,), jnp.float32), 'ln_gamma': jnp.ones((MODEL_DIM,), jnp.float32), 'ln_beta': jnp.zeros((MODEL_DIM,), jnp.float32)}
        return d
    _L1_xattn_all = _L1_xattn_setup()
    _L1_xattn_in = {k: v for k, v in _L1_xattn_all.items() if k in ('Wq', 'bq', 'Wk', 'bk', 'Wv', 'bv', 'Wo', 'bo', 'ln_gamma', 'ln_beta')}
    del _L1_xattn_all

    def _L1_ffn_setup():
        import jax, jax.numpy as jnp
        import numpy as np
        DIM = 128
        HIDDEN = 384
        SCALE = 1.0 / 127.0

        def _dequant(w_int, dtype):
            return w_int.astype(dtype) * jnp.asarray(SCALE, dtype)
        key = jax.random.key(seed)
        k_x, k_g, k_u, k_d = jax.random.split(key, 4)
        x = jax.random.normal(k_x, (4, 256, DIM), dtype=jnp.float32)
        w_gate = jax.random.randint(k_g, (HIDDEN, DIM), -127, 128, dtype=jnp.int32)
        w_up = jax.random.randint(k_u, (HIDDEN, DIM), -127, 128, dtype=jnp.int32)
        w_down = jax.random.randint(k_d, (DIM, HIDDEN), -127, 128, dtype=jnp.int32)
        return {'x': x, 'w_gate': w_gate, 'w_up': w_up, 'w_down': w_down}
    _L1_ffn_all = _L1_ffn_setup()
    _L1_ffn_in = {k: v for k, v in _L1_ffn_all.items() if k in ('w_gate', 'w_up', 'w_down')}
    del _L1_ffn_all
    return {'x': x, 'ctx_1024': ctx_1024, 'itok_BxSx64_0_2047': itok_BxSx64_0_2047, 'g_xattn': g_xattn, 'g_ffn': g_ffn, 'L0_xattn_W_q': _L0_xattn_in['W_q'], 'L0_xattn_W_kv_down': _L0_xattn_in['W_kv_down'], 'L0_xattn_W_kv_up': _L0_xattn_in['W_kv_up'], 'L0_xattn_W_out': _L0_xattn_in['W_out'], 'L0_ffn_W1': _L0_ffn_in['W1'], 'L0_ffn_b1': _L0_ffn_in['b1'], 'L0_ffn_quantum_phases': _L0_ffn_in['quantum_phases'], 'L0_ffn_quantum_weights_real': _L0_ffn_in['quantum_weights_real'], 'L0_ffn_quantum_weights_imag': _L0_ffn_in['quantum_weights_imag'], 'L0_ffn_W2': _L0_ffn_in['W2'], 'L0_ffn_b2': _L0_ffn_in['b2'], 'L1_xattn_Wq': _L1_xattn_in['Wq'], 'L1_xattn_bq': _L1_xattn_in['bq'], 'L1_xattn_Wk': _L1_xattn_in['Wk'], 'L1_xattn_bk': _L1_xattn_in['bk'], 'L1_xattn_Wv': _L1_xattn_in['Wv'], 'L1_xattn_bv': _L1_xattn_in['bv'], 'L1_xattn_Wo': _L1_xattn_in['Wo'], 'L1_xattn_bo': _L1_xattn_in['bo'], 'L1_xattn_ln_gamma': _L1_xattn_in['ln_gamma'], 'L1_xattn_ln_beta': _L1_xattn_in['ln_beta'], 'L1_ffn_w_gate': _L1_ffn_in['w_gate'], 'L1_ffn_w_up': _L1_ffn_in['w_up'], 'L1_ffn_w_down': _L1_ffn_in['w_down']}

def reference(x, ctx_1024, itok_BxSx64_0_2047, g_xattn, g_ffn, L0_xattn_W_q, L0_xattn_W_kv_down, L0_xattn_W_kv_up, L0_xattn_W_out, L0_ffn_W1, L0_ffn_b1, L0_ffn_quantum_phases, L0_ffn_quantum_weights_real, L0_ffn_quantum_weights_imag, L0_ffn_W2, L0_ffn_b2, L1_xattn_Wq, L1_xattn_bq, L1_xattn_Wk, L1_xattn_bk, L1_xattn_Wv, L1_xattn_bv, L1_xattn_Wo, L1_xattn_bo, L1_xattn_ln_gamma, L1_xattn_ln_beta, L1_ffn_w_gate, L1_ffn_w_up, L1_ffn_w_down):
    import jax
    import jax.numpy as jnp

    def _L0_xattn_ref(x_q, x_kv, indices, W_q, W_kv_down, W_kv_up, W_out):
        import jax, jax.numpy as jnp
        import numpy as np
        B, NQ, NKV, K = (2, 128, 256, 64)
        D, H, LAT = (128, 16, 128)
        HD = D // H
        SCALE = 1.0 / np.sqrt(HD)
        b, nq, d = x_q.shape
        q = (x_q @ W_q.T).reshape(b, nq, H, HD)
        c_kv = x_kv @ W_kv_down.T
        c_sel = c_kv[jnp.arange(b)[:, None, None], indices]
        kv = (c_sel @ W_kv_up.T).reshape(b, nq, K, 2, H, HD)
        k = kv[:, :, :, 0]
        v = kv[:, :, :, 1]
        scores = jnp.einsum('bqhd,bqkhd->bqkh', q, k) * SCALE
        attn = jax.nn.softmax(scores, axis=2)
        out = jnp.einsum('bqkh,bqkhd->bqhd', attn, v).reshape(b, nq, d)
        return out @ W_out.T

    def _L0_ffn_ref(x, W1, b1, quantum_phases, quantum_weights_real, quantum_weights_imag, W2, b2):
        import jax, jax.numpy as jnp
        import numpy as np
        B, S, D_MODEL, D_FF = (4, 256, 128, 512)

        def _quantum_transform(hidden, theta, w_real, w_imag):
            imag = w_imag * jnp.sin(theta + hidden * 0.1)
            quantum_phase = jnp.cos(theta) * w_real + jnp.sin(theta) * w_imag
            return hidden + quantum_phase * imag * 0.1
        hidden = jnp.einsum('bsd,df->bsf', x, W1) + b1
        q = _quantum_transform(hidden, quantum_phases, quantum_weights_real, quantum_weights_imag)
        act = jax.nn.relu(q)
        return jnp.einsum('bsf,fd->bsd', act, W2) + b2

    def _L1_xattn_ref(query, key, value, Wq, bq, Wk, bk, Wv, bv, Wo, bo, ln_gamma, ln_beta):
        import jax, jax.numpy as jnp
        import numpy as np
        N_HEAD, MODEL_DIM, KEY_DIM, VALUE_DIM = (16, 128, 64, 64)
        B, S = (4, 256)
        EPS = 1e-05
        TEMP = float(np.sqrt(KEY_DIM))
        b, sq, _ = query.shape
        residual = query
        q = (query @ Wq + bq).reshape(b, sq, N_HEAD, KEY_DIM)
        k = (key @ Wk + bk).reshape(b, key.shape[1], N_HEAD, KEY_DIM)
        v = (value @ Wv + bv).reshape(b, value.shape[1], N_HEAD, VALUE_DIM)
        scores = jnp.einsum('bqhd,bkhd->bhqk', q, k) / TEMP
        attn = jax.nn.softmax(scores, axis=-1)
        out = jnp.einsum('bhqk,bkhd->bqhd', attn, v).reshape(b, sq, N_HEAD * VALUE_DIM)
        out = out @ Wo + bo + residual
        mu = jnp.mean(out, axis=-1, keepdims=True)
        var = jnp.var(out, axis=-1, keepdims=True)
        return (out - mu) * jax.lax.rsqrt(var + EPS) * ln_gamma + ln_beta

    def _L1_ffn_ref(x, w_gate, w_up, w_down):
        import jax, jax.numpy as jnp
        import numpy as np
        DIM = 128
        HIDDEN = 384
        SCALE = 1.0 / 127.0

        def _dequant(w_int, dtype):
            return w_int.astype(dtype) * jnp.asarray(SCALE, dtype)
        wg = _dequant(w_gate, x.dtype)
        wu = _dequant(w_up, x.dtype)
        wd = _dequant(w_down, x.dtype)
        gate = jnp.einsum('bsd,hd->bsh', x, wg)
        up = jnp.einsum('bsd,hd->bsh', x, wu)
        h = jax.nn.silu(gate) * up
        return jnp.einsum('bsh,dh->bsd', h, wd)
    x = x + jnp.tanh(g_xattn[0]) * _L0_xattn_ref(_layernorm(x, axis=-1), ctx_1024, itok_BxSx64_0_2047, L0_xattn_W_q, L0_xattn_W_kv_down, L0_xattn_W_kv_up, L0_xattn_W_out)
    x = x + jnp.tanh(g_ffn[0]) * _L0_ffn_ref(_layernorm(x, axis=-1), L0_ffn_W1, L0_ffn_b1, L0_ffn_quantum_phases, L0_ffn_quantum_weights_real, L0_ffn_quantum_weights_imag, L0_ffn_W2, L0_ffn_b2)
    x = x + jnp.tanh(g_xattn[1]) * _L1_xattn_ref(_layernorm(x, axis=-1), ctx_1024, ctx_1024, L1_xattn_Wq, L1_xattn_bq, L1_xattn_Wk, L1_xattn_bk, L1_xattn_Wv, L1_xattn_bv, L1_xattn_Wo, L1_xattn_bo, L1_xattn_ln_gamma, L1_xattn_ln_beta)
    x = x + jnp.tanh(g_ffn[1]) * _L1_ffn_ref(_layernorm(x, axis=-1), L1_ffn_w_gate, L1_ffn_w_up, L1_ffn_w_down)
    return x

_drawn_inputs = setup_inputs


def setup_inputs(seed=0):
    import zlib

    import numpy as np

    out = dict(_drawn_inputs(seed))
    spreads = {'g_ffn': (-1.0, 0.2),
     'L0_ffn_b1': (0.0, 0.1),
     'L0_ffn_b2': (0.0, 0.1),
     'L1_xattn_bq': (0.0, 0.1),
     'L1_xattn_bk': (0.0, 2.0),
     'L1_xattn_bv': (0.0, 0.1),
     'L1_xattn_bo': (0.0, 0.1),
     'L1_xattn_ln_gamma': (1.0, 0.2),
     'L1_xattn_ln_beta': (0.0, 0.1)}
    factors = {'L0_ffn_quantum_phases': 8.0,
     'L0_ffn_quantum_weights_real': 40.121,
     'L0_ffn_quantum_weights_imag': 8.0}
    for name, (base, spread) in spreads.items():
        noise = np.random.default_rng([zlib.crc32(name.encode()), seed]).standard_normal(out[name].shape)
        drawn = base * np.exp(spread * noise) if base else spread * noise
        out[name] = jnp.asarray(drawn.astype(out[name].dtype))
    for name, factor in factors.items():
        out[name] = (out[name] * factor).astype(out[name].dtype)
    return out
```

```python
from contextlib import ExitStack

import numpy as np

import concourse.bass as bass
from concourse import mybir

F32 = mybir.dt.float32
F32R = mybir.dt.float32r
BF16 = mybir.dt.bfloat16
I32 = mybir.dt.int32
ALU = mybir.AluOpType
ACT = mybir.ActivationFunctionType
AX = mybir.AxisListType

P = 128
B, SQ, SKV = 4, 256, 1601
ROWS = B * SQ
NT = ROWS // P
QT = SQ // P
EPS = 1e-5
PI = float(np.pi)

H0, HD0, PICK, KEYS0 = 16, 8, 64, 256
KT0 = KEYS0 // P
SCALE0 = HD0 ** -0.5
NEVER = -1e30

H1, HD1 = 16, 64
PAIRS = H1 // 2
IT = B * PAIRS
SCALE1 = HD1 ** -0.5
NK = -(-SKV // P)
LASTK = SKV - (NK - 1) * P
SPAD = SKV + 1
CHUNK = [(0, 402), (402, 400), (802, 400), (1202, 400)]
NC = len(CHUNK)
VG = -(-NK // 4)
PACK = 3 * P + 2
PACKO = P + 1

F0, FC0 = 512, 4
F1, FC1 = 384, 3
MAGIC = 1.5 * 2.0 ** 23
TWO_PI_HI = 6.28125
TWO_PI_LO = 2 * np.pi - 6.28125
PI_DOWN = 3.1415925


def program(nc, x, ctxT, ctx0, idx, gates, wqT, wdT, wuT, woT, w1, b1, theta, wre, wim, w2, b2,
            wqkv, wout, bo, gamma, beta, wgT, wupT, wdnT, out):
    with ExitStack() as stack:
        def sb(name, shape, dt=F32):
            return stack.enter_context(nc.sbuf_tensor(name, shape, dt))

        def sem(name):
            return stack.enter_context(nc.semaphore(name))

        early = ExitStack()

        def eb(name, shape, dt=F32):
            return early.enter_context(nc.sbuf_tensor(name, shape, dt))

        X = sb("X", [P, NT, P])
        XN = sb("XN", [P, NT, P])
        XNT = sb("XNT", [P, ROWS])
        stats = sb("stats", [P, NT, 6])
        mv = sb("mv", [P, NT, 2])
        std = sb("std", [P, NT])
        rstd = sb("rstd", [P, NT])
        ident = sb("ident", [P, P])
        identb = sb("identb", [P, P], BF16)
        gate = sb("gate", [P, 4])
        graw = sb("graw", [P, 4])

        W1 = sb("W1", [P, F0])
        W2 = sb("W2", [P, FC0, P])
        fcol = sb("fcol", [P, 4, FC0])
        trig = sb("trig", [P, 8, FC0])
        B2 = sb("B2", [P, P])
        yb = sb("yb", [P, 2, 4, P])
        wi = sb("wi", [P, 2 * F1 + FC1 * P], I32)
        wf = sb("wf", [P, 2 * F1 + FC1 * P])
        Y = sb("Y", [P, NT, P])
        rowv = sb("rowv", [P, 3, P])

        w0 = eb("w0", [P, 5, P])
        C0 = eb("C0", [P, B, KEYS0])
        CKV = eb("CKV", [P, B * KEYS0])
        K0T = eb("K0T", [P, B * KEYS0])
        V0 = eb("V0", [P, B * KT0, P])
        Q0T = eb("Q0T", [P, ROWS])
        headmask = eb("headmask", [P, H0])
        QM = eb("QM", [P, 2, H0, P])
        iota_i = eb("iota_i", [P, KEYS0], I32)
        iota = eb("iota", [P, KEYS0], BF16)
        idxi = eb("idxi", [P, NT, PICK], I32)
        idxf = eb("idxf", [P, NT, PICK])
        onehot = eb("onehot", [P, PICK, KEYS0], BF16)
        count1 = eb("count1", [P, KEYS0])
        never = eb("never", [P, KEYS0])
        logc = eb("logc", [P, KEYS0])
        mask = eb("mask", [P, 2, KEYS0])
        T0 = eb("T0", [P, 2, 2, KEYS0])
        P0 = eb("P0", [P, 2, 2, KEYS0])
        P0T = eb("P0T", [P, 2, 2, KT0, P])
        mx0 = eb("mx0", [P, H0])
        nb0 = eb("nb0", [P, H0])
        sum0 = eb("sum0", [P, 2, H0])
        rec0 = eb("rec0", [P, H0])
        O0 = eb("O0", [P, H0, HD0])
        O0T = eb("O0T", [P, P])

        ff = eb("ff", [P, 2, 5, 512])
        AT = eb("AT", [P, FC0, ROWS])
        early.close()

        CT = sb("CT", [P, SPAD])
        XB = sb("XB", [P, SQ])
        WP = sb("WP", [P, 2, PACK])
        WO = sb("WO", [P, 2, PACKO])
        KA = sb("KA", [P, 2, 2, SPAD], F32R)
        KB = sb("KB", [P, 2, 2, SPAD], F32R)
        QA = sb("QA", [P, 2, 2, SQ], F32R)
        QB = sb("QB", [P, 2, 2, SQ], F32R)
        V1 = sb("V1", [P, 2, NK, 2, P])
        PR = sb("PR", [P, 2, 2 * SQ])
        negpart = sb("negpart", [P, 2 * QT, NC])
        negmax = sb("negmax", [P, 2 * QT])
        neghi = sb("neghi", [P, 2 * QT], F32R)
        negsplit = sb("negsplit", [P, 2 * QT, 2])
        recip = sb("recip", [HD1, 2 * SQ])
        ONR = sb("ONR", [P, SQ])
        ON = sb("ON", [P, SQ])

        PS = stack.enter_context(nc.psum_tensor("PS", [P, 8, 512], F32))

        s_x, s_idx, s_w0, s_ff, s_row, s_gate, s_wi = (sem(n) for n in (
            "x_loaded", "idx_loaded", "w0_loaded", "ffn_loaded", "rows_loaded", "gates_loaded",
            "int_weights_loaded"))
        s_const0, s_const = sem("const_cleared"), sem("const_ready")
        s_iota = sem("iota_ready")
        s_tanh = sem("gates_ready")
        s_ln, s_var, s_std, s_rstd, s_xn = (sem(n) for n in (
            "ln_stats", "var_ready", "std_ready", "rstd_ready", "xn_ready"))
        s_tp, s_xnt = sem("xn_transposed"), sem("xnt_stored")
        s_x0 = sem("x_updated")
        s_pro, s_proe = sem("prologue_matmuls"), sem("prologue_stored")
        s_idxf = sem("idx_float")
        s_oh, s_cnt, s_c1, s_log, s_nv, s_mask = (sem(n) for n in (
            "onehot_ready", "counts_ready", "count1_ready", "log_ready", "never_ready", "mask_ready"))
        s_qm = sem("masked_q_ready")
        s_s0, s_t0, s_nb, s_p0, s_pt, s_pts, s_o0, s_rec, s_on0, s_ot, s_ots, s_y0 = (
            sem(n) for n in ("l0_scores", "l0_max", "l0_negmax", "l0_probs", "l0_probsT",
                             "l0_probsT_stored", "l0_out", "l0_recip", "l0_normed", "l0_outT",
                             "l0_outT_stored", "l0_proj"))
        s_h, s_hid, s_dv, s_sin, s_act, s_q, s_fy, s_yb = (sem(n) for n in (
            "hidden_ready", "hidden_stored", "dve_step", "sin_ready", "act_ready", "q_ready",
            "ffn_out", "ffn_biased"))
        s_dv2 = sem("dve_chain")
        s_th, s_ths = sem("theta_reduced"), sem("theta_sin")
        s_wf = sem("int_weights_float")
        s_g, s_gs, s_ht = sem("gate_up_ready"), sem("silu_ready"), sem("h_ready")
        s_ones = sem("l1_constants")
        s_ct = sem("context_loaded")
        s_wp = [sem(f"qkv_weights_loaded{u}") for u in range(2)]
        s_wo = [sem(f"out_weights_loaded{u}") for u in range(2)]
        (s_qp, s_qh, s_ql, s_kp, s_kh, s_kl, s_vp, s_vs, s_ms, s_mr, s_nm, s_nh, s_nl, s_nt, s_nq,
         s_sc, s_pr, s_pv, s_rc, s_nr, s_bv, s_po, s_ya) = (sem(n) for n in (
            "q_projected", "q_high", "q_low", "k_projected", "k_high", "k_low", "v_projected",
            "v_stored", "max_scores", "max_reduced", "negmax_ready", "negmax_high", "negmax_split",
            "negmax_rows", "negmax_stored", "scores_ready", "probs_ready", "pv_done",
            "recip_ready", "normed", "bias_added", "pair_projected", "pair_added"))
        s_yi, s_yl, s_yg = sem("y_started"), sem("y_scaled"), sem("y_normed")
        s_out = sem("out_stored")

        block = stack.enter_context(nc.Block())

        def ln_vector(v, k, src, dst):
            for t in range(NT):
                v.bn_stats(stats[:, t, :], src[:, t, :]).then_inc(s_ln, 1)
            v.wait_ge(s_ln, 2 * NT * k + NT)
            for t in range(NT):
                v.bn_aggr(mv[:, t, :], stats[:, t, :]).then_inc(s_ln, 1)
            v.wait_ge(s_ln, 2 * NT * (k + 1))
            v.tensor_scalar(std[:, :], mv[:, :, 1], EPS, None, ALU.add).then_inc(s_var, 1)
            v.wait_ge(s_std, k + 1)
            v.reciprocal(rstd[:, :], std[:, :]).then_inc(s_rstd, 1)
            v.wait_ge(s_rstd, k + 1)
            for t in range(NT):
                v.tensor_scalar(dst[:, t, :], src[:, t, :], mv[:, t, 0:1], rstd[:, t:t + 1],
                                ALU.subtract, ALU.mult).then_inc(s_xn, 1)

        def ln_scalar(a, k):
            a.wait_ge(s_var, k + 1)
            a.activation(std[:, :], std[:, :], ACT.Sqrt).then_inc(s_std, 1)

        def transpose_tensor(pe, k, ln):
            pe.wait_ge(s_xn, NT * (ln + 1))
            for n in range(2):
                if k:
                    pe.wait_ge(s_xnt, 2 * k)
                for t in range(4 * n, 4 * n + 4):
                    last = pe.transpose(PS[:, 6 + n, (t % 4) * P:(t % 4 + 1) * P], XN[:, t, :],
                                        ident[:, :])
                last.then_inc(s_tp, 1)

        def transpose_scalar(a, k):
            for n in range(2):
                a.wait_ge(s_tp, 2 * k + n + 1)
                a.activation(XNT[:, 512 * n:512 * (n + 1)], PS[:, 6 + n, :], ACT.Copy)\
                    .then_inc(s_xnt, 1)

        @block.sync
        def _(sp):
            sp.dma_start(X[:, :, :], x.rearrange("(t p) d -> p t d", p=P)).then_inc(s_x, 16)
            sp.dma_start(idxi[:, :, :], idx.rearrange("(t p) k -> p t k", p=P)).then_inc(s_idx, 16)
            sp.dma_start(w0[:, 0, :], wqT).then_inc(s_w0, 16)
            sp.dma_start(w0[:, 1, :], wdT).then_inc(s_w0, 16)
            sp.dma_start(w0[:, 2:4, :], wuT.rearrange("l (s o) -> l s o", s=2)).then_inc(s_w0, 16)
            sp.dma_start(w0[:, 4, :], woT).then_inc(s_w0, 16)
            sp.dma_start(C0[:, :, :], ctx0.rearrange("b d k -> d b k")).then_inc(s_w0, 16)
            sp.dma_start(graw[:, :], gates.partition_broadcast(P)).then_inc(s_gate, 16)
            sp.dma_start(W1[:, :], w1).then_inc(s_ff, 16)
            sp.dma_start(W2[:, :, :], w2.rearrange("(c p) d -> p c d", p=P)).then_inc(s_ff, 16)
            for n, src in enumerate((b1, theta, wre, wim)):
                sp.dma_start(fcol[:, n, :], src).then_inc(s_ff, 16)
            sp.dma_start(B2[:, :], b2.partition_broadcast(P)).then_inc(s_ff, 16)
            for n, src in enumerate((bo, gamma, beta)):
                sp.dma_start(rowv[:, n, :], src.partition_broadcast(P)).then_inc(s_row, 16)
            sp.dma_start(wi[:, 0:F1], wgT).then_inc(s_wi, 16)
            sp.dma_start(wi[:, F1:2 * F1], wupT).then_inc(s_wi, 16)
            sp.dma_start(wi[:, 2 * F1:], wdnT).then_inc(s_wi, 16)

            def met():
                sp.wait_ge(s_xnt, 6)

            def load_batch(b):
                sp.dma_start(CT[:, :], ctxT[b]).then_inc(s_ct, 16)
                sp.dma_start(XB[:, :], XNT[:, bass.ds(b * SQ, SQ)]).then_inc(s_ct, 16)
                sp.wait_ge(s_ct, 32 * (b + 1))

            def load_pair(b, g, u):
                sp.dma_start(WP[:, u, :], wqkv[g]).then_inc(s_wp[u], 16)

            def load_out(g, u):
                sp.dma_start(WO[:, u, :], wout[g]).then_inc(s_wo[u], 16)

            sp.wait_ge(s_xnt, 6)
            load_batch(0)
            for g in range(2):
                load_pair(0, g, g)
                load_out(g, g)

            def next_pair(i, b, g, u):
                sp.wait_ge(s_vs, VG * (i - 1))
                sp.wait_ge(s_kl, NC * (i - 1))
                sp.wait_ge(s_ql, i - 1)
                met()
                load_pair(b, g, u)
                sp.wait_ge(s_po, i - 1)
                met()
                load_out(g, u)

            with sp.Fori(1, PAIRS // 2) as j:
                for u in range(2):
                    next_pair(2 * j + u, 0, 2 * j + u, u)
            for b in range(1, B):
                sp.wait_ge(s_vp, VG * PAIRS * b)
                sp.wait_ge(s_qp, PAIRS * b)
                load_batch(b)
                with sp.Fori(0, PAIRS // 2) as j:
                    for u in range(2):
                        next_pair(b * PAIRS + 2 * j + u, b, 2 * j + u, u)
            sp.wait_ge(s_x0, NT * 4)
            sp.dma_start(out.rearrange("(t p) d -> p t d", p=P), X[:, :, :]).then_inc(s_out, 16)
            sp.wait_ge(s_out, 16)

        @block.gpsimd
        def _(pool):
            pool.memset(ident[:, :], 0.0).then_inc(s_const0, 1)
            pool.memset(identb[:, :], 0.0).then_inc(s_const0, 1)
            pool.memset(headmask[:, :], 1.0).then_inc(s_const0, 1)
            pool.iota(iota_i[:, :], pattern=[[1, KEYS0]], base=0, channel_multiplier=0)\
                .then_inc(s_iota, 1)
            pool.wait_ge(s_const0, 3)
            for m in (ident, identb):
                pool.affine_select(out=m[:, :], in_=m[:, :], compare_op=ALU.not_equal, fill=1.0,
                                   base=0, pattern=[[-1, P]], channel_multiplier=1)\
                    .then_inc(s_const, 1)
            pool.affine_select(out=headmask[:, :], in_=headmask[:, :], compare_op=ALU.is_ge, fill=0.0,
                               base=0, pattern=[[-HD0, H0]], channel_multiplier=1)\
                .then_inc(s_const, 1)
            pool.wait_ge(s_const, 3)
            pool.affine_select(out=headmask[:, :], in_=headmask[:, :], compare_op=ALU.is_ge, fill=0.0,
                               base=HD0 - 1, pattern=[[HD0, H0]], channel_multiplier=-1)\
                .then_inc(s_const, 1)
            pool.wait_ge(s_const, 4)
            pool.wait_ge(s_proe, 8)

            def masked_q(t, u):
                q = Q0T[:, bass.ds(t * P, P)]
                pool.tensor_tensor(QM[:, u, :, :],
                                   q.rearrange("p (o n) -> p o n", o=1).to_broadcast([P, H0, P]),
                                   headmask[:, :].rearrange("p (h o) -> p h o", o=1)
                                   .to_broadcast([P, H0, P]), ALU.mult).then_inc(s_qm, 1)

            masked_q(0, 0)
            masked_q(1, 1)
            with pool.Fori(1, NT // 2) as j:
                for u in range(2):
                    pool.wait_ge(s_s0, 8 * (2 * j + u - 1))
                    masked_q(2 * j + u, u)
            pool.wait_ge(s_x0, 2 * NT)
            pool.memset(KB[HD1:, :, :, :].bitcast(F32), 0.0).then_inc(s_ones, 1)
            pool.wait_ge(s_ones, 1)
            pool.memset(QB[HD1:, :, :, :].bitcast(F32), 0.0).then_inc(s_ones, 1)
            pool.wait_ge(s_ones, 2)
            pool.memset(V1[:, :, :, :, HD1:], 1.0).then_inc(s_ones, 1)
            pool.wait_ge(s_ones, 3)
            pool.memset(KB[HD1:HD1 + 2, :, :, :].bitcast(F32), 1.0).then_inc(s_ones, 1)

        @block.tensor
        def _(pe):
            pe.wait_ge(s_const, 2)
            transpose_tensor(pe, 0, 0)
            pe.wait_ge(s_w0, 16 * 5)
            C0f = C0[:, :, :].rearrange("p b k -> p (b k)")
            for n in range(2):
                pe.matmul(PS[:, n, :], w0[:, 1, :], C0f[:, 512 * n:512 * (n + 1)],
                          start=True, stop=True).then_inc(s_pro, 1)
            pe.wait_ge(s_proe, 2)
            for n in range(2):
                pe.matmul(PS[:, 2 + n, :], w0[:, 2, :], CKV[:, 512 * n:512 * (n + 1)],
                          start=True, stop=True).then_inc(s_pro, 1)
            for n in range(2):
                for t in range(4 * n, 4 * n + 4):
                    last = pe.matmul(PS[:, 4 + n, (t % 4) * P:(t % 4 + 1) * P],
                                     CKV[:, t * P:(t + 1) * P], w0[:, 3, :], start=True, stop=True)
                last.then_inc(s_pro, 1)
            pe.wait_ge(s_xnt, 2)
            for n in range(2):
                pe.matmul(PS[:, n, :], w0[:, 0, :], XNT[:, 512 * n:512 * (n + 1)],
                          start=True, stop=True).then_inc(s_pro, 1)
            pe.wait_ge(s_proe, 8)

            def count_part(t, part):
                pe.wait_ge(s_oh, 8 * t + part + 1)
                if part == 0 and not (isinstance(t, int) and t == 0):
                    pe.wait_ge(s_nv, t)
                for k in range(8 * part, 8 * part + 8):
                    last = pe.matmul(PS[:, 6, 0:KEYS0], identb[:, :], onehot[:, k, :],
                                     start=(k == 0), stop=(k == PICK - 1))
                last.then_inc(s_cnt, 1)

            def scores0(t, b, u, hp):
                n = 8 * t + hp
                if hp == 0:
                    pe.wait_ge(s_qm, t + 1)
                if not (isinstance(n, int) and n < 2):
                    pe.wait_ge(s_t0, n - 1)
                for r in range(2):
                    last = pe.matmul(PS[:, hp % 2, r * KEYS0:(r + 1) * KEYS0],
                                     QM[:, u, 2 * hp + r, :], K0T[:, bass.ds(b * KEYS0, KEYS0)],
                                     start=True, stop=True)
                last.then_inc(s_s0, 1)

            def turn0(t, hp):
                n = 8 * t + hp
                pe.wait_ge(s_p0, n + 1)
                if not (isinstance(n, int) and n < 2):
                    pe.wait_ge(s_pts, n - 1)
                for r in range(2):
                    for kt in range(KT0):
                        c = (r * KT0 + kt) * P
                        last = pe.transpose(PS[:, 2 + hp % 2, c:c + P],
                                            P0[:, hp % 2, r, kt * P:(kt + 1) * P], ident[:, :])
                last.then_inc(s_pt, 1)

            def out0(t, b, hp):
                pe.wait_ge(s_pts, 8 * t + hp + 1)
                half = hp // 4
                if hp % 4 == 0 and not (isinstance(t, int) and t + half == 0):
                    pe.wait_ge(s_on0, 2 * t + half)
                for r in range(2):
                    h = 2 * (hp % 4) + r
                    for kt in range(KT0):
                        last = pe.matmul(PS[:, 4 + h // 4, (h % 4) * P:(h % 4 + 1) * P],
                                         P0T[:, hp % 2, r, kt, :], V0[:, bass.ds(b * KT0 + kt, 1), :]
                                         .rearrange("p o n -> p (o n)"),
                                         start=(kt == 0), stop=(kt == KT0 - 1))
                last.then_inc(s_o0, 1)

            def tail0(t):
                pe.wait_ge(s_on0, 2 * t + 2)
                if not (isinstance(t, int) and t == 0):
                    pe.wait_ge(s_x0, t)
                pe.transpose(PS[:, 7, 0:P], O0[:, :, :].rearrange("p h e -> p (h e)"), ident[:, :])\
                    .then_inc(s_ot, 1)
                pe.wait_ge(s_ots, t + 1)
                pe.matmul(PS[:, 7, P:2 * P], O0T[:, :], w0[:, 4, :], start=True, stop=True)\
                    .then_inc(s_y0, 1)

            def attend0(t, b, u, more):
                scores0(t, b, u, 0)
                for hp in range(8):
                    if hp < 7:
                        scores0(t, b, u, hp + 1)
                    if more:
                        count_part(t + 1, hp)
                    turn0(t, hp)
                    if hp:
                        out0(t, b, hp - 1)
                out0(t, b, 7)
                tail0(t)

            for part in range(8):
                count_part(0, part)
            attend0(0, 0, 0, True)
            with pe.Fori(0, NT // 2 - 1) as j:
                attend0(2 * j + 1, j, 1, True)
                attend0(2 * j + 2, j + 1, 0, True)
            attend0(NT - 1, B - 1, 1, False)

            transpose_tensor(pe, 1, 1)
            pe.wait_ge(s_xnt, 4)
            pe.wait_ge(s_ff, 16 * 7)
            for n in range(8):
                f, half = n // 2, n % 2
                if n >= 2:
                    pe.wait_ge(s_hid, n - 1)
                pe.matmul(PS[:, n % 2, :], W1[:, f * P:(f + 1) * P], XNT[:, 512 * half:512 * half + 512],
                          start=True, stop=True).then_inc(s_h, 1)
            pe.wait_ge(s_act, 8)
            for t in range(NT):
                for f in range(FC0):
                    last = pe.matmul(PS[:, 2 + t // 4, (t % 4) * P:(t % 4 + 1) * P],
                                     AT[:, f, t * P:(t + 1) * P], W2[:, f, :],
                                     start=(f == 0), stop=(f == FC0 - 1))
                if t % 4 == 3:
                    last.then_inc(s_fy, 1)

            transpose_tensor(pe, 2, 2)

            MAXB, SCB, OB, PJ = (0, 1), (2, 3), (4, 5), (6, 7)

            def side(s, u):
                def later(i):
                    return not (isinstance(i, int) and i <= 0)

                def q():
                    pe.wait_ge(s_wp[u], 16 * ((s - u) // 2 + 1) if isinstance(s, int) else
                               8 * (s - u) + 16)
                    if later(s):
                        pe.wait_ge(s_nq, s)
                    pe.matmul(PS[:, PJ[0], 0:SQ], WP[:, u, 0:P], XB[:, :], start=True, stop=True)\
                        .then_inc(s_qp, 1)

                def k(c):
                    def go():
                        if c == 0:
                            if later(s):
                                pe.wait_ge(s_vs, VG * s)
                        elif c == 1:
                            pe.wait_ge(s_ql, s + 1)
                            pe.wait_ge(s_qh, s + 1)
                        else:
                            pe.wait_ge(s_kl, NC * s + c - 1)
                        k0, n = CHUNK[c]
                        pe.matmul(PS[:, PJ[1 - c % 2], 0:n], WP[:, u, P:2 * P], CT[:, k0:k0 + n],
                                  start=True, stop=True).then_inc(s_kp, 1)
                    return go

                def v(g):
                    def go():
                        if g < 2:
                            pe.wait_ge(s_kl, NC * s + NC - 1 + g)
                        else:
                            pe.wait_ge(s_vs, VG * s + g - 1)
                        for kt in range(4 * g, min(4 * g + 4, NK)):
                            m = P if kt < NK - 1 else LASTK
                            last = pe.matmul(PS[0:m, PJ[1 - g % 2], (kt % 4) * P:(kt % 4 + 1) * P],
                                             CT[:, kt * P:kt * P + m], WP[:, u, 2 * P:3 * P],
                                             start=True, stop=True)
                        last.then_inc(s_vp, 1)
                    return go

                def m(n):
                    def go():
                        h, qt, c = n // (QT * NC), n // NC % QT, n % NC
                        if n == 0:
                            pe.wait_ge(s_ql, s + 1)
                            pe.wait_ge(s_kh, NC * s + NC)
                        if n >= 2 or later(s):
                            pe.wait_ge(s_mr, 16 * s + n - 1)
                        k0, cols = CHUNK[c]
                        pe.matmul(PS[:, MAXB[n % 2], 0:cols], QA[:, u, h, qt * P:(qt + 1) * P],
                                  KA[:, u, h, k0:k0 + cols], start=True, stop=True).then_inc(s_ms, 1)
                    return go

                def rows():
                    pe.wait_ge(s_nl, s + 1)
                    pe.wait_ge(s_vs, VG * s + VG)
                    for n in range(2 * QT):
                        last = pe.matmul(PS[0:2, PJ[0], n * P:(n + 1) * P], negsplit[:, n, :],
                                         ident[:, :], start=True, stop=True)
                    last.then_inc(s_nt, 1)
                return q, k, v, m, rows

            def scores(i, u, kt):
                n = NK * i + kt
                if kt == 0:
                    pe.wait_ge(s_nq, i + 1)
                    pe.wait_ge(s_kl, NC * i + NC)
                if not (isinstance(n, int) and n < 2):
                    pe.wait_ge(s_pr, n - 1)
                m = P if kt < NK - 1 else LASTK
                bank = SCB[(u + kt) % 2]
                for h in range(2):
                    o = PS[0:m, bank, h * SQ:(h + 1) * SQ]
                    pe.matmul(o, KA[:, u, h, kt * P:kt * P + m], QA[:, u, h, :], start=True, stop=False)
                    last = pe.matmul(o, KB[:, u, h, kt * P:kt * P + m], QB[:, u, h, :],
                                     start=False, stop=True)
                last.then_inc(s_sc, 1)

            def attend_v(i, u, kt, between=None):
                pe.wait_ge(s_pr, NK * i + kt + 1)
                if kt == 0:
                    pe.wait_ge(s_vs, VG * i + VG)
                    if not (isinstance(i, int) and i < 2):
                        pe.wait_ge(s_nr, i - 1)
                m = P if kt < NK - 1 else LASTK
                for h in range(2):
                    last = pe.matmul(PS[:, OB[u], h * SQ:(h + 1) * SQ], V1[0:m, u, kt, h, :],
                                     PR[0:m, (u + kt) % 2, h * SQ:(h + 1) * SQ],
                                     start=(kt == 0 and h == 0), stop=(kt == NK - 1),
                                     skip_group_check=True)
                    if h == 0 and between:
                        between()
                last.then_inc(s_pv, 1)

            def project_pair(i, u):
                pe.wait_ge(s_wo[u], 16 * (i // 2 + 1) if isinstance(i, int) else 8 * (i - u) + 16)
                pe.wait_ge(s_bv, i + 1)
                pe.wait_ge(s_vs, VG * i + 3 * VG - 1 if not isinstance(i, int) or i < IT - 2
                           else VG * IT)
                for qt in range(QT):
                    last = pe.matmul(PS[:, PJ[1], qt * P:(qt + 1) * P], ON[:, qt * P:(qt + 1) * P],
                                     WO[:, u, 0:P], start=True, stop=True)
                last.then_inc(s_po, 1)

            def step(i, u, first=False, last=False):
                pieces = {n: [] for n in range(NK + 1)}
                mids = {n: None for n in range(NK + 1)}
                if not last:
                    q, k, v, m, rows = side(i + 1, 1 - u)
                    pieces[0] = [q]
                    pieces[1] = [k(0)]
                    pieces[2] = [k(1)]
                    pieces[3] = [k(2)]
                    pieces[4] = [k(3), v(0)]
                    pieces[5] = [v(1)]
                    pieces[6] = [v(2), v(3)]
                    order = list(range(16))
                    pieces[6] = [v(2), v(3), m(order.pop(0))]
                    for n in range(7, 12):
                        pieces[n] = [m(order.pop(0)) for _ in range(2)]
                        mids[n] = m(order.pop(0))
                    pieces[13] = [rows]
                if not first:
                    pieces[8].insert(0, lambda: project_pair(i - 1, 1 - u))
                scores(i, u, 0)
                for kt in range(NK):
                    if kt + 1 < NK:
                        scores(i, u, kt + 1)
                    for piece in pieces[kt]:
                        piece()
                    attend_v(i, u, kt, mids[kt])
                for piece in pieces[NK]:
                    piece()

            pe.wait_ge(s_ones, 4)
            q, k, v, m, rows = side(0, 0)
            q()
            for c in range(NC):
                k(c)()
            for g in range(VG):
                v(g)()
            for n in range(16):
                m(n)()
            rows()
            step(0, 0, first=True)
            with pe.Fori(0, IT // 2 - 1) as j:
                step(2 * j + 1, 1)
                step(2 * j + 2, 0)
            step(IT - 1, 1, last=True)
            project_pair(IT - 1, 1)

            transpose_tensor(pe, 3, 4)
            pe.wait_ge(s_xnt, 8)
            pe.wait_ge(s_wf, 1)
            for n in range(2 * FC1):
                c, half = n // 2, n % 2
                if n >= 2:
                    pe.wait_ge(s_ht, n - 1)
                pe.matmul(PS[:, n % 2, :], wf[:, c * P:(c + 1) * P], XNT[:, 512 * half:512 * half + 512],
                          start=True, stop=True)
                pe.matmul(PS[:, 2 + n % 2, :], wf[:, F1 + c * P:F1 + (c + 1) * P],
                          XNT[:, 512 * half:512 * half + 512], start=True, stop=True).then_inc(s_g, 1)
            pe.wait_ge(s_ht, 2 * FC1)
            for t in range(NT):
                for c in range(FC1):
                    last = pe.matmul(PS[:, 4 + t // 4, (t % 4) * P:(t % 4 + 1) * P],
                                     AT[:, c, t * P:(t + 1) * P],
                                     wf[:, 2 * F1 + c * P:2 * F1 + (c + 1) * P],
                                     start=(c == 0), stop=(c == FC1 - 1))
                if t % 4 == 3:
                    last.then_inc(s_fy, 1)

        @block.scalar
        def _(a):
            a.wait_ge(s_gate, 16)
            a.activation(gate[:, :], graw[:, :], ACT.Tanh).then_inc(s_tanh, 1)
            ln_scalar(a, 0)
            transpose_scalar(a, 0)
            for n, (dst, bank) in enumerate(((CKV, 0), (CKV, 1), (K0T, 2), (K0T, 3), (V0, 4), (V0, 5),
                                             (Q0T, 0), (Q0T, 1))):
                a.wait_ge(s_pro, n + 1)
                flat = dst[:, :, :].rearrange("p t n -> p (t n)") if dst is V0 else dst[:, :]
                a.activation(flat[:, 512 * (n % 2):512 * (n % 2) + 512], PS[:, bank, :], ACT.Copy)\
                    .then_inc(s_proe, 1)

            def log_counts(t):
                a.wait_ge(s_c1, t + 1)
                a.activation(logc[:, :], count1[:, :], ACT.Ln).then_inc(s_log, 1)

            def exps0(t, u, hp):
                n = 8 * t + hp
                a.wait_ge(s_nb, n + 1)
                if not (isinstance(n, int) and n < 2):
                    a.wait_ge(s_pt, n - 1)
                if hp == 0 and not (isinstance(t, int) and t < 2):
                    a.wait_ge(s_rec, 2 * t - 2)
                for r in range(2):
                    h = 2 * hp + r
                    last = a.activation(P0[:, hp % 2, r, :], T0[:, hp % 2, r, :], ACT.Exp,
                                        bias=nb0[:, h:h + 1], accum_out=sum0[:, u, h:h + 1])
                last.then_inc(s_p0, 1)

            def store0(t, hp):
                n = 8 * t + hp
                a.wait_ge(s_pt, n + 1)
                if not (isinstance(n, int) and n < 2):
                    a.wait_ge(s_o0, n - 1)
                a.activation(P0T[:, hp % 2, :, :, :].rearrange("p r k n -> p (r k n)"),
                             PS[:, 2 + hp % 2, :], ACT.Copy).then_inc(s_pts, 1)

            def attend0(t, u, more):
                exps0(t, u, 0)
                for hp in range(8):
                    if hp < 7:
                        exps0(t, u, hp + 1)
                    store0(t, hp)
                a.wait_ge(s_ot, t + 1)
                a.activation(O0T[:, :], PS[:, 7, 0:P], ACT.Copy).then_inc(s_ots, 1)
                if more:
                    log_counts(t + 1)

            log_counts(0)
            attend0(0, 0, True)
            with a.Fori(0, NT // 2 - 1) as j:
                attend0(2 * j + 1, 1, True)
                attend0(2 * j + 2, 0, True)
            attend0(NT - 1, 1, False)

            ln_scalar(a, 1)
            a.wait_ge(s_th, 2)
            a.activation(trig[:, 4:6, :], trig[:, 2:4, :], ACT.Sin).then_inc(s_ths, 1)
            transpose_scalar(a, 1)
            for n in range(9):
                if n < 8:
                    a.wait_ge(s_h, n + 1)
                    if n >= 2:
                        a.wait_ge(s_act, n - 1)
                    a.activation(ff[:, n % 2, 0, :], PS[:, n % 2, :], ACT.Identity,
                                 bias=fcol[:, 0, n // 2:n // 2 + 1]).then_inc(s_hid, 1)
                if n:
                    m = n - 1
                    a.wait_ge(s_dv, 5 * m + 5)
                    a.activation(ff[:, m % 2, 3, :], ff[:, m % 2, 2, :], ACT.Sin).then_inc(s_sin, 1)
                    a.wait_ge(s_q, m + 1)
                    a.activation(AT[:, m // 2, 512 * (m % 2):512 * (m % 2) + 512], ff[:, m % 2, 4, :],
                                 ACT.Relu).then_inc(s_act, 1)
            ln_scalar(a, 2)
            transpose_scalar(a, 2)

            def side(s, u):
                def q():
                    a.wait_ge(s_qp, s + 1)
                    for dst in (QA, QB):
                        for h in range(2):
                            last = a.activation(dst[0:HD1, u, h, :], PS[HD1 * h:HD1 * h + HD1, 6, 0:SQ],
                                                ACT.Identity,
                                                bias=WP[HD1 * h:HD1 * h + HD1, u, 3 * P:3 * P + 1])
                    last.then_inc(s_qh, 1)

                def k(c):
                    def go():
                        a.wait_ge(s_kp, NC * s + c + 1)
                        k0, n = CHUNK[c]
                        for h in range(2):
                            for half in range(2):
                                last = a.activation(
                                    KA[HD1 * half:HD1 * half + HD1, u, h, k0:k0 + n],
                                    PS[HD1 * h:HD1 * h + HD1, 7 - c % 2, 0:n], ACT.Identity,
                                    bias=WP[HD1 * h:HD1 * h + HD1, u, 3 * P + 1:3 * P + 2])
                        last.then_inc(s_kh, 1)
                    return go

                def v(g):
                    def go():
                        a.wait_ge(s_vp, VG * s + g + 1)
                        k0, k1 = 4 * g, min(4 * g + 4, NK)
                        m = P if k1 < NK else LASTK
                        a.activation(V1[0:m, u, k0:k1, :, 0:HD1],
                                     PS[0:m, 7 - g % 2, 0:(k1 - k0) * P]
                                     .rearrange("p (k h d) -> p k h d", h=2, d=HD1), ACT.Copy)\
                            .then_inc(s_vs, 1)
                    return go
                return q, k, v

            def exps(i, u, kt):
                n = NK * i + kt
                a.wait_ge(s_sc, n + 1)
                if not (isinstance(n, int) and n < 2):
                    a.wait_ge(s_pv, n - 1)
                m = P if kt < NK - 1 else LASTK
                a.activation(PR[0:m, (u + kt) % 2, :], PS[0:m, 2 + (u + kt) % 2, :], ACT.Exp,
                             scale=SCALE1).then_inc(s_pr, 1)

            def add_bv(i, u):
                a.wait_ge(s_nr, i + 1)
                a.wait_ge(s_wo[u], 16 * (i // 2 + 1) if isinstance(i, int) else 8 * (i - u) + 16)
                if not (isinstance(i, int) and i == 0):
                    a.wait_ge(s_po, i)
                a.activation(ON[:, :], ONR[:, :], ACT.Identity, bias=WO[:, u, P:P + 1])\
                    .then_inc(s_bv, 1)

            def step(i, u, first=False, last=False):
                pieces = {n: [] for n in range(NK + 1)}
                if not last:
                    q, k, v = side(i + 1, 1 - u)
                    pieces[0] = [q]
                    pieces[1] = [k(0)]
                    pieces[2] = [k(1)]
                    pieces[3] = [k(2)]
                    pieces[4] = [k(3), v(0)]
                    pieces[5] = [v(1)]
                    pieces[6] = [v(2), v(3)]
                if not first:
                    pieces[7].insert(0, lambda: add_bv(i - 1, 1 - u))
                for kt in range(NK):
                    exps(i, u, kt)
                    for piece in pieces[kt]:
                        piece()

            q, k, v = side(0, 0)
            q()
            for c in range(NC):
                k(c)()
            for g in range(VG):
                v(g)()
            step(0, 0, first=True)
            with a.Fori(0, IT // 2 - 1) as j:
                step(2 * j + 1, 1)
                step(2 * j + 2, 0)
            step(IT - 1, 1, last=True)
            add_bv(IT - 1, 1)

            ln_scalar(a, 3)
            ln_scalar(a, 4)
            transpose_scalar(a, 3)
            for n in range(2 * FC1):
                a.wait_ge(s_g, n + 1)
                if n >= 2:
                    a.wait_ge(s_ht, n - 1)
                a.activation(ff[:, n % 2, 0, :], PS[:, n % 2, :], ACT.Silu).then_inc(s_gs, 1)

        @block.vector
        def _(v):
            v.wait_ge(s_iota, 1)
            v.tensor_copy(iota[:, :], iota_i[:, :]).then_inc(s_idxf, 1)
            v.wait_ge(s_idx, 16)
            v.tensor_copy(idxf[:, :, :], idxi[:, :, :]).then_inc(s_idxf, 1)
            v.wait_ge(s_x, 16)
            ln_vector(v, 0, X, XN)
            v.wait_ge(s_idxf, 2)

            def picks(t, part):
                if not (isinstance(t, int) and t == 0):
                    v.wait_ge(s_cnt, 8 * t - 7 + part)
                for k in range(8 * part, 8 * part + 8):
                    last = v.tensor_scalar(onehot[:, k, :], iota[:, :], idxf[:, t, k:k + 1]
                                           if isinstance(t, int) else
                                           idxf[:, bass.ds(t, 1), k:k + 1].rearrange("p o n -> p (o n)"),
                                           None, ALU.is_equal)
                last.then_inc(s_oh, 1)

            def count_mask(t, u):
                v.wait_ge(s_cnt, 8 * t + 8)
                if not (isinstance(t, int) and t == 0):
                    v.wait_ge(s_mask, t)
                v.tensor_scalar(count1[:, :], PS[:, 6, 0:KEYS0], 1.0, None, ALU.max).then_inc(s_c1, 1)
                v.tensor_scalar(never[:, :], PS[:, 6, 0:KEYS0], 0.5, NEVER, ALU.is_lt, ALU.mult)\
                    .then_inc(s_nv, 1)
                v.wait_ge(s_log, t + 1)
                v.wait_ge(s_nv, t + 1)
                v.scalar_tensor_tensor(mask[:, u, :], logc[:, :], 1.0 / SCALE0, never[:, :],
                                       ALU.mult, ALU.add).then_inc(s_mask, 1)

            def max0(t, u, hp, more):
                n = 8 * t + hp
                if hp == 0:
                    v.wait_ge(s_mask, t + 1)
                v.wait_ge(s_s0, n + 1)
                if not (isinstance(n, int) and n < 2):
                    v.wait_ge(s_p0, n - 1)
                if more:
                    picks(t + 1, hp)
                for r in range(2):
                    last = v.tensor_tensor_reduce(T0[:, hp % 2, r, :],
                                                  PS[:, hp % 2, r * KEYS0:(r + 1) * KEYS0],
                                                  mask[:, u, :], SCALE0, -3e38, ALU.add, ALU.max,
                                                  mx0[:, 2 * hp + r:2 * hp + r + 1])
                last.then_inc(s_t0, 1)
                v.wait_ge(s_t0, n + 1)
                v.tensor_scalar(nb0[:, 2 * hp:2 * hp + 2], mx0[:, 2 * hp:2 * hp + 2], -1.0, None,
                                ALU.mult).then_inc(s_nb, 1)

            def norm0(t, u, half):
                v.wait_ge(s_p0, 8 * t + 4 * half + 4)
                v.reciprocal(rec0[:, 8 * half:8 * half + 8], sum0[:, u, 8 * half:8 * half + 8])\
                    .then_inc(s_rec, 1)
                v.wait_ge(s_rec, 2 * t + half + 1)
                v.wait_ge(s_o0, 8 * t + 4 * half + 4)
                if half == 0 and not (isinstance(t, int) and t == 0):
                    v.wait_ge(s_ot, t)
                own = PS[:, 4:6, :].rearrange("p b n -> p (b n)")
                own = bass.AP(own.tensor, own.offset + 64 * half, [own.ap[0], [P + HD0, 8], [1, HD0]])
                v.tensor_tensor(O0[:, 8 * half:8 * half + 8, :], own,
                                rec0[:, 8 * half:8 * half + 8].rearrange("p (h o) -> p h o", o=1)
                                .to_broadcast([P, 8, HD0]), ALU.mult).then_inc(s_on0, 1)

            def add0(t):
                v.wait_ge(s_y0, t + 1)
                xt = X[:, bass.ds(t, 1), :].rearrange("p o n -> p (o n)")
                v.scalar_tensor_tensor(xt, PS[:, 7, P:2 * P], gate[:, 0:1], xt, ALU.mult, ALU.add)\
                    .then_inc(s_x0, 1)

            def attend0(t, u, more):
                for hp in range(8):
                    max0(t, u, hp, more)
                    if hp == 5:
                        norm0(t, u, 0)
                norm0(t, u, 1)
                if more:
                    count_mask(t + 1, 1 - u)
                add0(t)

            for part in range(8):
                picks(0, part)
            count_mask(0, 0)
            v.wait_ge(s_tanh, 1)
            attend0(0, 0, True)
            with v.Fori(0, NT // 2 - 1) as j:
                attend0(2 * j + 1, 1, True)
                attend0(2 * j + 2, 0, True)
            attend0(NT - 1, 1, False)

            v.wait_ge(s_x0, NT)
            ln_vector(v, 1, X, XN)
            v.wait_ge(s_ff, 16 * 7)

            class Steps:
                n = 0

            def chain(ins):
                Steps.n += 1
                ins.then_inc(s_dv2, 1)
                v.wait_ge(s_dv2, Steps.n)

            def reduce_angle(dst, src, tmp):
                chain(v.tensor_scalar(tmp, src, 1 / (2 * PI), MAGIC, ALU.mult, ALU.add))
                chain(v.tensor_scalar(tmp, tmp, MAGIC, None, ALU.subtract))
                chain(v.scalar_tensor_tensor(dst, tmp, -TWO_PI_HI, src, ALU.mult, ALU.add))
                chain(v.scalar_tensor_tensor(dst, tmp, -TWO_PI_LO, dst, ALU.mult, ALU.add))

            reduce_angle(trig[:, 1, :], fcol[:, 1, :], trig[:, 0, :])
            chain(v.tensor_scalar(trig[:, 3, :], trig[:, 1, :], PI / 2, None, ALU.add))
            chain(v.tensor_scalar(trig[:, 0, :], trig[:, 3, :], PI, -2 * PI, ALU.is_gt, ALU.mult))
            chain(v.tensor_tensor(trig[:, 3, :], trig[:, 3, :], trig[:, 0, :], ALU.add))
            v.tensor_scalar(trig[:, 3, :], trig[:, 3, :], PI_DOWN, -PI_DOWN, ALU.min, ALU.max)\
                .then_inc(s_th, 1)
            v.tensor_scalar(trig[:, 2, :], trig[:, 1, :], PI_DOWN, -PI_DOWN, ALU.min, ALU.max)\
                .then_inc(s_th, 1)
            v.wait_ge(s_ths, 1)
            chain(v.tensor_tensor(trig[:, 0, :], trig[:, 5, :], fcol[:, 2, :], ALU.mult))
            chain(v.tensor_tensor(trig[:, 7, :], trig[:, 4, :], fcol[:, 3, :], ALU.mult))
            chain(v.tensor_tensor(trig[:, 0, :], trig[:, 0, :], trig[:, 7, :], ALU.add))
            chain(v.tensor_tensor(trig[:, 0, :], trig[:, 0, :], fcol[:, 3, :], ALU.mult))
            chain(v.tensor_scalar(trig[:, 6, :], trig[:, 0, :], 0.1, None, ALU.mult))

            def angle(n):
                f, u = n // 2, n % 2
                v.wait_ge(s_hid, n + 1)
                hid, arg, tmp = ff[:, u, 0, :], ff[:, u, 1, :], ff[:, u, 4, :]
                step = 5 * n
                if n >= 2:
                    v.wait_ge(s_act, n - 1)
                v.tensor_scalar(arg, hid, 0.1, trig[:, 1, f:f + 1], ALU.mult, ALU.add).then_inc(s_dv, 1)
                v.wait_ge(s_dv, step + 1)
                v.tensor_scalar(tmp, arg, 1 / (2 * PI), MAGIC, ALU.mult, ALU.add).then_inc(s_dv, 1)
                v.wait_ge(s_dv, step + 2)
                chain(v.tensor_scalar(tmp, tmp, MAGIC, None, ALU.subtract))
                v.scalar_tensor_tensor(arg, tmp, -TWO_PI_HI, arg, ALU.mult, ALU.add).then_inc(s_dv, 1)
                v.wait_ge(s_dv, step + 3)
                v.scalar_tensor_tensor(arg, tmp, -TWO_PI_LO, arg, ALU.mult, ALU.add).then_inc(s_dv, 1)
                v.wait_ge(s_dv, step + 4)
                v.tensor_scalar(ff[:, u, 2, :], arg, PI_DOWN, -PI_DOWN, ALU.min, ALU.max)\
                    .then_inc(s_dv, 1)

            for n in range(9):
                if n < 8:
                    angle(n)
                if n:
                    m = n - 1
                    v.wait_ge(s_sin, m + 1)
                    v.wait_ge(s_dv, 5 * m + 5)
                    v.scalar_tensor_tensor(ff[:, m % 2, 4, :], ff[:, m % 2, 3, :],
                                           trig[:, 6, m // 2:m // 2 + 1], ff[:, m % 2, 0, :],
                                           ALU.mult, ALU.add).then_inc(s_q, 1)

            def add_ffn(n, g, bias, base):
                y = PS[:, base + n % 2, :].rearrange("p (t d) -> p t d", d=P)
                v.wait_ge(s_fy, n + 1)
                if bias:
                    v.tensor_tensor(yb[:, n, :, :], y, B2[:, :].rearrange("p (o d) -> p o d", o=1)
                                    .to_broadcast([P, 4, P]), ALU.add).then_inc(s_yb, 1)
                    v.wait_ge(s_yb, n + 1)
                    y = yb[:, n, :, :]
                xs = X[:, 4 * (n % 2):4 * (n % 2) + 4, :]
                v.scalar_tensor_tensor(xs, y, gate[:, g:g + 1], xs, ALU.mult, ALU.add)\
                    .then_inc(s_x0, 4)

            for n in range(2):
                add_ffn(n, 2, True, 2)
            v.wait_ge(s_x0, 2 * NT)
            ln_vector(v, 2, X, XN)
            v.wait_ge(s_row, 16 * 3)
            v.wait_ge(s_xn, 3 * NT)
            v.tensor_tensor(Y[:, :, :], XN[:, :, :], rowv[:, 0:1, :].to_broadcast([P, NT, P]), ALU.add)\
                .then_inc(s_yi, 1)
            v.wait_ge(s_wi, 16 * 3)
            v.tensor_scalar(wf[:, :], wi[:, :], 1.0 / 127.0, None, ALU.mult).then_inc(s_wf, 1)
            v.wait_ge(s_ones, 4)
            v.wait_ge(s_yi, 1)

            def side(s, u):
                def q():
                    v.wait_ge(s_qh, s + 1)
                    for h in range(2):
                        last = v.scalar_tensor_tensor(
                            QA[HD1:P, u, h, :], PS[HD1 * h:HD1 * h + HD1, 6, 0:SQ],
                            WP[HD1 * h:HD1 * h + HD1, u, 3 * P:3 * P + 1],
                            QA[0:HD1, u, h, :].bitcast(F32), ALU.add, ALU.subtract)
                    last.then_inc(s_ql, 1)

                def k(c):
                    def go():
                        v.wait_ge(s_kh, NC * s + c + 1)
                        k0, n = CHUNK[c]
                        for h in range(2):
                            last = v.scalar_tensor_tensor(
                                KB[0:HD1, u, h, k0:k0 + n], PS[HD1 * h:HD1 * h + HD1, 7 - c % 2, 0:n],
                                WP[HD1 * h:HD1 * h + HD1, u, 3 * P + 1:3 * P + 2],
                                KA[0:HD1, u, h, k0:k0 + n].bitcast(F32), ALU.add, ALU.subtract)
                        last.then_inc(s_kl, 1)
                    return go

                def m(n):
                    def go():
                        if n == 0 and not (isinstance(s, int) and s == 0):
                            v.wait_ge(s_nm, s)
                        v.wait_ge(s_ms, 16 * s + n + 1)
                        cols = CHUNK[n % NC][1]
                        v.tensor_reduce(negpart[:, n // NC, n % NC:n % NC + 1],
                                        PS[:, n % 2, 0:cols], AX.X, ALU.max, negate=True)\
                            .then_inc(s_mr, 1)
                    return go

                def split():
                    v.wait_ge(s_mr, 16 * s + 16)
                    if not (isinstance(s, int) and s == 0):
                        v.wait_ge(s_nl, s)
                        v.wait_ge(s_nt, s)
                    v.tensor_reduce(negmax[:, :], negpart[:, :, :], AX.X, ALU.min).then_inc(s_nm, 1)
                    v.wait_ge(s_nm, s + 1)
                    v.tensor_copy(neghi[:, :], negmax[:, :]).then_inc(s_nh, 1)
                    v.wait_ge(s_nh, s + 1)
                    v.tensor_copy(negsplit[:, :, 0], neghi[:, :].bitcast(F32))
                    v.tensor_tensor(negsplit[:, :, 1], negmax[:, :], neghi[:, :].bitcast(F32),
                                    ALU.subtract).then_inc(s_nl, 1)

                def store():
                    v.wait_ge(s_nt, s + 1)
                    for h in range(2):
                        last = v.tensor_copy(QB[HD1:HD1 + 2, u, h, :], PS[0:2, 6, h * SQ:(h + 1) * SQ])
                    last.then_inc(s_nq, 1)
                return q, k, m, split, store

            def recip_sums(i, u):
                v.wait_ge(s_pv, NK * i + NK)
                v.reciprocal(recip[:, :], PS[HD1:P, 4 + u, :]).then_inc(s_rc, 1)

            def normalise(i, u):
                v.wait_ge(s_rc, i + 1)
                if not (isinstance(i, int) and i == 0):
                    v.wait_ge(s_bv, i)
                for h in range(2):
                    last = v.tensor_tensor(ONR[HD1 * h:HD1 * h + HD1, :],
                                           PS[0:HD1, 4 + u, h * SQ:(h + 1) * SQ],
                                           recip[:, h * SQ:(h + 1) * SQ], ALU.mult)
                last.then_inc(s_nr, 1)

            def add_pair(i, b):
                v.wait_ge(s_po, i + 1)
                if not (isinstance(i, int) and i == 0):
                    v.wait_ge(s_ya, i)
                y = Y[:, bass.ds(b * QT, QT), :].rearrange("p t d -> p (t d)")
                v.tensor_tensor(y, y, PS[:, 7, 0:QT * P], ALU.add).then_inc(s_ya, 1)

            def step(i, u, b_prev, first=False, last=False):
                pieces = {n: [] for n in range(NK + 1)}
                if not last:
                    q, k, m, split, store = side(i + 1, 1 - u)
                    pieces[0] = [q]
                    pieces[1] = [k(0)]
                    pieces[2] = [k(1)]
                    pieces[3] = [k(2)]
                    pieces[4] = [k(3)]
                    pieces[6] = [m(0)]
                    for n in range(7, 12):
                        pieces[n] = [m(3 * n - 20), m(3 * n - 19), m(3 * n - 18)]
                    pieces[12] = [split]
                    pieces[13] = [store]
                if not first:
                    pieces[4].append(lambda: recip_sums(i - 1, 1 - u))
                    pieces[5].append(lambda: normalise(i - 1, 1 - u))
                    pieces[8].insert(0, lambda: add_pair(i - 1, b_prev))
                for kt in range(NK + 1):
                    for piece in pieces[kt]:
                        piece()

            q, k, m, split, store = side(0, 0)
            q()
            for c in range(NC):
                k(c)()
            for n in range(16):
                m(n)()
            split()
            store()
            step(0, 0, 0, first=True)
            with v.Fori(0, B - 1) as b:
                with v.Fori(0, PAIRS // 2) as j:
                    step(PAIRS * b + 2 * j + 1, 1, b)
                    step(PAIRS * b + 2 * j + 2, 0, b)
            with v.Fori(0, PAIRS // 2 - 1) as j:
                step(PAIRS * (B - 1) + 2 * j + 1, 1, B - 1)
                step(PAIRS * (B - 1) + 2 * j + 2, 0, B - 1)
            step(IT - 1, 1, B - 1, last=True)
            recip_sums(IT - 1, 1)
            normalise(IT - 1, 1)
            add_pair(IT - 1, B - 1)

            v.wait_ge(s_ya, IT)
            ln_vector(v, 3, Y, Y)
            v.wait_ge(s_xn, 4 * NT)
            v.tensor_tensor(Y[:, :, :], Y[:, :, :], rowv[:, 1:2, :].to_broadcast([P, NT, P]),
                            ALU.mult).then_inc(s_yl, 1)
            v.wait_ge(s_yl, 1)
            v.tensor_tensor(Y[:, :, :], Y[:, :, :], rowv[:, 2:3, :].to_broadcast([P, NT, P]),
                            ALU.add).then_inc(s_yg, 1)
            v.wait_ge(s_yg, 1)
            v.scalar_tensor_tensor(X[:, :, :], Y[:, :, :], gate[:, 1:2], X[:, :, :],
                                   ALU.mult, ALU.add).then_inc(s_x0, NT)
            v.wait_ge(s_x0, 3 * NT)
            ln_vector(v, 4, X, XN)
            for n in range(2 * FC1):
                v.wait_ge(s_gs, n + 1)
                v.tensor_tensor(AT[:, n // 2, 512 * (n % 2):512 * (n % 2) + 512], ff[:, n % 2, 0, :],
                                PS[:, 2 + n % 2, :], ALU.mult).then_inc(s_ht, 1)
            for n in range(2, 4):
                add_ffn(n, 3, False, 4)


def kernel(**inputs):
    import numpy as _np
    import concourse.bacc as _bacc
    from concourse import mybir as _mybir
    from concourse.bass_utils import run_bass_kernel_spmd as _run

    g = {k: _np.asarray(v) for k, v in inputs.items()}
    ctxT = g["ctx_1024"].transpose(0, 2, 1)
    pair = lambda w: w.reshape(P, PAIRS, P).transpose(1, 0, 2)
    cols = lambda v: v.reshape(PAIRS, P, 1)
    arrays = {
        "x": g["x"].reshape(ROWS, P),
        "ctxT": _np.concatenate([ctxT, ctxT[:, :, -1:]], axis=2),
        "ctx0": ctxT[:, :, :KEYS0],
        "idx": g["itok_BxSx64_0_2047"].reshape(ROWS, PICK),
        "gates": _np.concatenate([g["g_xattn"], g["g_ffn"]]),
        "wqT": g["L0_xattn_W_q"].T, "wdT": g["L0_xattn_W_kv_down"].T,
        "wuT": g["L0_xattn_W_kv_up"].T, "woT": g["L0_xattn_W_out"].T,
        "w1": g["L0_ffn_W1"], "b1": g["L0_ffn_b1"].reshape(FC0, P).T,
        "theta": g["L0_ffn_quantum_phases"].reshape(FC0, P).T,
        "wre": g["L0_ffn_quantum_weights_real"].reshape(FC0, P).T,
        "wim": g["L0_ffn_quantum_weights_imag"].reshape(FC0, P).T,
        "w2": g["L0_ffn_W2"], "b2": g["L0_ffn_b2"],
        "wqkv": _np.concatenate([pair(g["L1_xattn_Wq"]), pair(g["L1_xattn_Wk"]),
                                 pair(g["L1_xattn_Wv"]), cols(g["L1_xattn_bq"]),
                                 cols(g["L1_xattn_bk"])], axis=2),
        "wout": _np.concatenate([g["L1_xattn_Wo"].reshape(PAIRS, P, P), cols(g["L1_xattn_bv"])],
                                axis=2),
        "bo": g["L1_xattn_bo"], "gamma": g["L1_xattn_ln_gamma"], "beta": g["L1_xattn_ln_beta"],
        "wgT": g["L1_ffn_w_gate"].T, "wupT": g["L1_ffn_w_up"].T,
        "wdnT": g["L1_ffn_w_down"].reshape(P, FC1, P).transpose(2, 1, 0).reshape(P, FC1 * P),
    }
    arrays = {k: _np.ascontiguousarray(v) for k, v in arrays.items()}
    nc = _bacc.Bacc("TRN2", target_bir_lowering=False, num_devices=1)
    args = [nc.dram_tensor(f"in_{k}", a.shape, _mybir.dt.from_np(a.dtype), kind="ExternalInput").ap()
            for k, a in arrays.items()]
    out = nc.dram_tensor("out_0", (ROWS, P), F32, kind="ExternalOutput").ap()
    program(nc, *args, out)
    r = _run(nc, [{f"in_{k}": a for k, a in arrays.items()}], core_ids=[0])
    return r.results[0]["out_0"].reshape(B, SQ, P)
```

```python
from contextlib import ExitStack

import numpy as np

import concourse.bass as bass
from concourse import mybir

F32 = mybir.dt.float32
F32R = mybir.dt.float32r
BF16 = mybir.dt.bfloat16
I32 = mybir.dt.int32
ALU = mybir.AluOpType
ACT = mybir.ActivationFunctionType
AX = mybir.AxisListType

P = 128
B, SQ, SKV = 4, 256, 1601
ROWS = B * SQ
NT = ROWS // P
QT = SQ // P
EPS = 1e-5
PI = float(np.pi)

H0, HD0, PICK, KEYS0 = 16, 8, 64, 256
KT0 = KEYS0 // P
SCALE0 = HD0 ** -0.5
NEVER = -1e30
BLOCKS = -(-SKV // KEYS0)

H1, HD1 = 16, 64
PAIRS = H1 // 2
IT = B * PAIRS
SCALE1 = HD1 ** -0.5
NK = -(-SKV // P)
TK = SKV // NK
LASTK = SKV - (NK - 1) * TK
SPAD = SKV + 1
CHUNK = [(0, 402), (402, 400), (802, 400), (1202, 400)]
NC = len(CHUNK)
MAXAT = [(5, 1), (5, 2), (6, 0), (6, 1), (6, 2), (7, 0), (7, 1), (7, 2), (8, 0), (8, 1), (8, 2),
         (9, 0), (9, 1), (9, 2), (10, 0), (10, 1)]
VG = -(-NK // 4)
PACK = 3 * P + 2
PACKO = P + 1

F0, FC0 = 512, 4
F1, FC1 = 384, 3
MAGIC = 1.5 * 2.0 ** 23
TWO_PI_HI = 6.28125
TWO_PI_LO = 2 * np.pi - 6.28125
PI_DOWN = 3.1415925


def program(nc, x, ctxT, ctx0, idx, gates, wqT, wdT, wuT, woT, w1, b1, theta, wre, wim, w2, b2,
            wqkv, wout, bo, gamma, beta, wgT, wupT, wdnT, out):
    with ExitStack() as stack:
        def sb(name, shape, dt=F32):
            return stack.enter_context(nc.sbuf_tensor(name, shape, dt))

        def sem(name):
            return stack.enter_context(nc.semaphore(name))

        early = ExitStack()

        def eb(name, shape, dt=F32):
            return early.enter_context(nc.sbuf_tensor(name, shape, dt))

        X = sb("X", [P, NT, P])
        XN = sb("XN", [P, NT, P])
        XNT = sb("XNT", [P, ROWS])
        stats = sb("stats", [P, NT, 6])
        mv = sb("mv", [P, NT, 2])
        std = sb("std", [P, NT])
        rstd = sb("rstd", [P, NT])
        ident = sb("ident", [P, P])
        identb = sb("identb", [P, P], BF16)
        gate = sb("gate", [P, 4])
        graw = sb("graw", [P, 4])
        flag = sb("flag", [1, 1], I32)

        W1 = sb("W1", [P, F0])
        W2 = sb("W2", [P, FC0, P])
        fcol = sb("fcol", [P, 4, FC0])
        trig = sb("trig", [P, 9, FC0])
        B2 = sb("B2", [P, P])
        yb = sb("yb", [P, 2, 4, P])
        wi = sb("wi", [P, 2 * F1 + FC1 * P], I32)
        wf = sb("wf", [P, 2 * F1 + FC1 * P])
        Y = sb("Y", [P, NT, P])
        rowv = sb("rowv", [P, 3, P])

        w0 = eb("w0", [P, 5, P])
        C0 = eb("C0", [P, B, KEYS0])
        CKV = eb("CKV", [P, B * KEYS0])
        K0T = eb("K0T", [P, B * KEYS0])
        V0 = eb("V0", [P, B * KT0, P])
        Q0T = eb("Q0T", [P, ROWS])
        headmask = eb("headmask", [P, H0])
        QM = eb("QM", [P, 2, H0, P])
        iota_i = eb("iota_i", [P, KEYS0], I32)
        iota = eb("iota", [P, KEYS0], BF16)
        idxi = eb("idxi", [P, NT, PICK], I32)
        idxf = eb("idxf", [P, NT, PICK])
        onehot = eb("onehot", [P, PICK, KEYS0], BF16)
        count1 = eb("count1", [P, KEYS0])
        never = eb("never", [P, KEYS0])
        logc = eb("logc", [P, KEYS0])
        mask = eb("mask", [P, 2, KEYS0])
        T0 = eb("T0", [P, 2, 2, KEYS0])
        P0 = eb("P0", [P, 2, 2, KEYS0])
        P0T = eb("P0T", [P, 2, 2, KT0, P])
        mx0 = eb("mx0", [P, H0])
        nb0 = eb("nb0", [P, H0])
        sum0 = eb("sum0", [P, 2, H0])
        rec0 = eb("rec0", [P, H0])
        O0 = eb("O0", [P, H0, HD0])
        O0T = eb("O0T", [P, P])

        flags = eb("flags", [P, 4])
        flagrow = eb("flagrow", [1, P])
        away = eb("away", [P, NT, PICK])
        GC = eb("GC", [P, KEYS0])
        GCKV = eb("GCKV", [P, KEYS0])
        gidx = eb("gidx", [P, PICK])
        gbest = eb("gbest", [P, 2, H0])
        gneg = eb("gneg", [P, H0])
        gshrink = eb("gshrink", [P, 2, H0])
        gpart = eb("gpart", [P, H0])
        gsum = eb("gsum", [P, H0])
        gacc = eb("gacc", [P, H0, HD0])
        gown = eb("gown", [P, H0, HD0])

        ff = eb("ff", [P, 3, 5, 512])
        AT = eb("AT", [P, FC0, ROWS])
        early.close()

        KB = sb("KB", [P, 2, 2, SPAD], F32R)
        QB = sb("QB", [P, 2, 2, SQ], F32R)
        VH = sb("VH", [P, 2, NK, 2, P], F32R)
        VL = sb("VL", [P, 2, NK, 2, P], F32R)
        CT = sb("CT", [P, SPAD])
        WP = sb("WP", [P, 2, PACK])
        XB = sb("XB", [P, SQ])
        WO = sb("WO", [P, 2, PACKO])
        KA = sb("KA", [P, 2, 2, SPAD], F32R)
        QA = sb("QA", [P, 2, 2, SQ], F32R)
        PR = sb("PR", [P, 2, 2 * SQ])
        PH = sb("PH", [P, 2, 2 * SQ], F32R)
        PL = sb("PL", [P, 2, 2 * SQ], F32R)
        negpart = sb("negpart", [P, 2 * QT, NC])
        negmax = sb("negmax", [P, 2 * QT])
        neghi = sb("neghi", [P, 2 * QT], F32R)
        negsplit = sb("negsplit", [P, 2 * QT, 2])
        sums = sb("sums", [P, SQ])
        recip = sb("recip", [P, SQ])
        ONR = sb("ONR", [P, SQ])
        ON = sb("ON", [P, SQ])

        PS = stack.enter_context(nc.psum_tensor("PS", [P, 8, 512], F32))

        s_x, s_idx, s_w0, s_ff, s_row, s_gate, s_wi = (sem(n) for n in (
            "x_loaded", "idx_loaded", "w0_loaded", "ffn_loaded", "rows_loaded", "gates_loaded",
            "int_weights_loaded"))
        s_const0, s_const = sem("const_cleared"), sem("const_ready")
        s_iota = sem("iota_ready")
        s_tanh = sem("gates_ready")
        s_ln, s_var, s_std, s_rstd, s_xn = (sem(n) for n in (
            "ln_stats", "var_ready", "std_ready", "rstd_ready", "xn_ready"))
        s_tp, s_xnt = sem("xn_transposed"), sem("xnt_stored")
        s_x0 = sem("x_updated")
        s_pro, s_proe = sem("prologue_matmuls"), sem("prologue_stored")
        s_idxf = sem("idx_float")
        s_oh, s_cnt, s_c1, s_log, s_nv, s_mask = (sem(n) for n in (
            "onehot_ready", "counts_ready", "count1_ready", "log_ready", "never_ready", "mask_ready"))
        s_qm = sem("masked_q_ready")
        s_s0, s_t0, s_nb, s_p0, s_pt, s_pts, s_o0, s_rec, s_on0, s_ot, s_ots, s_y0 = (
            sem(n) for n in ("l0_scores", "l0_max", "l0_negmax", "l0_probs", "l0_probsT",
                             "l0_probsT_stored", "l0_out", "l0_recip", "l0_normed", "l0_outT",
                             "l0_outT_stored", "l0_proj"))
        s_range, s_rrow, s_flag = sem("pick_range"), sem("pick_range_row"), sem("flag_ready")
        (g_xl, g_go, g_qm, g_ctx, g_ckv, g_ckvs, g_kv, g_kvs, g_oh, g_cnt, g_c1, g_nv, g_log,
         g_mask, g_s, g_t, g_best, g_shr, g_p, g_pt, g_pts, g_o, g_step, g_norm, g_ot,
         g_ots, g_y, g_x) = (sem("all_" + n) for n in (
            "x_loaded", "block_started", "masked_q", "context", "ckv", "ckv_stored", "kv", "kv_stored",
            "onehot", "counts", "count1", "never", "log", "mask", "scores", "max", "best",
            "shrink", "probs", "probsT", "probsT_stored", "out", "vector_step",
            "normed", "outT", "outT_stored", "projected", "x_updated"))
        s_red = sem("angle_reduced")
        s_h, s_hid, s_dv, s_sin, s_act, s_q, s_fy, s_yb = (sem(n) for n in (
            "hidden_ready", "hidden_stored", "angle_ready", "sin_ready", "act_ready", "q_ready",
            "ffn_out", "ffn_biased"))
        s_dv2 = sem("dve_chain")
        s_th, s_ths = sem("theta_reduced"), sem("theta_sin")
        s_wf = sem("int_weights_float")
        s_g, s_gs, s_ht = sem("gate_up_ready"), sem("silu_ready"), sem("h_ready")
        s_ones = sem("l1_constants")
        s_ct = sem("context_loaded")
        s_wp = [sem(f"qkv_weights_loaded{u}") for u in range(2)]
        s_wo = [sem(f"out_weights_loaded{u}") for u in range(2)]
        (s_qp, s_qh, s_ql, s_kp, s_kh, s_kl, s_vp, s_vs, s_ms, s_mr, s_nm, s_nh, s_nl, s_nt, s_nq,
         s_sc, s_pr, s_ph, s_pl, s_pv, s_pvl, s_vl, s_rc, s_nr, s_bv, s_po, s_ya) = (sem(n) for n in (
            "q_projected", "q_high", "q_low", "k_projected", "k_high", "k_low", "v_projected",
            "v_stored", "max_scores", "max_reduced", "negmax_ready", "negmax_high", "negmax_split",
            "negmax_rows", "negmax_stored", "scores_ready", "probs_ready", "probs_high",
            "probs_low", "pv_high_done", "pv_low_done", "v_low",
            "recip_ready", "normed", "bias_added", "pair_projected", "pair_added"))
        s_dup = [[sem(f"k_high_twice{u}{half}") for half in range(2)] for u in range(2)]
        s_su = sem("sums_copied")
        s_yi, s_yl, s_yg = sem("y_started"), sem("y_scaled"), sem("y_normed")
        s_out = sem("out_stored")

        block = stack.enter_context(nc.Block())

        def outside(engine):
            engine.wait_ge(s_flag, 1)
            return engine.value_load(flag[0:1, 0:1], min_val=0, max_val=1)

        def all_blocks(engine, before, tile_start, block, tile_end, after=lambda: None):
            with engine.If(outside(engine) >= 1):
                before()
                with engine.Fori(0, B) as b:
                    with engine.Fori(0, QT) as q:
                        t = b * QT + q
                        tile_start(t)
                        with engine.Fori(0, BLOCKS) as j:
                            block(b, t, j, t * BLOCKS + j)
                        tile_end(t)
                after()

        def nothing(*_):
            pass

        ALLP = AT[:, :, :].rearrange("p f n -> p (f n)").rearrange("p (h k) -> p h k", k=KEYS0)

        def ln_vector(v, k, src, dst):
            for t in range(NT):
                v.bn_stats(stats[:, t, :], src[:, t, :]).then_inc(s_ln, 1)
            v.wait_ge(s_ln, 2 * NT * k + NT)
            for t in range(NT):
                v.bn_aggr(mv[:, t, :], stats[:, t, :]).then_inc(s_ln, 1)
            v.wait_ge(s_ln, 2 * NT * (k + 1))
            v.tensor_scalar(std[:, :], mv[:, :, 1], EPS, None, ALU.add).then_inc(s_var, 1)
            v.wait_ge(s_std, k + 1)
            v.reciprocal(rstd[:, :], std[:, :]).then_inc(s_rstd, 1)
            v.wait_ge(s_rstd, k + 1)
            for t in range(NT):
                v.tensor_scalar(dst[:, t, :], src[:, t, :], mv[:, t, 0:1], rstd[:, t:t + 1],
                                ALU.subtract, ALU.mult).then_inc(s_xn, 1)

        def ln_scalar(a, k):
            a.wait_ge(s_var, k + 1)
            a.activation(std[:, :], std[:, :], ACT.Sqrt).then_inc(s_std, 1)

        def transpose_tensor(pe, k, ln):
            pe.wait_ge(s_xn, NT * (ln + 1))
            for n in range(2):
                if k:
                    pe.wait_ge(s_xnt, 2 * k)
                for t in range(4 * n, 4 * n + 4):
                    last = pe.transpose(PS[:, 6 + n, (t % 4) * P:(t % 4 + 1) * P], XN[:, t, :],
                                        ident[:, :])
                last.then_inc(s_tp, 1)

        def transpose_scalar(a, k):
            for n in range(2):
                a.wait_ge(s_tp, 2 * k + n + 1)
                a.activation(XNT[:, 512 * n:512 * (n + 1)], PS[:, 6 + n, :], ACT.Copy)\
                    .then_inc(s_xnt, 1)

        @block.sync
        def _(sp):
            sp.dma_start(X[:, :, :], x.rearrange("(t p) d -> p t d", p=P)).then_inc(s_x, 16)
            sp.dma_start(idxi[:, :, :], idx.rearrange("(t p) k -> p t k", p=P)).then_inc(s_idx, 16)
            sp.dma_start(w0[:, 0, :], wqT).then_inc(s_w0, 16)
            sp.dma_start(w0[:, 1, :], wdT).then_inc(s_w0, 16)
            sp.dma_start(w0[:, 2:4, :], wuT.rearrange("l (s o) -> l s o", s=2)).then_inc(s_w0, 16)
            sp.dma_start(w0[:, 4, :], woT).then_inc(s_w0, 16)
            sp.dma_start(C0[:, :, :], ctx0[:, :, 0:KEYS0].rearrange("b d k -> d b k")).then_inc(s_w0, 16)
            sp.dma_start(graw[:, :], gates.partition_broadcast(P)).then_inc(s_gate, 16)
            sp.dma_start(W1[:, :], w1).then_inc(s_ff, 16)
            sp.dma_start(W2[:, :, :], w2.rearrange("(c p) d -> p c d", p=P)).then_inc(s_ff, 16)
            for n, src in enumerate((b1, theta, wre, wim)):
                sp.dma_start(fcol[:, n, :], src).then_inc(s_ff, 16)
            sp.dma_start(B2[:, :], b2.partition_broadcast(P)).then_inc(s_ff, 16)
            for n, src in enumerate((bo, gamma, beta)):
                sp.dma_start(rowv[:, n, :], src.partition_broadcast(P)).then_inc(s_row, 16)
            sp.dma_start(wi[:, 0:F1], wgT).then_inc(s_wi, 16)
            sp.dma_start(wi[:, F1:2 * F1], wupT).then_inc(s_wi, 16)
            sp.dma_start(wi[:, 2 * F1:], wdnT).then_inc(s_wi, 16)

            def reload():
                sp.wait_ge(s_x0, NT)
                sp.dma_start(X[:, :, :], x.rearrange("(t p) d -> p t d", p=P)).then_inc(g_xl, 16)

            def load_block(b, t, j, n):
                sp.wait_ge(g_go, n + 1)
                sp.dma_start(GC[:, :], ctx0[b, :, bass.ds(j * KEYS0, KEYS0)]).then_inc(g_ctx, 16)

            all_blocks(sp, reload, nothing, load_block, nothing)

            def met():
                sp.wait_ge(s_xnt, 6)

            def load_batch(b):
                if b:
                    sp.dma_start(CT[:, :], ctxT[b]).then_inc(s_ct, 16)
                sp.dma_start(XB[:, :], XNT[:, bass.ds(b * SQ, SQ)]).then_inc(s_ct, 16)
                sp.wait_ge(s_ct, 32 * (b + 1))

            def load_pair(g, u):
                sp.dma_start(WP[:, u, :], wqkv[g]).then_inc(s_wp[u], 16)

            def load_out(g, u):
                sp.dma_start(WO[:, u, :], wout[g]).then_inc(s_wo[u], 16)

            def duplicate(s, u):
                for half, (k0, k1) in enumerate(((0, CHUNK[2][0]), (CHUNK[2][0], SPAD))):
                    sp.wait_ge(s_kh, NC * s + 2 * half + 2)
                    for h in range(2):
                        sp.dma_start(KA[HD1:P, u, h, k0:k1].bitcast(F32),
                                     KA[0:HD1, u, h, k0:k1].bitcast(F32)).then_inc(s_dup[u][half], 16)
                    if half == 0:
                        sp.dma_start(QB[0:HD1, u, :, :].bitcast(F32),
                                     QA[0:HD1, u, :, :].bitcast(F32)).then_inc(s_dup[u][half], 16)

            def feed(s, g, u, last=False):
                duplicate(s, u)
                if not last:
                    if not (isinstance(s, int) and s == 0):
                        sp.wait_ge(s_vl, VG * s)
                        sp.wait_ge(s_kl, NC * s)
                        sp.wait_ge(s_ql, s)
                        met()
                    load_pair(g + 1, 1 - u)
                if not (isinstance(s, int) and s < 2):
                    sp.wait_ge(s_po, s - 1)
                    met()
                load_out(g, u)

            sp.wait_ge(s_xn, 2 * NT)
            sp.dma_start(CT[:, :], ctxT[0]).then_inc(s_ct, 16)
            load_pair(0, 0)
            sp.wait_ge(s_xnt, 6)
            load_batch(0)
            for b in range(B):
                s0 = PAIRS * b
                if b:
                    sp.wait_ge(s_vp, VG * s0)
                    sp.wait_ge(s_qp, s0)
                    load_batch(b)
                    sp.wait_ge(s_vl, VG * s0 - VG)
                    sp.wait_ge(s_kl, NC * s0 - NC)
                    load_pair(0, 0)
                feed(s0, 0, 0)
                feed(s0 + 1, 1, 1)
                with sp.Fori(1, PAIRS // 2 - 1) as j:
                    for u in range(2):
                        feed(s0 + 2 * j + u, 2 * j + u, u)
                feed(s0 + PAIRS - 2, PAIRS - 2, 0)
                feed(s0 + PAIRS - 1, PAIRS - 1, 1, last=True)
            sp.wait_ge(s_x0, NT * 4)
            sp.dma_start(out.rearrange("(t p) d -> p t d", p=P), X[:, :, :]).then_inc(s_out, 16)
            sp.wait_ge(s_out, 16)

        @block.gpsimd
        def _(pool):
            pool.memset(ident[:, :], 0.0).then_inc(s_const0, 1)
            pool.memset(identb[:, :], 0.0).then_inc(s_const0, 1)
            pool.memset(headmask[:, :], 1.0).then_inc(s_const0, 1)
            pool.iota(iota_i[:, :], pattern=[[1, KEYS0]], base=0, channel_multiplier=0)\
                .then_inc(s_iota, 1)
            pool.wait_ge(s_const0, 3)
            for m in (ident, identb):
                pool.affine_select(out=m[:, :], in_=m[:, :], compare_op=ALU.not_equal, fill=1.0,
                                   base=0, pattern=[[-1, P]], channel_multiplier=1)\
                    .then_inc(s_const, 1)
            pool.affine_select(out=headmask[:, :], in_=headmask[:, :], compare_op=ALU.is_ge, fill=0.0,
                               base=0, pattern=[[-HD0, H0]], channel_multiplier=1)\
                .then_inc(s_const, 1)
            pool.wait_ge(s_const, 3)
            pool.affine_select(out=headmask[:, :], in_=headmask[:, :], compare_op=ALU.is_ge, fill=0.0,
                               base=HD0 - 1, pattern=[[HD0, H0]], channel_multiplier=-1)\
                .then_inc(s_const, 1)
            pool.wait_ge(s_const, 4)
            pool.wait_ge(s_proe, 8)

            def masked_q(t, u):
                q = Q0T[:, bass.ds(t * P, P)]
                pool.tensor_tensor(QM[:, u, :, :],
                                   q.rearrange("p (o n) -> p o n", o=1).to_broadcast([P, H0, P]),
                                   headmask[:, :].rearrange("p (h o) -> p h o", o=1)
                                   .to_broadcast([P, H0, P]), ALU.mult).then_inc(s_qm, 1)

            masked_q(0, 0)
            masked_q(1, 1)
            with pool.Fori(1, NT // 2) as j:
                for u in range(2):
                    pool.wait_ge(s_s0, 8 * (2 * j + u - 1))
                    masked_q(2 * j + u, u)
            pool.wait_ge(s_xn, 2 * NT)
            for n in range(8):
                pool.wait_ge(s_red, n + 1)
                if n:
                    pool.wait_ge(s_dv, n)
                pool.tensor_scalar(ff[:, n % 3, 2, :], ff[:, n % 3, 1, :], PI_DOWN, -PI_DOWN, ALU.min,
                                   ALU.max).then_inc(s_dv, 1)
            pool.wait_ge(s_dv, 8)
            pool.memset(KB[HD1:, :, :, :].bitcast(F32), 0.0).then_inc(s_ones, 1)
            pool.wait_ge(s_ones, 1)
            pool.memset(QB[HD1:, :, :, :].bitcast(F32), 0.0).then_inc(s_ones, 1)
            pool.wait_ge(s_ones, 2)
            pool.memset(VH[:, :, :, :, HD1:].bitcast(F32), 1.0).then_inc(s_ones, 1)
            pool.wait_ge(s_ones, 3)
            pool.memset(VL[:, :, :, :, HD1:].bitcast(F32), 0.0).then_inc(s_ones, 1)
            pool.wait_ge(s_ones, 4)
            pool.memset(KB[HD1:HD1 + 2, :, :, :].bitcast(F32), 1.0).then_inc(s_ones, 1)

            def low_part(i, u, kt):
                n = NK * i + kt
                pool.wait_ge(s_pr, n + 1)
                if not (isinstance(n, int) and n < 2):
                    pool.wait_ge(s_pvl, n - 1)
                m = TK if kt < NK - 1 else LASTK
                c = (u + kt) % 2
                pool.tensor_tensor(PL[0:m, c, :], PR[0:m, c, :], PH[0:m, c, :].bitcast(F32),
                                   ALU.subtract).then_inc(s_pl, 1)

            for kt in range(NK):
                low_part(0, 0, kt)
            with pool.Fori(0, IT // 2 - 1) as j:
                for u in (1, 0):
                    for kt in range(NK):
                        low_part(2 * j + 2 - u, u, kt)
            for kt in range(NK):
                low_part(IT - 1, 1, kt)

        @block.tensor
        def _(pe):
            pe.wait_ge(s_const, 2)
            transpose_tensor(pe, 0, 0)
            pe.wait_ge(s_w0, 16 * 5)
            C0f = C0[:, :, :].rearrange("p b k -> p (b k)")
            for n in range(2):
                pe.matmul(PS[:, n, :], w0[:, 1, :], C0f[:, 512 * n:512 * (n + 1)],
                          start=True, stop=True).then_inc(s_pro, 1)
            pe.wait_ge(s_proe, 2)
            for n in range(2):
                pe.matmul(PS[:, 2 + n, :], w0[:, 2, :], CKV[:, 512 * n:512 * (n + 1)],
                          start=True, stop=True).then_inc(s_pro, 1)
            for n in range(2):
                for t in range(4 * n, 4 * n + 4):
                    last = pe.matmul(PS[:, 4 + n, (t % 4) * P:(t % 4 + 1) * P],
                                     CKV[:, t * P:(t + 1) * P], w0[:, 3, :], start=True, stop=True)
                last.then_inc(s_pro, 1)
            pe.wait_ge(s_xnt, 2)
            for n in range(2):
                pe.matmul(PS[:, n, :], w0[:, 0, :], XNT[:, 512 * n:512 * (n + 1)],
                          start=True, stop=True).then_inc(s_pro, 1)
            pe.wait_ge(s_proe, 8)

            def count_part(t, part):
                pe.wait_ge(s_oh, 8 * t + part + 1)
                if part == 0 and not (isinstance(t, int) and t == 0):
                    pe.wait_ge(s_nv, t)
                for k in range(8 * part, 8 * part + 8):
                    last = pe.matmul(PS[:, 6, 0:KEYS0], identb[:, :], onehot[:, k, :],
                                     start=(k == 0), stop=(k == PICK - 1))
                last.then_inc(s_cnt, 1)

            def scores0(t, b, u, hp):
                n = 8 * t + hp
                if hp == 0:
                    pe.wait_ge(s_qm, t + 1)
                if not (isinstance(n, int) and n < 2):
                    pe.wait_ge(s_t0, n - 1)
                for r in range(2):
                    last = pe.matmul(PS[:, hp % 2, r * KEYS0:(r + 1) * KEYS0],
                                     QM[:, u, 2 * hp + r, :], K0T[:, bass.ds(b * KEYS0, KEYS0)],
                                     start=True, stop=True)
                last.then_inc(s_s0, 1)

            def turn0(t, hp):
                n = 8 * t + hp
                pe.wait_ge(s_p0, n + 1)
                if not (isinstance(n, int) and n < 2):
                    pe.wait_ge(s_pts, n - 1)
                for r in range(2):
                    for kt in range(KT0):
                        c = (r * KT0 + kt) * P
                        last = pe.transpose(PS[:, 2 + hp % 2, c:c + P],
                                            P0[:, hp % 2, r, kt * P:(kt + 1) * P], ident[:, :])
                last.then_inc(s_pt, 1)

            def out0(t, b, hp):
                pe.wait_ge(s_pts, 8 * t + hp + 1)
                half = hp // 4
                if hp % 4 == 0 and not (isinstance(t, int) and t + half == 0):
                    pe.wait_ge(s_on0, 2 * t + half)
                for r in range(2):
                    h = 2 * (hp % 4) + r
                    for kt in range(KT0):
                        last = pe.matmul(PS[:, 4 + h // 4, (h % 4) * P:(h % 4 + 1) * P],
                                         P0T[:, hp % 2, r, kt, :], V0[:, bass.ds(b * KT0 + kt, 1), :]
                                         .rearrange("p o n -> p (o n)"),
                                         start=(kt == 0), stop=(kt == KT0 - 1))
                last.then_inc(s_o0, 1)

            def tail0(t):
                pe.wait_ge(s_on0, 2 * t + 2)
                if not (isinstance(t, int) and t == 0):
                    pe.wait_ge(s_x0, t)
                pe.transpose(PS[:, 7, 0:P], O0[:, :, :].rearrange("p h e -> p (h e)"), ident[:, :])\
                    .then_inc(s_ot, 1)
                pe.wait_ge(s_ots, t + 1)
                pe.matmul(PS[:, 7, P:2 * P], O0T[:, :], w0[:, 4, :], start=True, stop=True)\
                    .then_inc(s_y0, 1)

            def attend0(t, b, u, more):
                scores0(t, b, u, 0)
                for hp in range(8):
                    if hp < 7:
                        scores0(t, b, u, hp + 1)
                    if more:
                        count_part(t + 1, hp)
                    turn0(t, hp)
                    if hp:
                        out0(t, b, hp - 1)
                out0(t, b, 7)
                tail0(t)

            for part in range(8):
                count_part(0, part)
            pe.wait_ge(s_range, 1)
            pe.transpose(PS[0:1, 7, 0:P], flags[:, 2:3], ident[:, :]).then_inc(s_rrow, 1)
            attend0(0, 0, 0, True)
            with pe.Fori(0, NT // 2 - 1) as j:
                attend0(2 * j + 1, j, 1, True)
                attend0(2 * j + 2, j + 1, 0, True)
            attend0(NT - 1, B - 1, 1, False)

            def block(b, t, j, n):
                pe.wait_ge(g_go, n + 1)
                pe.wait_ge(g_ctx, 16 * n + 16)
                pe.matmul(PS[:, 0, 0:KEYS0], w0[:, 1, :], GC[:, :], start=True, stop=True)\
                    .then_inc(g_ckv, 1)
                pe.wait_ge(g_ckvs, n + 1)
                pe.matmul(PS[:, 0, KEYS0:2 * KEYS0], w0[:, 2, :], GCKV[:, :], start=True, stop=True)
                for kt in range(KT0):
                    last = pe.matmul(PS[:, 1, kt * P:(kt + 1) * P], GCKV[:, kt * P:(kt + 1) * P],
                                     w0[:, 3, :], start=True, stop=True)
                last.then_inc(g_kv, 1)
                pe.wait_ge(g_oh, n + 1)
                for k in range(PICK):
                    last = pe.matmul(PS[:, 6, 0:KEYS0], identb[:, :], onehot[:, k, :],
                                     start=(k == 0), stop=(k == PICK - 1))
                last.then_inc(g_cnt, 1)
                pe.wait_ge(g_kvs, n + 1)
                pe.wait_ge(g_qm, t + 1)
                for hp in range(8):
                    if hp:
                        pe.wait_ge(g_t, 8 * n + hp)
                    for r in range(2):
                        last = pe.matmul(PS[:, 0, r * KEYS0:(r + 1) * KEYS0], QM[:, 0, 2 * hp + r, :],
                                         K0T[:, 0:KEYS0], start=True, stop=True)
                    last.then_inc(g_s, 1)
                pe.wait_ge(g_p, n + 1)
                for hp in range(8):
                    for r in range(2):
                        for kt in range(KT0):
                            c = (r * KT0 + kt) * P
                            last = pe.transpose(PS[:, 1, c:c + P],
                                                ALLP[:, 2 * hp + r, kt * P:(kt + 1) * P], ident[:, :])
                    last.then_inc(g_pt, 1)
                    pe.wait_ge(g_pts, 8 * n + hp + 1)
                    for r in range(2):
                        h = 2 * hp + r
                        for kt in range(KT0):
                            last = pe.matmul(PS[:, 2 + h // 4, (h % 4) * P:(h % 4 + 1) * P],
                                             P0T[:, 0, r, kt, :], V0[:, kt, :],
                                             start=(kt == 0), stop=(kt == KT0 - 1))
                    last.then_inc(g_o, 1)

            def project(t):
                pe.wait_ge(g_norm, t + 1)
                pe.transpose(PS[:, 7, 0:P], O0[:, :, :].rearrange("p h e -> p (h e)"), ident[:, :])\
                    .then_inc(g_ot, 1)
                pe.wait_ge(g_ots, t + 1)
                pe.matmul(PS[:, 7, P:2 * P], O0T[:, :], w0[:, 4, :], start=True, stop=True)\
                    .then_inc(g_y, 1)

            all_blocks(pe, nothing, nothing, block, project)

            transpose_tensor(pe, 1, 1)
            pe.wait_ge(s_xnt, 4)
            pe.wait_ge(s_ff, 16 * 7)

            def second(n):
                f, half = n // 2, n % 2
                pe.wait_ge(s_act, n + 1)
                for t in range(4 * half, 4 * half + 4):
                    last = pe.matmul(PS[:, 2 + half, (t % 4) * P:(t % 4 + 1) * P],
                                     AT[:, f, t * P:(t + 1) * P], W2[:, f, :],
                                     start=(f == 0 and t % 4 == 0), stop=(f == FC0 - 1),
                                     skip_group_check=True)
                if f == FC0 - 1:
                    last.then_inc(s_fy, 1)

            for n in range(8):
                f, half = n // 2, n % 2
                if n >= 2:
                    pe.wait_ge(s_hid, 2 * n - 2)
                pe.matmul(PS[:, n % 2, :], W1[:, f * P:(f + 1) * P], XNT[:, 512 * half:512 * half + 512],
                          start=True, stop=True).then_inc(s_h, 1)
                if n >= 4:
                    second(n - 4)
            for n in range(4, 8):
                second(n)

            transpose_tensor(pe, 2, 2)

            MAXB, SCB, OB, PJ = (0, 1), (2, 3), (4, 5), (6, 7)

            def side(s, u):
                def later(i):
                    return not (isinstance(i, int) and i <= 0)

                def q():
                    pe.wait_ge(s_wp[u], 16 * (s // 2 + 1) if isinstance(s, int) else
                               8 * (s - u) + 16)
                    if later(s):
                        pe.wait_ge(s_vl, VG * s - 1)
                    pe.matmul(PS[:, PJ[0], 0:SQ], WP[:, u, 0:P], XB[:, :], start=True, stop=True)\
                        .then_inc(s_qp, 1)

                def k(c):
                    def go():
                        if c == 0:
                            if later(s):
                                pe.wait_ge(s_vl, VG * s)
                        elif c == 1:
                            pe.wait_ge(s_ql, s + 1)
                            pe.wait_ge(s_qh, s + 1)
                        else:
                            pe.wait_ge(s_kl, NC * s + c - 1)
                        k0, n = CHUNK[c]
                        pe.matmul(PS[:, PJ[1 - c % 2], 0:n], WP[:, u, P:2 * P], CT[:, k0:k0 + n],
                                  start=True, stop=True).then_inc(s_kp, 1)
                    return go

                def v(g):
                    def go():
                        if g == 0:
                            pe.wait_ge(s_kl, NC * s + NC)
                        elif g == 1:
                            if not (isinstance(s, int) and s < 2):
                                pe.wait_ge(s_ya, s - 1)
                        else:
                            pe.wait_ge(s_vl, VG * s + g - 1)
                        for kt in range(4 * g, min(4 * g + 4, NK)):
                            m = TK if kt < NK - 1 else LASTK
                            last = pe.matmul(PS[0:m, PJ[g % 2], (kt % 4) * P:(kt % 4 + 1) * P],
                                             CT[:, kt * TK:kt * TK + m], WP[:, u, 2 * P:3 * P],
                                             start=True, stop=True)
                        last.then_inc(s_vp, 1)
                    return go

                def m(n):
                    def go():
                        c, h, qt = n // (2 * QT), n // QT % 2, n % QT
                        if n == 0:
                            pe.wait_ge(s_ql, s + 1)
                            if later(s):
                                pe.wait_ge(s_nq, s)
                        if n in (0, 8):
                            each = 32 if n else 48
                            pe.wait_ge(s_dup[u][n // 8], each * (s // 2 + 1) if isinstance(s, int)
                                       else each // 2 * (s - u) + each)
                        if n >= 2 or later(s):
                            pe.wait_ge(s_mr, 16 * s + n - 1)
                        k0, cols = CHUNK[c]
                        pe.matmul(PS[:, MAXB[n % 2], 0:cols], QA[:, u, h, qt * P:(qt + 1) * P],
                                  KA[:, u, h, k0:k0 + cols], start=True, stop=True).then_inc(s_ms, 1)
                    return go

                def rows():
                    pe.wait_ge(s_nl, s + 1)
                    for n in range(2 * QT):
                        last = pe.transpose(PS[0:2, MAXB[0], n * P:(n + 1) * P], negsplit[:, n, :],
                                            ident[:, :])
                    last.then_inc(s_nt, 1)
                return q, k, v, m, rows

            def scores(i, u, kt):
                n = NK * i + kt
                if kt == 0:
                    pe.wait_ge(s_nq, i + 1)
                    pe.wait_ge(s_kl, NC * i + NC)
                if not (isinstance(n, int) and n < 2):
                    pe.wait_ge(s_pr, n - 1)
                m = TK if kt < NK - 1 else LASTK
                bank = SCB[(u + kt) % 2]
                for h in range(2):
                    o = PS[0:m, bank, h * SQ:(h + 1) * SQ]
                    pe.matmul(o, KA[:, u, h, kt * TK:kt * TK + m], QA[:, u, h, :], start=True, stop=False)
                    last = pe.matmul(o, KB[:, u, h, kt * TK:kt * TK + m], QB[:, u, h, :],
                                     start=False, stop=True)
                last.then_inc(s_sc, 1)

            def values_high(i, u, kt, h):
                if h == 0:
                    pe.wait_ge(s_ph, NK * i + kt + 1)
                    if kt % 4 == 0:
                        pe.wait_ge(s_vl, VG * i + kt // 4 + 1)
                    if kt == 0 and not (isinstance(i, int) and i < 2):
                        pe.wait_ge(s_nr, i - 1)
                m = TK if kt < NK - 1 else LASTK
                o = PS[:, OB[u], h * SQ:(h + 1) * SQ]
                p = PH[0:m, (u + kt) % 2, h * SQ:(h + 1) * SQ]
                pe.matmul(o, VH[0:m, u, kt, h, :], p, start=(kt == 0 and h == 0), stop=False,
                          skip_group_check=True)
                last = pe.matmul(o, VL[0:m, u, kt, h, :], p, start=False, stop=False,
                                 skip_group_check=True)
                if h:
                    last.then_inc(s_pv, 1)

            def values_low(i, u, kt):
                pe.wait_ge(s_pl, NK * i + kt + 1)
                m = TK if kt < NK - 1 else LASTK
                for h in range(2):
                    last = pe.matmul(PS[:, OB[u], h * SQ:(h + 1) * SQ], VH[0:m, u, kt, h, :],
                                     PL[0:m, (u + kt) % 2, h * SQ:(h + 1) * SQ], start=False,
                                     stop=(kt == NK - 1), skip_group_check=True)
                last.then_inc(s_pvl, 1)

            def project_pair(i, u):
                pe.wait_ge(s_wo[u], 16 * (i // 2 + 1) if isinstance(i, int) else 8 * (i - u) + 16)
                pe.wait_ge(s_bv, i + 1)
                if isinstance(i, int) and i >= IT - 2:
                    pe.wait_ge(s_vl, VG * IT)
                    pe.wait_ge(s_ya, i)
                else:
                    pe.wait_ge(s_kl, NC * i + 2 * NC + 3)
                for qt in range(QT):
                    last = pe.matmul(PS[:, PJ[1], qt * P:(qt + 1) * P], ON[:, qt * P:(qt + 1) * P],
                                     WO[:, u, 0:P], start=True, stop=True)
                last.then_inc(s_po, 1)

            def step(i, u, first=False, last=False):
                after = {(n, place): [] for n in range(NK) for place in range(3)}
                if not last:
                    q, k, v, m, rows = side(i + 1, 1 - u)
                    after[0, 0] = [q]
                    for c in range(NC):
                        after[c, 2] = [k(c)]
                    for g in range(VG):
                        after[8 + g, 2] = [v(g)]
                    for n, at in enumerate(MAXAT):
                        after[at].append(m(n))
                    after[NK - 2, 2].append(rows)
                    after[NK - 1, 2].append(lambda: scores(i + 1, 1 - u, 0))
                if not first:
                    after[6, 0].insert(0, lambda: project_pair(i - 1, 1 - u))
                for kt in range(NK):
                    if kt + 1 < NK:
                        scores(i, u, kt + 1)
                    for piece in after[kt, 0]:
                        piece()
                    values_high(i, u, kt, 0)
                    for piece in after[kt, 1]:
                        piece()
                    values_high(i, u, kt, 1)
                    if kt:
                        values_low(i, u, kt - 1)
                    for piece in after[kt, 2]:
                        piece()
                values_low(i, u, NK - 1)

            pe.wait_ge(s_ones, 5)
            pe.wait_ge(s_ct, 32)
            q, k, v, m, rows = side(0, 0)
            q()
            for c in range(NC):
                k(c)()
            for g in range(VG):
                v(g)()
            for n in range(16):
                m(n)()
            rows()
            scores(0, 0, 0)
            step(0, 0, first=True)
            with pe.Fori(0, IT // 2 - 1) as j:
                step(2 * j + 1, 1)
                step(2 * j + 2, 0)
            step(IT - 1, 1, last=True)
            project_pair(IT - 1, 1)

            transpose_tensor(pe, 3, 4)
            pe.wait_ge(s_xnt, 8)
            pe.wait_ge(s_wf, 1)

            def down(n):
                c, half = n // 2, n % 2
                pe.wait_ge(s_ht, n + 1)
                for t in range(4 * half, 4 * half + 4):
                    last = pe.matmul(PS[:, 4 + half, (t % 4) * P:(t % 4 + 1) * P],
                                     AT[:, c, t * P:(t + 1) * P],
                                     wf[:, 2 * F1 + c * P:2 * F1 + (c + 1) * P],
                                     start=(c == 0 and t % 4 == 0), stop=(c == FC1 - 1),
                                     skip_group_check=True)
                if c == FC1 - 1:
                    last.then_inc(s_fy, 1)

            for n in range(2 * FC1):
                c, half = n // 2, n % 2
                if n >= 2:
                    pe.wait_ge(s_ht, n - 1)
                pe.matmul(PS[:, n % 2, :], wf[:, c * P:(c + 1) * P], XNT[:, 512 * half:512 * half + 512],
                          start=True, stop=True)
                pe.matmul(PS[:, 2 + n % 2, :], wf[:, F1 + c * P:F1 + (c + 1) * P],
                          XNT[:, 512 * half:512 * half + 512], start=True, stop=True).then_inc(s_g, 1)
                if n >= 2:
                    down(n - 2)
            for n in range(2 * FC1 - 2, 2 * FC1):
                down(n)

        @block.scalar
        def _(a):
            a.wait_ge(s_gate, 16)
            a.activation(gate[:, :], graw[:, :], ACT.Tanh).then_inc(s_tanh, 1)
            ln_scalar(a, 0)
            transpose_scalar(a, 0)
            for n, (dst, bank) in enumerate(((CKV, 0), (CKV, 1), (K0T, 2), (K0T, 3), (V0, 4), (V0, 5),
                                             (Q0T, 0), (Q0T, 1))):
                a.wait_ge(s_pro, n + 1)
                flat = dst[:, :, :].rearrange("p t n -> p (t n)") if dst is V0 else dst[:, :]
                a.activation(flat[:, 512 * (n % 2):512 * (n % 2) + 512], PS[:, bank, :], ACT.Copy)\
                    .then_inc(s_proe, 1)

            def log_counts(t):
                a.wait_ge(s_c1, t + 1)
                a.activation(logc[:, :], count1[:, :], ACT.Ln).then_inc(s_log, 1)

            def exps0(t, u, hp):
                n = 8 * t + hp
                a.wait_ge(s_nb, n + 1)
                if not (isinstance(n, int) and n < 2):
                    a.wait_ge(s_pt, n - 1)
                if hp == 0 and not (isinstance(t, int) and t < 2):
                    a.wait_ge(s_rec, 2 * t - 2)
                for r in range(2):
                    h = 2 * hp + r
                    last = a.activation(P0[:, hp % 2, r, :], T0[:, hp % 2, r, :], ACT.Exp,
                                        bias=nb0[:, h:h + 1], accum_out=sum0[:, u, h:h + 1])
                last.then_inc(s_p0, 1)

            def store0(t, hp):
                n = 8 * t + hp
                a.wait_ge(s_pt, n + 1)
                if not (isinstance(n, int) and n < 2):
                    a.wait_ge(s_o0, n - 1)
                a.activation(P0T[:, hp % 2, :, :, :].rearrange("p r k n -> p (r k n)"),
                             PS[:, 2 + hp % 2, :], ACT.Copy).then_inc(s_pts, 1)

            def attend0(t, u, more):
                exps0(t, u, 0)
                for hp in range(8):
                    if hp < 7:
                        exps0(t, u, hp + 1)
                    store0(t, hp)
                a.wait_ge(s_ot, t + 1)
                a.activation(O0T[:, :], PS[:, 7, 0:P], ACT.Copy).then_inc(s_ots, 1)
                if more:
                    log_counts(t + 1)

            log_counts(0)
            attend0(0, 0, True)
            with a.Fori(0, NT // 2 - 1) as j:
                attend0(2 * j + 1, 1, True)
                attend0(2 * j + 2, 0, True)
            attend0(NT - 1, 1, False)

            def block(b, t, j, n):
                a.wait_ge(g_ckv, n + 1)
                a.activation(GCKV[:, :], PS[:, 0, 0:KEYS0], ACT.Copy).then_inc(g_ckvs, 1)
                a.wait_ge(g_kv, n + 1)
                a.activation(K0T[:, 0:KEYS0], PS[:, 0, KEYS0:2 * KEYS0], ACT.Copy)
                a.activation(V0[:, 0:KT0, :].rearrange("p t n -> p (t n)"), PS[:, 1, 0:KEYS0],
                             ACT.Copy).then_inc(g_kvs, 1)
                a.wait_ge(g_c1, n + 1)
                a.activation(logc[:, :], count1[:, :], ACT.Ln).then_inc(g_log, 1)
                a.wait_ge(g_best, n + 1)
                a.activation(gshrink[:, 1, :], gshrink[:, 0, :], ACT.Exp).then_inc(g_shr, 1)
                for h in range(H0):
                    last = a.activation(ALLP[:, h, :], ALLP[:, h, :], ACT.Exp, bias=gneg[:, h:h + 1],
                                        accum_out=gpart[:, h:h + 1])
                last.then_inc(g_p, 1)
                for hp in range(8):
                    a.wait_ge(g_pt, 8 * n + hp + 1)
                    if hp:
                        a.wait_ge(g_o, 8 * n + hp)
                    a.activation(P0T[:, 0, :, :, :].rearrange("p r k n -> p (r k n)"), PS[:, 1, :],
                                 ACT.Copy).then_inc(g_pts, 1)

            def turned(t):
                a.wait_ge(g_ot, t + 1)
                a.activation(O0T[:, :], PS[:, 7, 0:P], ACT.Copy).then_inc(g_ots, 1)

            all_blocks(a, nothing, nothing, block, turned)

            ln_scalar(a, 1)
            a.wait_ge(s_th, 2)
            a.activation(trig[:, 4:6, :], trig[:, 2:4, :], ACT.Sin).then_inc(s_ths, 1)
            transpose_scalar(a, 1)
            a.wait_ge(s_th, 3)
            for n in range(10):
                if n < 8:
                    f, u = n // 2, n % 3
                    a.wait_ge(s_h, n + 1)
                    if n >= 3:
                        a.wait_ge(s_act, n - 2)
                    a.activation(ff[:, u, 0, :], PS[:, n % 2, :], ACT.Identity,
                                 bias=fcol[:, 0, f:f + 1]).then_inc(s_hid, 1)
                    a.activation(ff[:, u, 1, :], PS[:, n % 2, :], ACT.Identity, scale=0.1,
                                 bias=trig[:, 8, f:f + 1]).then_inc(s_hid, 1)
                if 1 <= n < 9:
                    a.wait_ge(s_dv, n)
                    a.activation(ff[:, (n - 1) % 3, 3, :], ff[:, (n - 1) % 3, 2, :], ACT.Sin)\
                        .then_inc(s_sin, 1)
                if n >= 2:
                    m = n - 2
                    a.wait_ge(s_q, m + 1)
                    a.activation(AT[:, m // 2, 512 * (m % 2):512 * (m % 2) + 512], ff[:, m % 3, 4, :],
                                 ACT.Relu).then_inc(s_act, 1)
            ln_scalar(a, 2)
            transpose_scalar(a, 2)

            def side(s, u):
                def q():
                    a.wait_ge(s_qp, s + 1)
                    for h in range(2):
                        last = a.activation(QA[0:HD1, u, h, :], PS[HD1 * h:HD1 * h + HD1, 6, 0:SQ],
                                            ACT.Identity,
                                            bias=WP[HD1 * h:HD1 * h + HD1, u, 3 * P:3 * P + 1])
                    last.then_inc(s_qh, 1)

                def k(c):
                    def go():
                        a.wait_ge(s_kp, NC * s + c + 1)
                        k0, n = CHUNK[c]
                        for h in range(2):
                            last = a.activation(KA[0:HD1, u, h, k0:k0 + n],
                                                PS[HD1 * h:HD1 * h + HD1, 7 - c % 2, 0:n],
                                                ACT.Identity,
                                                bias=WP[HD1 * h:HD1 * h + HD1, u, 3 * P + 1:3 * P + 2])
                        last.then_inc(s_kh, 1)
                    return go

                def v(g):
                    def go():
                        a.wait_ge(s_vp, VG * s + g + 1)
                        k0, k1 = 4 * g, min(4 * g + 4, NK)
                        m = TK if k1 < NK else LASTK
                        a.activation(VH[0:m, u, k0:k1, :, 0:HD1],
                                     PS[0:m, 6 + g % 2, 0:(k1 - k0) * P]
                                     .rearrange("p (k h d) -> p k h d", h=2, d=HD1), ACT.Copy)\
                            .then_inc(s_vs, 1)
                    return go
                return q, k, v

            def exps(i, u, kt):
                n = NK * i + kt
                a.wait_ge(s_sc, n + 1)
                if not (isinstance(n, int) and n < 2):
                    a.wait_ge(s_pv, n - 1)
                    a.wait_ge(s_pl, n - 1)
                m = TK if kt < NK - 1 else LASTK
                c = (u + kt) % 2
                a.activation(PH[0:m, c, :], PS[0:m, 2 + c, :], ACT.Exp, scale=SCALE1).then_inc(s_ph, 1)
                a.activation(PR[0:m, c, :], PS[0:m, 2 + c, :], ACT.Exp, scale=SCALE1).then_inc(s_pr, 1)

            def add_bv(i, u):
                a.wait_ge(s_nr, i + 1)
                a.wait_ge(s_wo[u], 16 * (i // 2 + 1) if isinstance(i, int) else 8 * (i - u) + 16)
                if not (isinstance(i, int) and i == 0):
                    a.wait_ge(s_po, i)
                a.activation(ON[:, :], ONR[:, :], ACT.Identity, bias=WO[:, u, P:P + 1])\
                    .then_inc(s_bv, 1)

            def step(i, u, first=False, last=False):
                pieces = {n: [] for n in range(NK + 1)}
                if not last:
                    q, k, v = side(i + 1, 1 - u)
                    pieces[0] = [q]
                    for c in range(NC):
                        pieces[c + 1] = [k(c)]
                    for g in range(VG):
                        pieces[9 + g] = [v(g)]
                if not first:
                    pieces[5].append(lambda: add_bv(i - 1, 1 - u))
                for kt in range(NK):
                    exps(i, u, kt)
                    for piece in pieces[kt]:
                        piece()

            q, k, v = side(0, 0)
            q()
            for c in range(NC):
                k(c)()
            for g in range(VG):
                v(g)()
            step(0, 0, first=True)
            with a.Fori(0, IT // 2 - 1) as j:
                step(2 * j + 1, 1)
                step(2 * j + 2, 0)
            step(IT - 1, 1, last=True)
            add_bv(IT - 1, 1)

            ln_scalar(a, 3)
            ln_scalar(a, 4)
            transpose_scalar(a, 3)
            for n in range(2 * FC1):
                a.wait_ge(s_g, n + 1)
                if n >= 2:
                    a.wait_ge(s_ht, n - 1)
                a.activation(ff[:, n % 2, 0, :], PS[:, n % 2, :], ACT.Silu).then_inc(s_gs, 1)

        @block.vector
        def _(v):
            v.wait_ge(s_iota, 1)
            v.tensor_copy(iota[:, :], iota_i[:, :]).then_inc(s_idxf, 1)
            v.wait_ge(s_idx, 16)
            v.tensor_copy(idxf[:, :, :], idxi[:, :, :]).then_inc(s_idxf, 1)
            v.wait_ge(s_x, 16)
            ln_vector(v, 0, X, XN)
            v.wait_ge(s_idxf, 2)
            v.tensor_reduce(flags[:, 0:1], idxf[:, :, :], AX.XY, ALU.max)
            v.tensor_reduce(flags[:, 1:2], idxf[:, :, :], AX.XY, ALU.min).then_inc(g_step, 1)
            v.wait_ge(g_step, 1)
            v.tensor_scalar(flags[:, 3:4], flags[:, 1:2], -1.0, KEYS0 - 1.0, ALU.mult, ALU.add)\
                .then_inc(g_step, 1)
            v.wait_ge(g_step, 2)
            v.tensor_tensor(flags[:, 2:3], flags[:, 0:1], flags[:, 3:4], ALU.max).then_inc(s_range, 1)

            def picks(t, part):
                if not (isinstance(t, int) and t == 0):
                    v.wait_ge(s_cnt, 8 * t - 7 + part)
                for k in range(8 * part, 8 * part + 8):
                    last = v.tensor_scalar(onehot[:, k, :], iota[:, :], idxf[:, t, k:k + 1]
                                           if isinstance(t, int) else
                                           idxf[:, bass.ds(t, 1), k:k + 1].rearrange("p o n -> p (o n)"),
                                           None, ALU.is_equal)
                last.then_inc(s_oh, 1)

            def count_mask(t, u):
                v.wait_ge(s_cnt, 8 * t + 8)
                if not (isinstance(t, int) and t == 0):
                    v.wait_ge(s_mask, t)
                v.tensor_scalar(count1[:, :], PS[:, 6, 0:KEYS0], 1.0, None, ALU.max).then_inc(s_c1, 1)
                v.tensor_scalar(never[:, :], PS[:, 6, 0:KEYS0], 0.5, NEVER, ALU.is_lt, ALU.mult)\
                    .then_inc(s_nv, 1)
                v.wait_ge(s_log, t + 1)
                v.wait_ge(s_nv, t + 1)
                v.scalar_tensor_tensor(mask[:, u, :], logc[:, :], 1.0 / SCALE0, never[:, :],
                                       ALU.mult, ALU.add).then_inc(s_mask, 1)

            def max0(t, u, hp, more):
                n = 8 * t + hp
                if hp == 0:
                    v.wait_ge(s_mask, t + 1)
                v.wait_ge(s_s0, n + 1)
                if not (isinstance(n, int) and n < 2):
                    v.wait_ge(s_p0, n - 1)
                if more:
                    picks(t + 1, hp)
                for r in range(2):
                    last = v.tensor_tensor_reduce(T0[:, hp % 2, r, :],
                                                  PS[:, hp % 2, r * KEYS0:(r + 1) * KEYS0],
                                                  mask[:, u, :], SCALE0, -3e38, ALU.add, ALU.max,
                                                  mx0[:, 2 * hp + r:2 * hp + r + 1])
                last.then_inc(s_t0, 1)
                v.wait_ge(s_t0, n + 1)
                v.tensor_scalar(nb0[:, 2 * hp:2 * hp + 2], mx0[:, 2 * hp:2 * hp + 2], -1.0, None,
                                ALU.mult).then_inc(s_nb, 1)

            def norm0(t, u, half):
                v.wait_ge(s_p0, 8 * t + 4 * half + 4)
                v.reciprocal(rec0[:, 8 * half:8 * half + 8], sum0[:, u, 8 * half:8 * half + 8])\
                    .then_inc(s_rec, 1)
                v.wait_ge(s_rec, 2 * t + half + 1)
                v.wait_ge(s_o0, 8 * t + 4 * half + 4)
                if half == 0 and not (isinstance(t, int) and t == 0):
                    v.wait_ge(s_ot, t)
                own = PS[:, 4:6, :].rearrange("p b n -> p (b n)")
                own = bass.AP(own.tensor, own.offset + 64 * half, [own.ap[0], [P + HD0, 8], [1, HD0]])
                v.tensor_tensor(O0[:, 8 * half:8 * half + 8, :], own,
                                rec0[:, 8 * half:8 * half + 8].rearrange("p (h o) -> p h o", o=1)
                                .to_broadcast([P, 8, HD0]), ALU.mult).then_inc(s_on0, 1)

            def add0(t):
                v.wait_ge(s_y0, t + 1)
                xt = X[:, bass.ds(t, 1), :].rearrange("p o n -> p (o n)")
                v.scalar_tensor_tensor(xt, PS[:, 7, P:2 * P], gate[:, 0:1], xt, ALU.mult, ALU.add)\
                    .then_inc(s_x0, 1)

            def attend0(t, u, more):
                for hp in range(8):
                    max0(t, u, hp, more)
                    if hp == 5:
                        norm0(t, u, 0)
                norm0(t, u, 1)
                if more:
                    count_mask(t + 1, 1 - u)
                add0(t)

            for part in range(8):
                picks(0, part)
            count_mask(0, 0)
            v.wait_ge(s_rrow, 1)
            v.tensor_reduce(flagrow[0:1, 0:1], PS[0:1, 7, 0:P], AX.X, ALU.max).then_inc(g_step, 1)
            v.wait_ge(g_step, 3)
            v.tensor_scalar(flagrow[0:1, 1:2], flagrow[0:1, 0:1], KEYS0 - 0.5, None, ALU.is_gt)\
                .then_inc(g_step, 1)
            v.wait_ge(g_step, 4)
            v.tensor_copy(flag[0:1, 0:1], flagrow[0:1, 1:2]).then_inc(s_flag, 1)
            v.wait_ge(s_tanh, 1)
            attend0(0, 0, True)
            with v.Fori(0, NT // 2 - 1) as j:
                attend0(2 * j + 1, 1, True)
                attend0(2 * j + 2, 0, True)
            attend0(NT - 1, 1, False)

            SO_FAR = 7
            TILE_STEPS, BLOCK_STEPS, END_STEPS = 3, 10, 1
            PER_TILE = TILE_STEPS + BLOCKS * BLOCK_STEPS + END_STEPS

            def done(ins, count):
                ins.then_inc(g_step, 1)
                v.wait_ge(g_step, count)

            def true_picks():
                done(v.tensor_scalar(away[:, :, :], idxf[:, :, :], 0.0, float(SKV), ALU.is_lt,
                                     ALU.mult), 5)
                done(v.tensor_tensor(idxf[:, :, :], idxf[:, :, :], away[:, :, :], ALU.add), 6)
                done(v.tensor_scalar(idxf[:, :, :], idxf[:, :, :], SKV - 1.0, 0.0, ALU.min,
                                     ALU.max), 7)
                v.wait_ge(g_xl, 16)

            def tile_start(t):
                v.tensor_tensor(QM[:, 0, :, :],
                                Q0T[:, bass.ds(t * P, P)].rearrange("p (o n) -> p o n", o=1)
                                .to_broadcast([P, H0, P]),
                                headmask[:, :].rearrange("p (h o) -> p h o", o=1)
                                .to_broadcast([P, H0, P]), ALU.mult).then_inc(g_qm, 1)
                v.tensor_scalar(gbest[:, 1, :], mx0[:, :], 0.0, -3e38, ALU.mult, ALU.add)
                v.memset(gsum[:, :], 0.0).then_inc(g_step, 1)
                v.memset(gacc[:, :, :], 0.0).then_inc(g_step, 1)
                v.tensor_scalar(gidx[:, :], idxf[:, bass.ds(t, 1), :].rearrange("p o k -> p (o k)"),
                                float(KEYS0), None, ALU.add).then_inc(g_step, 1)

            def block(b, t, j, n):
                base = t * PER_TILE + SO_FAR + TILE_STEPS + j * BLOCK_STEPS
                v.wait_ge(g_step, base)
                v.tensor_scalar(gidx[:, :], gidx[:, :], float(KEYS0), None, ALU.subtract)\
                    .then_inc(g_go, 1)
                v.wait_ge(g_go, n + 1)
                for k in range(PICK):
                    last = v.tensor_scalar(onehot[:, k, :], iota[:, :], gidx[:, k:k + 1], None,
                                           ALU.is_equal)
                last.then_inc(g_oh, 1)
                v.wait_ge(g_cnt, n + 1)
                v.tensor_scalar(count1[:, :], PS[:, 6, 0:KEYS0], 1.0, None, ALU.max).then_inc(g_c1, 1)
                v.tensor_scalar(never[:, :], PS[:, 6, 0:KEYS0], 0.5, NEVER, ALU.is_lt, ALU.mult)\
                    .then_inc(g_nv, 1)
                v.wait_ge(g_log, n + 1)
                v.wait_ge(g_nv, n + 1)
                v.scalar_tensor_tensor(mask[:, 0, :], logc[:, :], 1.0 / SCALE0, never[:, :],
                                       ALU.mult, ALU.add).then_inc(g_mask, 1)
                v.wait_ge(g_mask, n + 1)
                for hp in range(8):
                    v.wait_ge(g_s, 8 * n + hp + 1)
                    v.tensor_tensor(ALLP[:, 2 * hp:2 * hp + 2, :],
                                    PS[:, 0, :].rearrange("p (r k) -> p r k", k=KEYS0),
                                    mask[:, 0:1, :].to_broadcast([P, 2, KEYS0]), ALU.add)\
                        .then_inc(g_t, 1)
                v.wait_ge(g_t, 8 * n + 8)
                done(v.tensor_scalar(ALLP[:, :, :], ALLP[:, :, :], SCALE0, None, ALU.mult), base + 1)
                done(v.tensor_reduce(mx0[:, :], ALLP[:, :, :], AX.X, ALU.max), base + 2)
                done(v.tensor_tensor(gbest[:, 0, :], mx0[:, :], gbest[:, 1, :], ALU.max), base + 3)
                v.tensor_scalar(gneg[:, :], gbest[:, 0, :], -1.0, None, ALU.mult).then_inc(g_step, 1)
                done(v.tensor_tensor(gshrink[:, 0, :], gbest[:, 1, :], gbest[:, 0, :], ALU.subtract),
                     base + 5)
                v.tensor_copy(gbest[:, 1, :], gbest[:, 0, :]).then_inc(g_best, 1)
                v.wait_ge(g_best, n + 1)
                v.wait_ge(g_shr, n + 1)
                v.wait_ge(g_p, n + 1)
                v.wait_ge(g_o, 8 * n + 8)
                for half in range(2):
                    own = PS[:, 2 + 2 * half:4 + 2 * half, :].rearrange("p b n -> p (b n)")
                    own = bass.AP(own.tensor, own.offset + 64 * half,
                                  [own.ap[0], [P + HD0, 8], [1, HD0]])
                    last = v.tensor_copy(gown[:, 8 * half:8 * half + 8, :], own)
                last.then_inc(g_step, 1)
                done(v.tensor_tensor(gacc[:, :, :], gacc[:, :, :],
                                     gshrink[:, 1, :].rearrange("p (h o) -> p h o", o=1)
                                     .to_broadcast([P, H0, HD0]), ALU.mult), base + 7)
                v.tensor_tensor(gacc[:, :, :], gacc[:, :, :], gown[:, :, :], ALU.add)\
                    .then_inc(g_step, 1)
                done(v.tensor_tensor(gsum[:, :], gsum[:, :], gshrink[:, 1, :], ALU.mult), base + 9)
                v.tensor_tensor(gsum[:, :], gsum[:, :], gpart[:, :], ALU.add).then_inc(g_step, 1)

            def tile_end(t):
                base = t * PER_TILE + SO_FAR + PER_TILE
                v.wait_ge(g_step, base - 1)
                done(v.reciprocal(rec0[:, :], gsum[:, :]), base)
                v.tensor_tensor(O0[:, :, :], gacc[:, :, :],
                                rec0[:, :].rearrange("p (h o) -> p h o", o=1)
                                .to_broadcast([P, H0, HD0]), ALU.mult).then_inc(g_norm, 1)
                v.wait_ge(g_y, t + 1)
                xt = X[:, bass.ds(t, 1), :].rearrange("p o n -> p (o n)")
                v.scalar_tensor_tensor(xt, PS[:, 7, P:2 * P], gate[:, 0:1], xt, ALU.mult, ALU.add)\
                    .then_inc(g_x, 1)

            v.wait_ge(s_x0, NT)
            all_blocks(v, true_picks, tile_start, block, tile_end, lambda: v.wait_ge(g_x, NT))

            ln_vector(v, 1, X, XN)
            v.wait_ge(s_ff, 16 * 7)

            links = []

            def chain(ins):
                links.append(1)
                ins.then_inc(s_dv2, 1)
                v.wait_ge(s_dv2, len(links))

            def reduce_angle(dst, src, tmp):
                chain(v.tensor_scalar(tmp, src, 1 / (2 * PI), MAGIC, ALU.mult, ALU.add))
                chain(v.tensor_scalar(tmp, tmp, MAGIC, None, ALU.subtract))
                chain(v.scalar_tensor_tensor(dst, tmp, -TWO_PI_HI, src, ALU.mult, ALU.add))
                chain(v.scalar_tensor_tensor(dst, tmp, -TWO_PI_LO, dst, ALU.mult, ALU.add))

            reduce_angle(trig[:, 1, :], fcol[:, 1, :], trig[:, 0, :])
            chain(v.tensor_scalar(trig[:, 3, :], trig[:, 1, :], PI / 2, None, ALU.add))
            chain(v.tensor_scalar(trig[:, 0, :], trig[:, 3, :], PI, -2 * PI, ALU.is_gt, ALU.mult))
            chain(v.tensor_tensor(trig[:, 3, :], trig[:, 3, :], trig[:, 0, :], ALU.add))
            v.tensor_scalar(trig[:, 3, :], trig[:, 3, :], PI_DOWN, -PI_DOWN, ALU.min, ALU.max)\
                .then_inc(s_th, 1)
            v.tensor_scalar(trig[:, 2, :], trig[:, 1, :], PI_DOWN, -PI_DOWN, ALU.min, ALU.max)\
                .then_inc(s_th, 1)
            v.scalar_tensor_tensor(trig[:, 8, :], fcol[:, 0, :], 0.1, trig[:, 1, :], ALU.mult, ALU.add)\
                .then_inc(s_th, 1)
            v.wait_ge(s_ths, 1)
            chain(v.tensor_tensor(trig[:, 0, :], trig[:, 5, :], fcol[:, 2, :], ALU.mult))
            chain(v.tensor_tensor(trig[:, 7, :], trig[:, 4, :], fcol[:, 3, :], ALU.mult))
            chain(v.tensor_tensor(trig[:, 0, :], trig[:, 0, :], trig[:, 7, :], ALU.add))
            chain(v.tensor_tensor(trig[:, 0, :], trig[:, 0, :], fcol[:, 3, :], ALU.mult))
            chain(v.tensor_scalar(trig[:, 6, :], trig[:, 0, :], 0.1, None, ALU.mult))

            for n in range(9):
                if n < 8:
                    v.wait_ge(s_hid, 2 * n + 2)
                    arg, tmp = ff[:, n % 3, 1, :], ff[:, n % 3, 4, :]
                    chain(v.tensor_scalar(tmp, arg, 1 / (2 * PI), MAGIC, ALU.mult, ALU.add))
                    chain(v.tensor_scalar(tmp, tmp, MAGIC, None, ALU.subtract))
                    chain(v.scalar_tensor_tensor(arg, tmp, -TWO_PI_HI, arg, ALU.mult, ALU.add))
                    v.scalar_tensor_tensor(arg, tmp, -TWO_PI_LO, arg, ALU.mult, ALU.add)\
                        .then_inc(s_red, 1)
                if n:
                    m = n - 1
                    v.wait_ge(s_red, m + 1)
                    v.wait_ge(s_sin, m + 1)
                    v.scalar_tensor_tensor(ff[:, m % 3, 4, :], ff[:, m % 3, 3, :],
                                           trig[:, 6, m // 2:m // 2 + 1], ff[:, m % 3, 0, :],
                                           ALU.mult, ALU.add).then_inc(s_q, 1)
            v.wait_ge(s_wi, 16 * 3)
            v.tensor_scalar(wf[:, :], wi[:, :], 1.0 / 127.0, None, ALU.mult).then_inc(s_wf, 1)

            def add_ffn(n, g, bias, base):
                y = PS[:, base + n % 2, :].rearrange("p (t d) -> p t d", d=P)
                v.wait_ge(s_fy, n + 1)
                if bias:
                    v.tensor_tensor(yb[:, n, :, :], y, B2[:, :].rearrange("p (o d) -> p o d", o=1)
                                    .to_broadcast([P, 4, P]), ALU.add).then_inc(s_yb, 1)
                    v.wait_ge(s_yb, n + 1)
                    y = yb[:, n, :, :]
                xs = X[:, 4 * (n % 2):4 * (n % 2) + 4, :]
                v.scalar_tensor_tensor(xs, y, gate[:, g:g + 1], xs, ALU.mult, ALU.add)\
                    .then_inc(s_x0, 4)

            for n in range(2):
                add_ffn(n, 2, True, 2)
            v.wait_ge(s_x0, 2 * NT)
            ln_vector(v, 2, X, XN)
            v.wait_ge(s_row, 16 * 3)
            v.wait_ge(s_xn, 3 * NT)
            v.tensor_tensor(Y[:, :, :], XN[:, :, :], rowv[:, 0:1, :].to_broadcast([P, NT, P]), ALU.add)\
                .then_inc(s_yi, 1)
            v.wait_ge(s_ones, 5)
            v.wait_ge(s_yi, 1)

            def side(s, u):
                def q():
                    v.wait_ge(s_qh, s + 1)
                    for h in range(2):
                        last = v.scalar_tensor_tensor(
                            QA[HD1:P, u, h, :], PS[HD1 * h:HD1 * h + HD1, 6, 0:SQ],
                            WP[HD1 * h:HD1 * h + HD1, u, 3 * P:3 * P + 1],
                            QA[0:HD1, u, h, :].bitcast(F32), ALU.add, ALU.subtract)
                    last.then_inc(s_ql, 1)

                def k(c):
                    def go():
                        v.wait_ge(s_kh, NC * s + c + 1)
                        k0, n = CHUNK[c]
                        for h in range(2):
                            last = v.scalar_tensor_tensor(
                                KB[0:HD1, u, h, k0:k0 + n], PS[HD1 * h:HD1 * h + HD1, 7 - c % 2, 0:n],
                                WP[HD1 * h:HD1 * h + HD1, u, 3 * P + 1:3 * P + 2],
                                KA[0:HD1, u, h, k0:k0 + n].bitcast(F32), ALU.add, ALU.subtract)
                        last.then_inc(s_kl, 1)
                    return go

                def low(g):
                    def go():
                        v.wait_ge(s_vs, VG * s + g + 1)
                        k0, k1 = 4 * g, min(4 * g + 4, NK)
                        n = TK if k1 < NK else LASTK
                        v.tensor_tensor(VL[0:n, u, k0:k1, :, 0:HD1],
                                        PS[0:n, 6 + g % 2, 0:(k1 - k0) * P]
                                        .rearrange("p (k h d) -> p k h d", h=2, d=HD1),
                                        VH[0:n, u, k0:k1, :, 0:HD1].bitcast(F32), ALU.subtract)\
                            .then_inc(s_vl, 1)
                    return go

                def m(n):
                    def go():
                        if n == 0 and not (isinstance(s, int) and s == 0):
                            v.wait_ge(s_nm, s)
                        v.wait_ge(s_ms, 16 * s + n + 1)
                        cols = CHUNK[n // NC][1]
                        v.tensor_reduce(negpart[:, n % NC, n // NC:n // NC + 1],
                                        PS[:, n % 2, 0:cols], AX.X, ALU.max, negate=True)\
                            .then_inc(s_mr, 1)
                    return go

                def split():
                    v.wait_ge(s_mr, 16 * s + 16)
                    if not (isinstance(s, int) and s == 0):
                        v.wait_ge(s_nl, s)
                        v.wait_ge(s_nt, s)
                    v.tensor_reduce(negmax[:, :], negpart[:, :, :], AX.X, ALU.min).then_inc(s_nm, 1)
                    v.wait_ge(s_nm, s + 1)
                    v.tensor_copy(neghi[:, :], negmax[:, :]).then_inc(s_nh, 1)
                    v.wait_ge(s_nh, s + 1)
                    v.tensor_copy(negsplit[:, :, 0], neghi[:, :].bitcast(F32))
                    v.tensor_tensor(negsplit[:, :, 1], negmax[:, :], neghi[:, :].bitcast(F32),
                                    ALU.subtract).then_inc(s_nl, 1)

                def store():
                    v.wait_ge(s_nt, s + 1)
                    for h in range(2):
                        last = v.tensor_copy(QB[HD1:HD1 + 2, u, h, :], PS[0:2, 0, h * SQ:(h + 1) * SQ])
                    last.then_inc(s_nq, 1)
                return q, k, low, m, split, store

            def copy_sums(i, u):
                v.wait_ge(s_pvl, NK * i + NK)
                if not (isinstance(i, int) and i == 0):
                    v.wait_ge(s_rc, i)
                for h in range(2):
                    last = v.tensor_copy(sums[HD1 * (1 - h):HD1 * (2 - h), :],
                                         PS[HD1:P, 4 + u, h * SQ:(h + 1) * SQ])
                last.then_inc(s_su, 1)

            def recip_sums(i, u):
                v.wait_ge(s_su, i + 1)
                if not (isinstance(i, int) and i == 0):
                    v.wait_ge(s_nr, i)
                v.reciprocal(recip[:, :], sums[:, :]).then_inc(s_rc, 1)

            def normalise(i, u):
                v.wait_ge(s_rc, i + 1)
                if not (isinstance(i, int) and i == 0):
                    v.wait_ge(s_bv, i)
                for h in range(2):
                    last = v.tensor_tensor(ONR[HD1 * h:HD1 * h + HD1, :],
                                           PS[0:HD1, 4 + u, h * SQ:(h + 1) * SQ],
                                           recip[HD1 * (1 - h):HD1 * (2 - h), :], ALU.mult)
                last.then_inc(s_nr, 1)

            def add_pair(i, b):
                v.wait_ge(s_po, i + 1)
                if not (isinstance(i, int) and i == 0):
                    v.wait_ge(s_ya, i)
                y = Y[:, bass.ds(b * QT, QT), :].rearrange("p t d -> p (t d)")
                v.tensor_tensor(y, y, PS[:, 7, 0:QT * P], ALU.add).then_inc(s_ya, 1)

            def step(i, u, b_prev, first=False, last=False):
                pieces = {n: [] for n in range(NK + 1)}
                if not last:
                    q, k, low, m, split, store = side(i + 1, 1 - u)
                    pieces[0] = [q]
                    for c in range(NC):
                        pieces[c + 1] = [k(c)]
                    for n, (kt, place) in enumerate(MAXAT):
                        pieces[kt].append(m(n))
                    for g in range(VG):
                        pieces[9 + g].append(low(g))
                    pieces[11].insert(0, split)
                    pieces[NK - 1].insert(0, store)
                if not first:
                    pieces[0].insert(0, lambda: copy_sums(i - 1, 1 - u))
                    pieces[0].insert(2, lambda: recip_sums(i - 1, 1 - u))
                    pieces[4].insert(0, lambda: normalise(i - 1, 1 - u))
                    pieces[6].insert(1, lambda: add_pair(i - 1, b_prev))
                for kt in range(NK + 1):
                    for piece in pieces[kt]:
                        piece()

            q, k, low, m, split, store = side(0, 0)
            q()
            for c in range(NC):
                k(c)()
            for g in range(VG):
                low(g)()
            for n in range(16):
                m(n)()
            split()
            store()
            step(0, 0, 0, first=True)
            with v.Fori(0, B - 1) as b:
                with v.Fori(0, PAIRS // 2) as j:
                    step(PAIRS * b + 2 * j + 1, 1, b)
                    step(PAIRS * b + 2 * j + 2, 0, b)
            with v.Fori(0, PAIRS // 2 - 1) as j:
                step(PAIRS * (B - 1) + 2 * j + 1, 1, B - 1)
                step(PAIRS * (B - 1) + 2 * j + 2, 0, B - 1)
            step(IT - 1, 1, B - 1, last=True)
            copy_sums(IT - 1, 1)
            recip_sums(IT - 1, 1)
            normalise(IT - 1, 1)
            add_pair(IT - 1, B - 1)

            v.wait_ge(s_ya, IT)
            ln_vector(v, 3, Y, Y)
            v.wait_ge(s_xn, 4 * NT)
            v.tensor_tensor(Y[:, :, :], Y[:, :, :], rowv[:, 1:2, :].to_broadcast([P, NT, P]),
                            ALU.mult).then_inc(s_yl, 1)
            v.wait_ge(s_yl, 1)
            v.tensor_tensor(Y[:, :, :], Y[:, :, :], rowv[:, 2:3, :].to_broadcast([P, NT, P]),
                            ALU.add).then_inc(s_yg, 1)
            v.wait_ge(s_yg, 1)
            v.scalar_tensor_tensor(X[:, :, :], Y[:, :, :], gate[:, 1:2], X[:, :, :],
                                   ALU.mult, ALU.add).then_inc(s_x0, NT)
            v.wait_ge(s_x0, 3 * NT)
            ln_vector(v, 4, X, XN)
            for n in range(2 * FC1):
                v.wait_ge(s_gs, n + 1)
                v.tensor_tensor(AT[:, n // 2, 512 * (n % 2):512 * (n % 2) + 512], ff[:, n % 2, 0, :],
                                PS[:, 2 + n % 2, :], ALU.mult).then_inc(s_ht, 1)
            for n in range(2, 4):
                add_ffn(n, 3, False, 4)


def kernel(**inputs):
    import numpy as _np
    import concourse.bacc as _bacc
    from concourse import mybir as _mybir
    from concourse.bass_utils import run_bass_kernel_spmd as _run

    g = {k: _np.asarray(v) for k, v in inputs.items()}
    ctxT = g["ctx_1024"].transpose(0, 2, 1)
    pair = lambda w: w.reshape(P, PAIRS, P).transpose(1, 0, 2)
    cols = lambda v: v.reshape(PAIRS, P, 1)
    arrays = {
        "x": g["x"].reshape(ROWS, P),
        "ctxT": _np.concatenate([ctxT, ctxT[:, :, -1:]], axis=2),
        "ctx0": _np.concatenate([ctxT, _np.zeros((B, P, BLOCKS * KEYS0 - SKV), ctxT.dtype)], axis=2),
        "idx": g["itok_BxSx64_0_2047"].reshape(ROWS, PICK),
        "gates": _np.concatenate([g["g_xattn"], g["g_ffn"]]),
        "wqT": g["L0_xattn_W_q"].T, "wdT": g["L0_xattn_W_kv_down"].T,
        "wuT": g["L0_xattn_W_kv_up"].T, "woT": g["L0_xattn_W_out"].T,
        "w1": g["L0_ffn_W1"], "b1": g["L0_ffn_b1"].reshape(FC0, P).T,
        "theta": g["L0_ffn_quantum_phases"].reshape(FC0, P).T,
        "wre": g["L0_ffn_quantum_weights_real"].reshape(FC0, P).T,
        "wim": g["L0_ffn_quantum_weights_imag"].reshape(FC0, P).T,
        "w2": g["L0_ffn_W2"], "b2": g["L0_ffn_b2"],
        "wqkv": _np.concatenate([pair(g["L1_xattn_Wq"]), pair(g["L1_xattn_Wk"]),
                                 pair(g["L1_xattn_Wv"]), cols(g["L1_xattn_bq"]),
                                 cols(g["L1_xattn_bk"])], axis=2),
        "wout": _np.concatenate([g["L1_xattn_Wo"].reshape(PAIRS, P, P), cols(g["L1_xattn_bv"])],
                                axis=2),
        "bo": g["L1_xattn_bo"], "gamma": g["L1_xattn_ln_gamma"], "beta": g["L1_xattn_ln_beta"],
        "wgT": g["L1_ffn_w_gate"].T, "wupT": g["L1_ffn_w_up"].T,
        "wdnT": g["L1_ffn_w_down"].reshape(P, FC1, P).transpose(2, 1, 0).reshape(P, FC1 * P),
    }
    arrays = {k: _np.ascontiguousarray(v) for k, v in arrays.items()}
    nc = _bacc.Bacc("TRN2", target_bir_lowering=False, num_devices=1)
    args = [nc.dram_tensor(f"in_{k}", a.shape, _mybir.dt.from_np(a.dtype), kind="ExternalInput").ap()
            for k, a in arrays.items()]
    out = nc.dram_tensor("out_0", (ROWS, P), F32, kind="ExternalOutput").ap()
    program(nc, *args, out)
    r = _run(nc, [{f"in_{k}": a for k, a in arrays.items()}], core_ids=[0])
    return r.results[0]["out_0"].reshape(B, SQ, P)
```

```python
from contextlib import ExitStack

import numpy as np

import concourse.bass as bass
from concourse import mybir

F32 = mybir.dt.float32
F32R = mybir.dt.float32r
BF16 = mybir.dt.bfloat16
I32 = mybir.dt.int32
ALU = mybir.AluOpType
ACT = mybir.ActivationFunctionType
AX = mybir.AxisListType

P = 128
B, SQ, SKV = 4, 256, 1601
ROWS = B * SQ
NT = ROWS // P
QT = SQ // P
EPS = 1e-5
PI = float(np.pi)

H0, HD0, PICK, KEYS0 = 16, 8, 64, 256
KT0 = KEYS0 // P
PARTS = [range(0, 11), range(11, 22), range(22, 33), range(33, 44), range(44, 54), range(54, 64)]
NP = len(PARTS)
SCALE0 = HD0 ** -0.5
GROUPS = 4
GH = H0 // GROUPS
GW = GH * HD0
NEVER = -1e30
BLOCKS = -(-SKV // KEYS0)

H1, HD1 = 16, 64
PAIRS = H1 // 2
IT = B * PAIRS
SCALE1 = HD1 ** -0.5
NK = -(-SKV // P)
TK = SKV // NK
LASTK = SKV - (NK - 1) * TK
SPAD = SKV + 1
CHUNK = [(0, 402), (402, 400), (802, 400), (1202, 400)]
NC = len(CHUNK)
PE_AT = {"q": (0, 0), "k0": (0, 0), "k1": (1, 0), "k2": (2, 0), "k3": (3, 1), "pair": (6, 1),
         "v0": (9, 1), "v1": (10, 1), "v2": (10, 2), "v3": (11, 1), "rows": (11, 2), "m0": (5, 0),
         "m1": (5, 2), "m2": (6, 0), "m3": (6, 1), "m4": (6, 2), "m5": (7, 0), "m6": (7, 1),
         "m7": (7, 2), "m8": (8, 0), "m9": (8, 1), "m10": (8, 2), "m11": (9, 0), "m12": (9, 1),
         "m13": (9, 2), "m14": (10, 0), "m15": (10, 1), "next": (12, 2)}
ACT_AT = {"q": 0, "k0": 1, "k1": 2, "k2": 3, "k3": 4, "bv": 5, "v0": 10, "v1": 10, "v2": 11,
          "v3": 12}
DVE_ORDER = ("sums recip q k0 k1 k2 norm k3 m0 m1 m2 pair m3 m4 m5 m6 m7 m8 m9 m10 m11 m12 "
             "m13 v0 m14 m15 v1 split v2 store v3").split()
VG = -(-NK // 4)
PACK = 3 * P + 2
PACKO = P + 1

F0, FC0 = 512, 4
F1, FC1 = 384, 3
MAGIC = 1.5 * 2.0 ** 23
TWO_PI_HI = 6.28125
TWO_PI_LO = 2 * np.pi - 6.28125
PI_DOWN = 3.1415925


def program(nc, x, ctxT, ctx0, idx, gates, wq4, wk4, select, wdT, wvT, woT, w1, b1, theta, wre, wim,
            w2, b2, wqkv, wout, bo, gamma, beta, wgT, wupT, wdnT, out):
    with ExitStack() as stack:
        def sb(name, shape, dt=F32):
            return stack.enter_context(nc.sbuf_tensor(name, shape, dt))

        def sem(name):
            return stack.enter_context(nc.semaphore(name))

        early = ExitStack()

        def eb(name, shape, dt=F32):
            return early.enter_context(nc.sbuf_tensor(name, shape, dt))

        X = sb("X", [P, NT, P])
        XN = sb("XN", [P, NT, P])
        XNT = sb("XNT", [P, ROWS])
        stats = sb("stats", [P, NT, 6])
        mv = sb("mv", [P, NT, 2])
        std = sb("std", [P, NT])
        rstd = sb("rstd", [P, NT])
        ident = sb("ident", [P, P])
        identb = sb("identb", [P, P], BF16)
        gate = sb("gate", [P, 4])
        graw = sb("graw", [P, 4])
        flag = sb("flag", [1, 1], I32)

        W1 = sb("W1", [P, F0])
        W2 = sb("W2", [P, FC0, P])
        fcol = sb("fcol", [P, 4, FC0])
        trig = sb("trig", [P, 9, FC0])
        B2 = sb("B2", [P, P])
        yb = sb("yb", [P, 2, 4, P])
        wi = sb("wi", [P, 2 * F1 + FC1 * P], I32)
        wf = sb("wf", [P, 2 * F1 + FC1 * P])
        Y = sb("Y", [P, NT, P])
        rowv = sb("rowv", [P, 3, P])

        w0 = eb("w0", [P, 3, P])
        wq = eb("wq", [P, GROUPS, P])
        wk = eb("wk", [P, GROUPS, P])
        K0 = eb("K0", [P, GROUPS, B * KEYS0], F32R)
        V0 = eb("V0", [P, B * KT0, P])
        sel = eb("sel", [P, GH + 2])
        QM = eb("QM", [P, 2, H0, P], F32R)
        iota_i = eb("iota_i", [P, KEYS0], I32)
        iota = eb("iota", [P, KEYS0], BF16)
        idxi = eb("idxi", [P, NT, PICK], I32)
        idxf = eb("idxf", [P, NT, PICK])
        onehot = eb("onehot", [P, PICK, KEYS0], BF16)
        count1 = eb("count1", [P, KEYS0])
        never = eb("never", [P, KEYS0])
        logc = eb("logc", [P, KEYS0])
        mask = eb("mask", [P, 2, KEYS0])
        T0 = eb("T0", [P, 2, 2, KEYS0])
        P0 = eb("P0", [P, 2, 2, KEYS0])
        P0T = eb("P0T", [P, 2, 2, KT0, P])
        mx0 = eb("mx0", [P, H0])
        nb0 = eb("nb0", [P, H0])
        sum0 = eb("sum0", [P, 2, H0])
        rec0 = eb("rec0", [P, H0])
        O0 = eb("O0", [P, H0, HD0])
        O0T = eb("O0T", [P, P])

        flags = eb("flags", [P, 4])
        flagrow = eb("flagrow", [1, P])
        away = eb("away", [P, NT, PICK])
        GC = eb("GC", [P, KEYS0])
        GCKV = eb("GCKV", [P, KEYS0])
        gidx = eb("gidx", [P, PICK])
        gbest = eb("gbest", [P, 2, H0])
        gneg = eb("gneg", [P, H0])
        gshrink = eb("gshrink", [P, 2, H0])
        gpart = eb("gpart", [P, H0])
        gsum = eb("gsum", [P, H0])
        gacc = eb("gacc", [P, H0, HD0])
        gown = eb("gown", [P, H0, HD0])

        ff = eb("ff", [P, 3, 5, 512])
        AT = eb("AT", [P, FC0, ROWS])
        Q0 = ff[:, :, :, :].rearrange("p u s n -> p (u s n)")[:, 0:GROUPS * ROWS]\
            .rearrange("p (g n) -> p g n", g=GROUPS)
        C0, CKV = AT[:, 0, :], AT[:, 1, :]
        early.close()

        KB = sb("KB", [P, 2, 2, SPAD], F32R)
        QB = sb("QB", [P, 2, 2, SQ], F32R)
        VH = sb("VH", [P, 2, NK, 2, P], F32R)
        VL = sb("VL", [P, 2, NK, 2, P], F32R)
        CT = sb("CT", [P, SPAD])
        WP = sb("WP", [P, 2, PACK])
        XB = sb("XB", [P, SQ])
        WO = sb("WO", [P, 2, PACKO])
        KA = sb("KA", [P, 2, 2, SPAD], F32R)
        QA = sb("QA", [P, 2, 2, SQ], F32R)
        PR = sb("PR", [P, 2, 2 * SQ])
        PH = sb("PH", [P, 2, 2 * SQ], F32R)
        PL = sb("PL", [P, 2, 2 * SQ], F32R)
        negpart = sb("negpart", [P, 2 * QT, NC])
        negmax = sb("negmax", [P, 2 * QT])
        neghi = sb("neghi", [P, 2 * QT], F32R)
        negsplit = sb("negsplit", [P, 2 * QT, 2])
        sums = sb("sums", [P, SQ])
        recip = sb("recip", [P, SQ])
        ONR = sb("ONR", [P, SQ])
        ON = sb("ON", [P, SQ])

        PS = stack.enter_context(nc.psum_tensor("PS", [P, 8, 512], F32))

        s_x, s_idx, s_w0, s_ff, s_row, s_gate, s_wi = (sem(n) for n in (
            "x_loaded", "idx_loaded", "w0_loaded", "ffn_loaded", "rows_loaded", "gates_loaded",
            "int_weights_loaded"))
        s_c0 = sem("keys_loaded")
        s_const0, s_const = sem("const_cleared"), sem("const_ready")
        s_iota = sem("iota_ready")
        s_tanh = sem("gates_ready")
        s_ln, s_var, s_std, s_rstd, s_xn = (sem(n) for n in (
            "ln_stats", "var_ready", "std_ready", "rstd_ready", "xn_ready"))
        s_tp, s_xnt = sem("xn_transposed"), sem("xnt_stored")
        s_x0 = sem("x_updated")
        s_pro, s_proe, s_prol = (sem(n) for n in (
            "prologue_matmuls", "prologue_stored", "prologue_parts"))
        s_idxf = sem("idx_float")
        s_oh, s_cnt, s_c1, s_log, s_nv, s_mask = (sem(n) for n in (
            "onehot_ready", "counts_ready", "count1_ready", "log_ready", "never_ready", "mask_ready"))
        s_qm = sem("masked_q_ready")
        s_s0, s_t0, s_nb, s_p0, s_pt, s_pts, s_o0, s_rec, s_on0, s_ot, s_ots, s_y0 = (
            sem(n) for n in ("l0_scores", "l0_max", "l0_negmax", "l0_probs", "l0_probsT",
                             "l0_probsT_stored", "l0_out", "l0_recip", "l0_normed", "l0_outT",
                             "l0_outT_stored", "l0_proj"))
        s_range, s_rrow, s_flag = sem("pick_range"), sem("pick_range_row"), sem("flag_ready")
        (g_xl, g_go, g_qm, g_ctx, g_ckv, g_ckvs, g_kv, g_kvs, g_oh, g_cnt, g_kl, g_c1, g_nv, g_log,
         g_mask, g_s, g_t, g_best, g_shr, g_p, g_pt, g_pts, g_o, g_step, g_norm, g_ot,
         g_ots, g_y, g_x) = (sem("all_" + n) for n in (
            "x_loaded", "block_started", "masked_q", "context", "ckv", "ckv_stored", "kv", "kv_stored",
            "onehot", "counts", "k_parts", "count1", "never", "log", "mask", "scores", "max", "best",
            "shrink", "probs", "probsT", "probsT_stored", "out", "vector_step",
            "normed", "outT", "outT_stored", "projected", "x_updated"))
        s_red = sem("angle_reduced")
        s_h, s_hid, s_dv, s_sin, s_act, s_q, s_fy, s_yb = (sem(n) for n in (
            "hidden_ready", "hidden_stored", "angle_ready", "sin_ready", "act_ready", "q_ready",
            "ffn_out", "ffn_biased"))
        s_dv2 = sem("dve_chain")
        s_th, s_ths = sem("theta_reduced"), sem("theta_sin")
        s_wf = sem("int_weights_float")
        s_g, s_gs, s_ht = sem("gate_up_ready"), sem("silu_ready"), sem("h_ready")
        s_ones = sem("l1_constants")
        s_ct = sem("context_loaded")
        s_wp = [sem(f"qkv_weights_loaded{u}") for u in range(2)]
        s_wo = [sem(f"out_weights_loaded{u}") for u in range(2)]
        (s_qp, s_qh, s_ql, s_kp, s_kh, s_kl, s_vp, s_vs, s_ms, s_mr, s_nm, s_nh, s_nl, s_nt, s_nq,
         s_sc, s_pr, s_ph, s_pl, s_pv, s_pvl, s_vl, s_rc, s_nr, s_bv, s_po, s_ya) = (sem(n) for n in (
            "q_projected", "q_high", "q_low", "k_projected", "k_high", "k_low", "v_projected",
            "v_stored", "max_scores", "max_reduced", "negmax_ready", "negmax_high", "negmax_split",
            "negmax_rows", "negmax_stored", "scores_ready", "probs_ready", "probs_high",
            "probs_low", "pv_high_done", "pv_low_done", "v_low",
            "recip_ready", "normed", "bias_added", "pair_projected", "pair_added"))
        s_dup = [[sem(f"k_high_twice{u}{half}") for half in range(2)] for u in range(2)]
        s_su = sem("sums_copied")
        s_yi, s_yl, s_yg = sem("y_started"), sem("y_scaled"), sem("y_normed")
        s_out = sem("out_stored")

        block = stack.enter_context(nc.Block())

        def outside(engine):
            engine.wait_ge(s_flag, 1)
            return engine.value_load(flag[0:1, 0:1], min_val=0, max_val=1)

        def all_blocks(engine, before, tile_start, block, tile_end, after=lambda: None):
            with engine.If(outside(engine) >= 1):
                before()
                with engine.Fori(0, B) as b:
                    with engine.Fori(0, QT) as q:
                        t = b * QT + q
                        tile_start(t)
                        with engine.Fori(0, BLOCKS) as j:
                            block(b, t, j, t * BLOCKS + j)
                        tile_end(t)
                after()

        def nothing(*_):
            pass

        ALLP = AT[:, :, :].rearrange("p f n -> p (f n)").rearrange("p (h k) -> p h k", k=KEYS0)

        JOBS = [("c", 0, 0), ("c", 0, 1), *[("k", g, n) for g in range(GROUPS) for n in range(2)],
                ("v", 0, 0), ("v", 0, 1), *[("q", g, n) for g in range(GROUPS) for n in range(2)]]

        def masked_q(engine, t, u):
            q = Q0[:, :, bass.ds(t * P, P)]
            return engine.tensor_tensor(
                QM[:, u, :, :].rearrange("p (g h) n -> p g h n", g=GROUPS),
                q.rearrange("p g (o n) -> p g o n", o=1).to_broadcast([P, GROUPS, GH, P]),
                sel[:, 0:GH].rearrange("p (a h o) -> p a h o", a=1, o=1)
                .to_broadcast([P, GROUPS, GH, P]), ALU.mult)

        HALVES = (range(0, NT // 2), range(NT // 2, NT))
        LN_TILES = [range(NT)] * 3 + [HALVES[0], HALVES[0], HALVES[1], HALVES[1]]
        LN_BEFORE = [sum(len(ts) for ts in LN_TILES[:k]) for k in range(len(LN_TILES) + 1)]

        def ln_moments(v, k, src):
            ts, before = LN_TILES[k], LN_BEFORE[k]
            for t in ts:
                v.bn_stats(stats[:, t, :], src[:, t, :]).then_inc(s_ln, 1)
            v.wait_ge(s_ln, 2 * before + len(ts))
            for t in ts:
                v.bn_aggr(mv[:, t, :], stats[:, t, :]).then_inc(s_ln, 1)
            v.wait_ge(s_ln, 2 * (before + len(ts)))
            v.tensor_scalar(std[:, ts[0]:ts[-1] + 1], mv[:, ts[0]:ts[-1] + 1, 1], EPS, None, ALU.add)\
                .then_inc(s_var, 1)

        def ln_apply(v, k, src, dst):
            ts = LN_TILES[k]
            v.wait_ge(s_std, k + 1)
            v.reciprocal(rstd[:, ts[0]:ts[-1] + 1], std[:, ts[0]:ts[-1] + 1]).then_inc(s_rstd, 1)
            v.wait_ge(s_rstd, k + 1)
            for t in ts:
                v.tensor_scalar(dst[:, t, :], src[:, t, :], mv[:, t, 0:1], rstd[:, t:t + 1],
                                ALU.subtract, ALU.mult).then_inc(s_xn, 1)

        def ln_vector(v, k, src, dst):
            ln_moments(v, k, src)
            ln_apply(v, k, src, dst)

        def ln_scalar(a, k):
            cols = slice(LN_TILES[k][0], LN_TILES[k][-1] + 1)
            a.wait_ge(s_var, k + 1)
            a.activation(std[:, cols], std[:, cols], ACT.Sqrt).then_inc(s_std, 1)

        def transpose_tensor(pe, k, n, call):
            pe.wait_ge(s_xn, LN_BEFORE[call + 1])
            if k:
                pe.wait_ge(s_xnt, 2 * k)
            for t in HALVES[n]:
                last = pe.transpose(PS[:, 6 + n, (t % 4) * P:(t % 4 + 1) * P], XN[:, t, :], ident[:, :])
            last.then_inc(s_tp, 1)

        def transpose_scalar(a, k, n):
            a.wait_ge(s_tp, 2 * k + n + 1)
            a.activation(XNT[:, 512 * n:512 * (n + 1)], PS[:, 6 + n, :], ACT.Copy).then_inc(s_xnt, 1)

        @block.sync
        def _(sp):
            sp.dma_start(X[:, :, :], x.rearrange("(t p) d -> p t d", p=P)).then_inc(s_x, 16)
            sp.dma_start(C0.rearrange("p (b k) -> p b k", b=B),
                         ctx0[:, :, 0:KEYS0].rearrange("b d k -> d b k")).then_inc(s_c0, 16)
            sp.dma_start(w0[:, 0, :], wdT).then_inc(s_c0, 16)
            sp.dma_start(idxi[:, :, :], idx.rearrange("(t p) k -> p t k", p=P)).then_inc(s_idx, 16)
            sp.dma_start(wk[:, :, :], wk4).then_inc(s_w0, 16)
            sp.dma_start(w0[:, 1, :], wvT).then_inc(s_w0, 16)
            sp.dma_start(wq[:, :, :], wq4).then_inc(s_w0, 16)
            sp.dma_start(w0[:, 2, :], woT).then_inc(s_w0, 16)
            sp.dma_start(sel[:, :], select).then_inc(s_w0, 16)
            sp.dma_start(graw[:, :], gates.partition_broadcast(P)).then_inc(s_gate, 16)
            sp.dma_start(W1[:, :], w1).then_inc(s_ff, 16)
            sp.dma_start(W2[:, :, :], w2.rearrange("(c p) d -> p c d", p=P)).then_inc(s_ff, 16)
            for n, src in enumerate((b1, theta, wre, wim)):
                sp.dma_start(fcol[:, n, :], src).then_inc(s_ff, 16)
            sp.dma_start(B2[:, :], b2.partition_broadcast(P)).then_inc(s_ff, 16)
            for n, src in enumerate((bo, gamma, beta)):
                sp.dma_start(rowv[:, n, :], src.partition_broadcast(P)).then_inc(s_row, 16)
            sp.dma_start(wi[:, 0:F1], wgT).then_inc(s_wi, 16)
            sp.dma_start(wi[:, F1:2 * F1], wupT).then_inc(s_wi, 16)
            sp.dma_start(wi[:, 2 * F1:], wdnT).then_inc(s_wi, 16)

            def reload():
                sp.wait_ge(s_x0, NT)
                sp.dma_start(X[:, :, :], x.rearrange("(t p) d -> p t d", p=P)).then_inc(g_xl, 16)

            def load_block(b, t, j, n):
                sp.wait_ge(g_go, n + 1)
                sp.dma_start(GC[:, :], ctx0[b, :, bass.ds(j * KEYS0, KEYS0)]).then_inc(g_ctx, 16)

            all_blocks(sp, reload, nothing, load_block, nothing)

            def met():
                sp.wait_ge(s_xnt, 6)

            def load_batch(b):
                if b:
                    sp.dma_start(CT[:, :], ctxT[b]).then_inc(s_ct, 16)
                sp.dma_start(XB[:, :], XNT[:, bass.ds(b * SQ, SQ)]).then_inc(s_ct, 16)
                sp.wait_ge(s_ct, 32 * (b + 1))

            def load_pair(g, u):
                sp.dma_start(WP[:, u, :], wqkv[g]).then_inc(s_wp[u], 16)

            def load_out(g, u):
                sp.dma_start(WO[:, u, :], wout[g]).then_inc(s_wo[u], 16)

            def duplicate(s, u):
                for half, (k0, k1) in enumerate(((0, CHUNK[2][0]), (CHUNK[2][0], SPAD))):
                    sp.wait_ge(s_kh, NC * s + 2 * half + 2)
                    for h in range(2):
                        sp.dma_start(KA[HD1:P, u, h, k0:k1].bitcast(F32),
                                     KA[0:HD1, u, h, k0:k1].bitcast(F32)).then_inc(s_dup[u][half], 16)
                    if half == 0:
                        sp.dma_start(QB[0:HD1, u, :, :].bitcast(F32),
                                     QA[0:HD1, u, :, :].bitcast(F32)).then_inc(s_dup[u][half], 16)

            def feed(s, g, u, last=False):
                duplicate(s, u)
                if not last:
                    if not (isinstance(s, int) and s == 0):
                        sp.wait_ge(s_vl, VG * s)
                        sp.wait_ge(s_kl, NC * s)
                        sp.wait_ge(s_ql, s)
                        met()
                    load_pair(g + 1, 1 - u)
                if not (isinstance(s, int) and s < 2):
                    sp.wait_ge(s_po, s - 1)
                    met()
                load_out(g, u)

            sp.wait_ge(s_xn, 2 * NT)
            sp.dma_start(CT[:, :], ctxT[0]).then_inc(s_ct, 16)
            load_pair(0, 0)
            sp.wait_ge(s_xnt, 6)
            load_batch(0)
            for b in range(B):
                s0 = PAIRS * b
                if b:
                    sp.wait_ge(s_vp, VG * s0)
                    sp.wait_ge(s_qp, s0)
                    load_batch(b)
                    sp.wait_ge(s_vl, VG * s0 - VG)
                    sp.wait_ge(s_kl, NC * s0 - NC)
                    load_pair(0, 0)
                feed(s0, 0, 0)
                feed(s0 + 1, 1, 1)
                with sp.Fori(1, PAIRS // 2 - 1) as j:
                    for u in range(2):
                        feed(s0 + 2 * j + u, 2 * j + u, u)
                feed(s0 + PAIRS - 2, PAIRS - 2, 0)
                feed(s0 + PAIRS - 1, PAIRS - 1, 1, last=True)
            for half, ts in enumerate(HALVES):
                sp.wait_ge(s_x0, NT * 3 + len(ts) * (half + 1))
                sp.dma_start(out.rearrange("(t p) d -> p t d", p=P)[:, ts[0]:ts[-1] + 1, :],
                             X[:, ts[0]:ts[-1] + 1, :]).then_inc(s_out, 16)
            sp.wait_ge(s_out, 16 * 2)

        @block.gpsimd
        def _(pool):
            pool.memset(ident[:, :], 0.0).then_inc(s_const0, 1)
            pool.memset(identb[:, :], 0.0).then_inc(s_const0, 1)
            pool.iota(iota_i[:, :], pattern=[[1, KEYS0]], base=0, channel_multiplier=0)\
                .then_inc(s_iota, 1)
            pool.wait_ge(s_const0, 2)
            for m in (ident, identb):
                pool.affine_select(out=m[:, :], in_=m[:, :], compare_op=ALU.not_equal, fill=1.0,
                                   base=0, pattern=[[-1, P]], channel_multiplier=1)\
                    .then_inc(s_const, 1)
            pool.wait_ge(s_const, 2)
            pool.wait_ge(s_w0, 16 * 5)
            pool.wait_ge(s_prol, 4 * GROUPS)

            masked_q(pool, 0, 0).then_inc(s_qm, 1)
            pool.wait_ge(s_qm, 1)
            masked_q(pool, 1, 1).then_inc(s_qm, 1)
            with pool.Fori(1, NT // 2) as j:
                for u in range(2):
                    pool.wait_ge(s_s0, 8 * (2 * j + u - 1))
                    pool.wait_ge(s_qm, 2 * j + u)
                    masked_q(pool, 2 * j + u, u).then_inc(s_qm, 1)
            pool.wait_ge(s_xn, 2 * NT)
            pool.memset(KB[HD1:, :, :, :].bitcast(F32), 0.0).then_inc(s_ones, 1)
            pool.wait_ge(s_ones, 1)
            for n in range(8):
                pool.wait_ge(s_red, n + 1)
                if n:
                    pool.wait_ge(s_dv, n)
                pool.tensor_scalar(ff[:, n % 3, 2, :], ff[:, n % 3, 1, :], PI_DOWN, -PI_DOWN, ALU.min,
                                   ALU.max).then_inc(s_dv, 1)
            pool.wait_ge(s_dv, 8)
            pool.memset(QB[HD1:, :, :, :].bitcast(F32), 0.0).then_inc(s_ones, 1)
            pool.wait_ge(s_ones, 2)
            pool.memset(VH[:, :, :, :, HD1:].bitcast(F32), 1.0).then_inc(s_ones, 1)
            pool.wait_ge(s_ones, 3)
            pool.memset(VL[:, :, :, :, HD1:].bitcast(F32), 0.0).then_inc(s_ones, 1)
            pool.wait_ge(s_ones, 4)
            pool.memset(KB[HD1:HD1 + 2, :, :, :].bitcast(F32), 1.0).then_inc(s_ones, 1)

            def low_part(i, u, kt):
                n = NK * i + kt
                pool.wait_ge(s_pr, n + 1)
                if not (isinstance(n, int) and n < 2):
                    pool.wait_ge(s_pvl, n - 1)
                m = TK if kt < NK - 1 else LASTK
                c = (u + kt) % 2
                pool.tensor_tensor(PL[0:m, c, :], PR[0:m, c, :], PH[0:m, c, :].bitcast(F32),
                                   ALU.subtract).then_inc(s_pl, 1)

            for kt in range(NK):
                low_part(0, 0, kt)
            with pool.Fori(0, IT // 2 - 1) as j:
                for u in (1, 0):
                    for kt in range(NK):
                        low_part(2 * j + 2 - u, u, kt)
            for kt in range(NK):
                low_part(IT - 1, 1, kt)

        @block.tensor
        def _(pe):
            def count_part(t, part):
                pe.wait_ge(s_oh, NP * t + part + 1)
                if part == 0 and not (isinstance(t, int) and t == 0):
                    pe.wait_ge(s_nv, t)
                for k in PARTS[part]:
                    last = pe.matmul(PS[:, 6, 0:KEYS0], identb[:, :], onehot[:, k, :],
                                     start=(k == 0), stop=(k == PICK - 1))
                last.then_inc(s_cnt, 1)

            pe.wait_ge(s_c0, 16 * 2)
            for n, (what, g, half) in enumerate(JOBS):
                bank, cols = n % 6, slice(512 * half, 512 * half + 512)
                if n == 6:
                    pe.wait_ge(s_const, 2)
                    transpose_tensor(pe, 0, 0, 0)
                    transpose_tensor(pe, 0, 1, 0)
                if n >= 6:
                    last_what = JOBS[n - 6][0]
                    if last_what in "cv":
                        pe.wait_ge(s_proe, n - 5)
                    else:
                        pe.wait_ge(s_prol, n - 7 if last_what == "k" else n - 9)
                if n == 2:
                    pe.wait_ge(s_w0, 16 * 5)
                    pe.wait_ge(s_proe, 2)
                if what == "q" and g == half == 0:
                    pe.wait_ge(s_xnt, 2)
                if what == "v":
                    for t in range(4 * half, 4 * half + 4):
                        last = pe.matmul(PS[:, bank, (t % 4) * P:(t % 4 + 1) * P],
                                         CKV[:, t * P:(t + 1) * P], w0[:, 1, :], start=True, stop=True)
                else:
                    weights, source = {"c": (w0[:, 0, :], C0), "k": (wk[:, g, :], CKV),
                                       "q": (wq[:, g, :], XNT[:, :])}[what]
                    last = pe.matmul(PS[:, bank, :], weights, source[:, cols], start=True, stop=True)
                last.then_inc(s_pro, 1)
                if n in (12, 13, 15, 17):
                    count_part(0, (12, 13, 15, 17).index(n))
            pe.wait_ge(s_proe, len(JOBS))
            pe.wait_ge(s_prol, 4 * GROUPS)

            def scores0(t, b, u, hp):
                n = 8 * t + hp
                if hp == 0:
                    pe.wait_ge(s_qm, t + 1)
                if not (isinstance(n, int) and n < 2):
                    pe.wait_ge(s_t0, n - 1)
                for r in range(2):
                    last = pe.matmul(PS[:, hp % 2, r * KEYS0:(r + 1) * KEYS0],
                                     QM[:, u, 2 * hp + r, :],
                                     K0[:, (2 * hp + r) // GH, bass.ds(b * KEYS0, KEYS0)],
                                     start=True, stop=True)
                last.then_inc(s_s0, 1)

            def turn0(t, hp):
                n = 8 * t + hp
                pe.wait_ge(s_p0, n + 1)
                if not (isinstance(n, int) and n < 2):
                    pe.wait_ge(s_pts, n - 1)
                for r in range(2):
                    for kt in range(KT0):
                        c = (r * KT0 + kt) * P
                        last = pe.transpose(PS[:, 2 + hp % 2, c:c + P],
                                            P0[:, hp % 2, r, kt * P:(kt + 1) * P], ident[:, :])
                last.then_inc(s_pt, 1)

            def out0(t, b, hp):
                pe.wait_ge(s_pts, 8 * t + hp + 1)
                half = hp // 4
                if hp % 4 == 0 and not (isinstance(t, int) and t + half == 0):
                    pe.wait_ge(s_on0, 2 * t + half)
                for r in range(2):
                    h = 2 * (hp % 4) + r
                    for kt in range(KT0):
                        last = pe.matmul(PS[:, 4 + h // 4, (h % 4) * P:(h % 4 + 1) * P],
                                         P0T[:, hp % 2, r, kt, :], V0[:, bass.ds(b * KT0 + kt, 1), :]
                                         .rearrange("p o n -> p (o n)"),
                                         start=(kt == 0), stop=(kt == KT0 - 1))
                last.then_inc(s_o0, 1)

            def turn_out0(t):
                pe.wait_ge(s_on0, 2 * t + 2)
                if not (isinstance(t, int) and t == 0):
                    pe.wait_ge(s_x0, t)
                pe.transpose(PS[:, 7, 0:P], O0[:, :, :].rearrange("p h e -> p (h e)"), ident[:, :])\
                    .then_inc(s_ot, 1)

            def project0(t):
                pe.wait_ge(s_ots, t + 1)
                pe.matmul(PS[:, 7, P:2 * P], O0T[:, :], w0[:, 2, :], start=True, stop=True)\
                    .then_inc(s_y0, 1)

            def attend0(t, u, batch, before=None, after=None):
                for hp in range(8):
                    if hp < 7:
                        scores0(t, batch, u, hp + 1)
                    elif after is not None:
                        scores0(t + 1, after, 1 - u, 0)
                    if after is not None and hp < NP:
                        count_part(t + 1, hp)
                    if hp:
                        turn0(t, hp)
                        out0(t, batch, hp - 1)
                    else:
                        if before is not None:
                            out0(t - 1, before, 7)
                        turn0(t, hp)
                    if before is not None and hp == 1:
                        turn_out0(t - 1)
                    if before is not None and hp == 2:
                        project0(t - 1)

            for part in range(4, NP):
                count_part(0, part)
            pe.wait_ge(s_range, 1)
            pe.transpose(PS[0:1, 7, 0:P], flags[:, 2:3], ident[:, :]).then_inc(s_rrow, 1)
            scores0(0, 0, 0, 0)
            attend0(0, 0, 0, after=0)
            attend0(1, 1, 0, before=0, after=1)
            attend0(2, 0, 1, before=0, after=1)
            with pe.Fori(1, NT // 2 - 1) as j:
                attend0(2 * j + 1, 1, j, before=j, after=j + 1)
                attend0(2 * j + 2, 0, j + 1, before=j, after=j + 1)
            attend0(NT - 1, 1, B - 1, before=B - 1)
            out0(NT - 1, B - 1, 7)
            turn_out0(NT - 1)
            project0(NT - 1)

            def block(b, t, j, n):
                pe.wait_ge(g_go, n + 1)
                pe.wait_ge(g_ctx, 16 * n + 16)
                pe.matmul(PS[:, 0, 0:KEYS0], w0[:, 0, :], GC[:, :], start=True, stop=True)\
                    .then_inc(g_ckv, 1)
                pe.wait_ge(g_ckvs, n + 1)
                for g in range(GROUPS):
                    pe.matmul(PS[:, 2 + g // 2, (g % 2) * KEYS0:(g % 2 + 1) * KEYS0], wk[:, g, :],
                              GCKV[:, :], start=True, stop=True)
                for kt in range(KT0):
                    last = pe.matmul(PS[:, 1, kt * P:(kt + 1) * P], GCKV[:, kt * P:(kt + 1) * P],
                                     w0[:, 1, :], start=True, stop=True)
                last.then_inc(g_kv, 1)
                pe.wait_ge(g_oh, n + 1)
                for k in range(PICK):
                    last = pe.matmul(PS[:, 6, 0:KEYS0], identb[:, :], onehot[:, k, :],
                                     start=(k == 0), stop=(k == PICK - 1))
                last.then_inc(g_cnt, 1)
                pe.wait_ge(g_kvs, n + 1)
                pe.wait_ge(g_kl, n + 1)
                pe.wait_ge(g_qm, t + 1)
                for hp in range(8):
                    if hp:
                        pe.wait_ge(g_t, 8 * n + hp)
                    for r in range(2):
                        last = pe.matmul(PS[:, 0, r * KEYS0:(r + 1) * KEYS0], QM[:, 0, 2 * hp + r, :],
                                         K0[:, (2 * hp + r) // GH, 0:KEYS0], start=True, stop=True)
                    last.then_inc(g_s, 1)
                pe.wait_ge(g_p, n + 1)
                for hp in range(8):
                    for r in range(2):
                        for kt in range(KT0):
                            c = (r * KT0 + kt) * P
                            last = pe.transpose(PS[:, 1, c:c + P],
                                                ALLP[:, 2 * hp + r, kt * P:(kt + 1) * P], ident[:, :])
                    last.then_inc(g_pt, 1)
                    pe.wait_ge(g_pts, 8 * n + hp + 1)
                    for r in range(2):
                        h = 2 * hp + r
                        for kt in range(KT0):
                            last = pe.matmul(PS[:, 2 + h // 4, (h % 4) * P:(h % 4 + 1) * P],
                                             P0T[:, 0, r, kt, :], V0[:, kt, :],
                                             start=(kt == 0), stop=(kt == KT0 - 1))
                    last.then_inc(g_o, 1)

            def project(t):
                pe.wait_ge(g_norm, t + 1)
                pe.transpose(PS[:, 7, 0:P], O0[:, :, :].rearrange("p h e -> p (h e)"), ident[:, :])\
                    .then_inc(g_ot, 1)
                pe.wait_ge(g_ots, t + 1)
                pe.matmul(PS[:, 7, P:2 * P], O0T[:, :], w0[:, 2, :], start=True, stop=True)\
                    .then_inc(g_y, 1)

            all_blocks(pe, nothing, nothing, block, project)

            transpose_tensor(pe, 1, 0, 1)
            transpose_tensor(pe, 1, 1, 1)
            pe.wait_ge(s_xnt, 4)
            pe.wait_ge(s_ff, 16 * 7)

            def second(n):
                f, half = n // 2, n % 2
                pe.wait_ge(s_act, n + 1)
                for t in range(4 * half, 4 * half + 4):
                    last = pe.matmul(PS[:, 2 + half, (t % 4) * P:(t % 4 + 1) * P],
                                     AT[:, f, t * P:(t + 1) * P], W2[:, f, :],
                                     start=(f == 0 and t % 4 == 0), stop=(f == FC0 - 1),
                                     skip_group_check=True)
                if f == FC0 - 1:
                    last.then_inc(s_fy, 1)

            for n in range(8):
                f, half = n // 2, n % 2
                if n >= 2:
                    pe.wait_ge(s_hid, 2 * n - 2)
                pe.matmul(PS[:, n % 2, :], W1[:, f * P:(f + 1) * P], XNT[:, 512 * half:512 * half + 512],
                          start=True, stop=True).then_inc(s_h, 1)
                if n >= 4:
                    second(n - 4)
            for n in range(4, 8):
                second(n)

            transpose_tensor(pe, 2, 0, 2)
            transpose_tensor(pe, 2, 1, 2)

            MAXB, SCB, OB, PJ = (0, 1), (2, 3), (4, 5), (6, 7)

            def side(s, u):
                def later(i):
                    return not (isinstance(i, int) and i <= 0)

                def q():
                    pe.wait_ge(s_wp[u], 16 * (s // 2 + 1) if isinstance(s, int) else
                               8 * (s - u) + 16)
                    if later(s):
                        pe.wait_ge(s_vl, VG * s - 1)
                    pe.matmul(PS[:, PJ[0], 0:SQ], WP[:, u, 0:P], XB[:, :], start=True, stop=True)\
                        .then_inc(s_qp, 1)

                def k(c):
                    def go():
                        if c == 0:
                            if later(s):
                                pe.wait_ge(s_vl, VG * s)
                        elif c == 1:
                            pe.wait_ge(s_ql, s + 1)
                            pe.wait_ge(s_qh, s + 1)
                        else:
                            pe.wait_ge(s_kl, NC * s + c - 1)
                        k0, n = CHUNK[c]
                        pe.matmul(PS[:, PJ[1 - c % 2], 0:n], WP[:, u, P:2 * P], CT[:, k0:k0 + n],
                                  start=True, stop=True).then_inc(s_kp, 1)
                    return go

                def v(g):
                    def go():
                        if g == 0:
                            pe.wait_ge(s_kl, NC * s + NC)
                        elif g == 1:
                            if not (isinstance(s, int) and s < 2):
                                pe.wait_ge(s_ya, s - 1)
                        else:
                            pe.wait_ge(s_vl, VG * s + g - 1)
                        for kt in range(4 * g, min(4 * g + 4, NK)):
                            m = TK if kt < NK - 1 else LASTK
                            last = pe.matmul(PS[0:m, PJ[g % 2], (kt % 4) * P:(kt % 4 + 1) * P],
                                             CT[:, kt * TK:kt * TK + m], WP[:, u, 2 * P:3 * P],
                                             start=True, stop=True)
                        last.then_inc(s_vp, 1)
                    return go

                def m(n):
                    def go():
                        c, h, qt = n // (2 * QT), n // QT % 2, n % QT
                        if n == 0:
                            pe.wait_ge(s_ql, s + 1)
                            if later(s):
                                pe.wait_ge(s_nq, s)
                        if n in (0, 8):
                            each = 32 if n else 48
                            pe.wait_ge(s_dup[u][n // 8], each * (s // 2 + 1) if isinstance(s, int)
                                       else each // 2 * (s - u) + each)
                        if n >= 2 or later(s):
                            pe.wait_ge(s_mr, 16 * s + n - 1)
                        k0, cols = CHUNK[c]
                        pe.matmul(PS[:, MAXB[n % 2], 0:cols], QA[:, u, h, qt * P:(qt + 1) * P],
                                  KA[:, u, h, k0:k0 + cols], start=True, stop=True).then_inc(s_ms, 1)
                    return go

                def rows():
                    pe.wait_ge(s_nl, s + 1)
                    for n in range(2 * QT):
                        last = pe.transpose(PS[0:2, MAXB[0], n * P:(n + 1) * P], negsplit[:, n, :],
                                            ident[:, :])
                    last.then_inc(s_nt, 1)
                return q, k, v, m, rows

            def scores(i, u, kt):
                n = NK * i + kt
                if kt == 0:
                    pe.wait_ge(s_nq, i + 1)
                    pe.wait_ge(s_kl, NC * i + NC)
                if not (isinstance(n, int) and n < 2):
                    pe.wait_ge(s_pr, n - 1)
                m = TK if kt < NK - 1 else LASTK
                bank = SCB[(u + kt) % 2]
                for h in range(2):
                    o = PS[0:m, bank, h * SQ:(h + 1) * SQ]
                    pe.matmul(o, KA[:, u, h, kt * TK:kt * TK + m], QA[:, u, h, :], start=True, stop=False)
                    last = pe.matmul(o, KB[:, u, h, kt * TK:kt * TK + m], QB[:, u, h, :],
                                     start=False, stop=True)
                last.then_inc(s_sc, 1)

            def values_high(i, u, kt, h):
                if h == 0:
                    pe.wait_ge(s_ph, NK * i + kt + 1)
                    if kt % 4 == 0:
                        pe.wait_ge(s_vl, VG * i + kt // 4 + 1)
                    if kt == 0 and not (isinstance(i, int) and i < 2):
                        pe.wait_ge(s_nr, i - 1)
                m = TK if kt < NK - 1 else LASTK
                o = PS[:, OB[u], h * SQ:(h + 1) * SQ]
                p = PH[0:m, (u + kt) % 2, h * SQ:(h + 1) * SQ]
                pe.matmul(o, VH[0:m, u, kt, h, :], p, start=(kt == 0 and h == 0), stop=False,
                          skip_group_check=True)
                last = pe.matmul(o, VL[0:m, u, kt, h, :], p, start=False, stop=False,
                                 skip_group_check=True)
                if h:
                    last.then_inc(s_pv, 1)

            def values_low(i, u, kt):
                pe.wait_ge(s_pl, NK * i + kt + 1)
                m = TK if kt < NK - 1 else LASTK
                for h in range(2):
                    last = pe.matmul(PS[:, OB[u], h * SQ:(h + 1) * SQ], VH[0:m, u, kt, h, :],
                                     PL[0:m, (u + kt) % 2, h * SQ:(h + 1) * SQ], start=False,
                                     stop=(kt == NK - 1), skip_group_check=True)
                last.then_inc(s_pvl, 1)

            def project_pair(i, u):
                pe.wait_ge(s_wo[u], 16 * (i // 2 + 1) if isinstance(i, int) else 8 * (i - u) + 16)
                pe.wait_ge(s_bv, i + 1)
                if isinstance(i, int) and i >= IT - 2:
                    pe.wait_ge(s_vl, VG * IT)
                    pe.wait_ge(s_ya, i)
                else:
                    pe.wait_ge(s_kl, NC * i + 2 * NC + 3)
                for qt in range(QT):
                    last = pe.matmul(PS[:, PJ[1], qt * P:(qt + 1) * P], ON[:, qt * P:(qt + 1) * P],
                                     WO[:, u, 0:P], start=True, stop=True)
                last.then_inc(s_po, 1)

            def step(i, u, first=False, last=False):
                work = {}
                if not first:
                    work["pair"] = lambda: project_pair(i - 1, 1 - u)
                if not last:
                    q, k, v, m, rows = side(i + 1, 1 - u)
                    work |= {"q": q, "rows": rows, "next": lambda: scores(i + 1, 1 - u, 0)}
                    work |= {f"k{c}": k(c) for c in range(NC)}
                    work |= {f"v{g}": v(g) for g in range(VG)}
                    work |= {f"m{n}": m(n) for n in range(NC * 2 * QT)}

                def beside(kt, place):
                    for name, at in PE_AT.items():
                        if at == (kt, place) and name in work:
                            work[name]()

                for kt in range(NK):
                    if kt + 1 < NK:
                        scores(i, u, kt + 1)
                    beside(kt, 0)
                    values_high(i, u, kt, 0)
                    beside(kt, 1)
                    values_high(i, u, kt, 1)
                    if kt:
                        values_low(i, u, kt - 1)
                    beside(kt, 2)
                values_low(i, u, NK - 1)

            pe.wait_ge(s_ones, 5)
            pe.wait_ge(s_ct, 32)
            q, k, v, m, rows = side(0, 0)
            q()
            for c in range(NC):
                k(c)()
            for g in range(VG):
                v(g)()
            for n in range(16):
                m(n)()
            rows()
            scores(0, 0, 0)
            step(0, 0, first=True)
            step(1, 1)
            step(2, 0)
            with pe.Fori(1, IT // 2 - 1) as j:
                step(2 * j + 1, 1)
                step(2 * j + 2, 0)
            step(IT - 1, 1, last=True)
            project_pair(IT - 1, 1)

            transpose_tensor(pe, 3, 0, 4)
            pe.wait_ge(s_wf, 1)

            def down(n):
                half, c = n // FC1, n % FC1
                pe.wait_ge(s_ht, n + 1)
                for t in range(4 * half, 4 * half + 4):
                    last = pe.matmul(PS[:, 4 + half, (t % 4) * P:(t % 4 + 1) * P],
                                     AT[:, c, t * P:(t + 1) * P],
                                     wf[:, 2 * F1 + c * P:2 * F1 + (c + 1) * P],
                                     start=(c == 0 and t % 4 == 0), stop=(c == FC1 - 1),
                                     skip_group_check=True)
                if c == FC1 - 1:
                    last.then_inc(s_fy, 1)

            for n in range(2 * FC1):
                half, c = n // FC1, n % FC1
                pe.wait_ge(s_xnt, 7 + half)
                if n == 2:
                    transpose_tensor(pe, 3, 1, 6)
                if n >= 2:
                    pe.wait_ge(s_ht, n - 1)
                pe.matmul(PS[:, n % 2, :], wf[:, c * P:(c + 1) * P], XNT[:, 512 * half:512 * half + 512],
                          start=True, stop=True)
                pe.matmul(PS[:, 2 + n % 2, :], wf[:, F1 + c * P:F1 + (c + 1) * P],
                          XNT[:, 512 * half:512 * half + 512], start=True, stop=True).then_inc(s_g, 1)
                if n >= 2:
                    down(n - 2)
            for n in range(2 * FC1 - 2, 2 * FC1):
                down(n)

        @block.scalar
        def _(a):
            a.wait_ge(s_gate, 16)
            a.activation(gate[:, :], graw[:, :], ACT.Tanh).then_inc(s_tanh, 1)
            for n, (what, g, half) in enumerate(JOBS):
                if n == 2:
                    ln_scalar(a, 0)
                if n == 6:
                    transpose_scalar(a, 0, 0)
                    transpose_scalar(a, 0, 1)
                a.wait_ge(s_pro, n + 1)
                cols = slice(512 * half, 512 * half + 512)
                dst = {"c": CKV[:, cols], "k": K0[:, g, cols], "q": Q0[:, g, cols].bitcast(F32R),
                       "v": V0[:, :, :].rearrange("p t n -> p (t n)")[:, cols]}[what]
                a.activation(dst, PS[:, n % 6, :], ACT.Copy).then_inc(s_proe, 1)

            def log_counts(t):
                a.wait_ge(s_c1, t + 1)
                a.activation(logc[:, :], count1[:, :], ACT.Ln).then_inc(s_log, 1)

            def exps0(t, u, hp):
                n = 8 * t + hp
                a.wait_ge(s_nb, n + 1)
                if not (isinstance(n, int) and n < 2):
                    a.wait_ge(s_pt, n - 1)
                if hp == 0 and not (isinstance(t, int) and t < 2):
                    a.wait_ge(s_rec, 2 * t - 2)
                for r in range(2):
                    h = 2 * hp + r
                    last = a.activation(P0[:, hp % 2, r, :], T0[:, hp % 2, r, :], ACT.Exp,
                                        bias=nb0[:, h:h + 1], accum_out=sum0[:, u, h:h + 1])
                last.then_inc(s_p0, 1)

            def store0(t, hp):
                n = 8 * t + hp
                a.wait_ge(s_pt, n + 1)
                if not (isinstance(n, int) and n < 2):
                    a.wait_ge(s_o0, n - 1)
                a.activation(P0T[:, hp % 2, :, :, :].rearrange("p r k n -> p (r k n)"),
                             PS[:, 2 + hp % 2, :], ACT.Copy).then_inc(s_pts, 1)

            def store_out0(t):
                a.wait_ge(s_ot, t + 1)
                a.activation(O0T[:, :], PS[:, 7, 0:P], ACT.Copy).then_inc(s_ots, 1)

            def attend0(t, u, first=False, last=False):
                for hp in range(8):
                    if hp < 7:
                        exps0(t, u, hp + 1)
                    elif not last:
                        exps0(t + 1, 1 - u, 0)
                    if hp == NP - 1 and not last:
                        log_counts(t + 1)
                    store0(t, hp)
                    if hp == 1 and not first:
                        store_out0(t - 1)

            a.preload_act_table_set("natural_log_exp_and_others")
            log_counts(0)
            exps0(0, 0, 0)
            attend0(0, 0, first=True)
            attend0(1, 1)
            attend0(2, 0)
            with a.Fori(1, NT // 2 - 1) as j:
                attend0(2 * j + 1, 1)
                attend0(2 * j + 2, 0)
            attend0(NT - 1, 1, last=True)
            store_out0(NT - 1)

            def block(b, t, j, n):
                a.wait_ge(g_ckv, n + 1)
                a.activation(GCKV[:, :], PS[:, 0, 0:KEYS0], ACT.Copy).then_inc(g_ckvs, 1)
                a.wait_ge(g_kv, n + 1)
                for half in range(2):
                    a.activation(K0[:, 2 * half:2 * half + 2, 0:KEYS0],
                                 PS[:, 2 + half, :].rearrange("p (g k) -> p g k", g=2), ACT.Copy)
                a.activation(V0[:, 0:KT0, :].rearrange("p t n -> p (t n)"), PS[:, 1, 0:KEYS0],
                             ACT.Copy).then_inc(g_kvs, 1)
                a.wait_ge(g_c1, n + 1)
                a.activation(logc[:, :], count1[:, :], ACT.Ln).then_inc(g_log, 1)
                a.wait_ge(g_best, n + 1)
                a.activation(gshrink[:, 1, :], gshrink[:, 0, :], ACT.Exp).then_inc(g_shr, 1)
                for h in range(H0):
                    last = a.activation(ALLP[:, h, :], ALLP[:, h, :], ACT.Exp, bias=gneg[:, h:h + 1],
                                        accum_out=gpart[:, h:h + 1])
                last.then_inc(g_p, 1)
                for hp in range(8):
                    a.wait_ge(g_pt, 8 * n + hp + 1)
                    if hp:
                        a.wait_ge(g_o, 8 * n + hp)
                    a.activation(P0T[:, 0, :, :, :].rearrange("p r k n -> p (r k n)"), PS[:, 1, :],
                                 ACT.Copy).then_inc(g_pts, 1)

            def turned(t):
                a.wait_ge(g_ot, t + 1)
                a.activation(O0T[:, :], PS[:, 7, 0:P], ACT.Copy).then_inc(g_ots, 1)

            all_blocks(a, nothing, nothing, block, turned)

            ln_scalar(a, 1)
            a.wait_ge(s_th, 2)
            a.activation(trig[:, 4:6, :], trig[:, 2:4, :], ACT.Sin).then_inc(s_ths, 1)
            transpose_scalar(a, 1, 0)
            transpose_scalar(a, 1, 1)
            a.wait_ge(s_th, 3)
            for n in range(10):
                if n < 8:
                    f, u = n // 2, n % 3
                    a.wait_ge(s_h, n + 1)
                    if n >= 3:
                        a.wait_ge(s_act, n - 2)
                    a.activation(ff[:, u, 0, :], PS[:, n % 2, :], ACT.Identity,
                                 bias=fcol[:, 0, f:f + 1]).then_inc(s_hid, 1)
                    a.activation(ff[:, u, 1, :], PS[:, n % 2, :], ACT.Identity, scale=0.1,
                                 bias=trig[:, 8, f:f + 1]).then_inc(s_hid, 1)
                if 1 <= n < 9:
                    a.wait_ge(s_dv, n)
                    a.activation(ff[:, (n - 1) % 3, 3, :], ff[:, (n - 1) % 3, 2, :], ACT.Sin)\
                        .then_inc(s_sin, 1)
                if n >= 2:
                    m = n - 2
                    a.wait_ge(s_q, m + 1)
                    a.activation(AT[:, m // 2, 512 * (m % 2):512 * (m % 2) + 512], ff[:, m % 3, 4, :],
                                 ACT.Relu).then_inc(s_act, 1)
            ln_scalar(a, 2)
            transpose_scalar(a, 2, 0)
            transpose_scalar(a, 2, 1)

            def side(s, u):
                def q():
                    a.wait_ge(s_qp, s + 1)
                    for h in range(2):
                        last = a.activation(QA[0:HD1, u, h, :], PS[HD1 * h:HD1 * h + HD1, 6, 0:SQ],
                                            ACT.Identity,
                                            bias=WP[HD1 * h:HD1 * h + HD1, u, 3 * P:3 * P + 1])
                    last.then_inc(s_qh, 1)

                def k(c):
                    def go():
                        a.wait_ge(s_kp, NC * s + c + 1)
                        k0, n = CHUNK[c]
                        for h in range(2):
                            last = a.activation(KA[0:HD1, u, h, k0:k0 + n],
                                                PS[HD1 * h:HD1 * h + HD1, 7 - c % 2, 0:n],
                                                ACT.Identity,
                                                bias=WP[HD1 * h:HD1 * h + HD1, u, 3 * P + 1:3 * P + 2])
                        last.then_inc(s_kh, 1)
                    return go

                def v(g):
                    def go():
                        a.wait_ge(s_vp, VG * s + g + 1)
                        k0, k1 = 4 * g, min(4 * g + 4, NK)
                        m = TK if k1 < NK else LASTK
                        a.activation(VH[0:m, u, k0:k1, :, 0:HD1],
                                     PS[0:m, 6 + g % 2, 0:(k1 - k0) * P]
                                     .rearrange("p (k h d) -> p k h d", h=2, d=HD1), ACT.Copy)\
                            .then_inc(s_vs, 1)
                    return go
                return q, k, v

            def exps(i, u, kt):
                n = NK * i + kt
                a.wait_ge(s_sc, n + 1)
                if not (isinstance(n, int) and n < 2):
                    a.wait_ge(s_pv, n - 1)
                    a.wait_ge(s_pl, n - 1)
                m = TK if kt < NK - 1 else LASTK
                c = (u + kt) % 2
                a.activation(PH[0:m, c, :], PS[0:m, 2 + c, :], ACT.Exp, scale=SCALE1).then_inc(s_ph, 1)
                a.activation(PR[0:m, c, :], PS[0:m, 2 + c, :], ACT.Exp, scale=SCALE1).then_inc(s_pr, 1)

            def add_bv(i, u):
                a.wait_ge(s_nr, i + 1)
                a.wait_ge(s_wo[u], 16 * (i // 2 + 1) if isinstance(i, int) else 8 * (i - u) + 16)
                if not (isinstance(i, int) and i == 0):
                    a.wait_ge(s_po, i)
                a.activation(ON[:, :], ONR[:, :], ACT.Identity, bias=WO[:, u, P:P + 1])\
                    .then_inc(s_bv, 1)

            def step(i, u, first=False, last=False):
                work = {}
                if not first:
                    work["bv"] = lambda: add_bv(i - 1, 1 - u)
                if not last:
                    q, k, v = side(i + 1, 1 - u)
                    work |= {"q": q}
                    work |= {f"k{c}": k(c) for c in range(NC)}
                    work |= {f"v{g}": v(g) for g in range(VG)}
                for kt in range(NK):
                    exps(i, u, kt)
                    for name, at in ACT_AT.items():
                        if at == kt and name in work:
                            work[name]()

            q, k, v = side(0, 0)
            q()
            for c in range(NC):
                k(c)()
            for g in range(VG):
                v(g)()
            step(0, 0, first=True)
            step(1, 1)
            step(2, 0)
            with a.Fori(1, IT // 2 - 1) as j:
                step(2 * j + 1, 1)
                step(2 * j + 2, 0)
            step(IT - 1, 1, last=True)
            ln_scalar(a, 3)
            add_bv(IT - 1, 1)
            ln_scalar(a, 4)
            transpose_scalar(a, 3, 0)
            ln_scalar(a, 5)
            ln_scalar(a, 6)
            for n in range(2 * FC1):
                if n == 2:
                    transpose_scalar(a, 3, 1)
                a.wait_ge(s_g, n + 1)
                if n >= 2:
                    a.wait_ge(s_ht, n - 1)
                a.activation(ff[:, n % 2, 0, :], PS[:, n % 2, :], ACT.Silu).then_inc(s_gs, 1)

        @block.vector
        def _(v):
            v.wait_ge(s_iota, 1)
            v.tensor_copy(iota[:, :], iota_i[:, :]).then_inc(s_idxf, 1)
            v.wait_ge(s_idx, 16)
            v.tensor_copy(idxf[:, :, :], idxi[:, :, :]).then_inc(s_idxf, 1)
            v.wait_ge(s_x, 16)
            ln_vector(v, 0, X, XN)
            v.wait_ge(s_idxf, 2)
            v.tensor_reduce(flags[:, 0:1], idxf[:, :, :], AX.XY, ALU.max)
            v.tensor_reduce(flags[:, 1:2], idxf[:, :, :], AX.XY, ALU.min).then_inc(g_step, 1)
            v.wait_ge(g_step, 1)
            v.tensor_scalar(flags[:, 3:4], flags[:, 1:2], -1.0, KEYS0 - 1.0, ALU.mult, ALU.add)\
                .then_inc(g_step, 1)
            v.wait_ge(g_step, 2)
            v.tensor_tensor(flags[:, 2:3], flags[:, 0:1], flags[:, 3:4], ALU.max).then_inc(s_range, 1)

            def one_hot(t, k):
                return v.tensor_scalar(onehot[:, k, :], iota[:, :], idxf[:, t, k:k + 1]
                                       if isinstance(t, int) else
                                       idxf[:, bass.ds(t, 1), k:k + 1].rearrange("p o n -> p (o n)"),
                                       None, ALU.is_equal)

            v.wait_ge(s_w0, 16 * 5)
            EARLY = {n: (4 * m, 4 * m + 4) for m, n in enumerate([*range(2, 10), *range(12, 20)])}
            for n, (what, g, half) in enumerate(JOBS):
                if what in "kq":
                    v.wait_ge(s_proe, n + 1)
                    cols = slice(512 * half, 512 * half + 512)
                    which, dst = (GH, K0[:, g, cols]) if what == "k" else \
                        (GH + 1, Q0[:, g, cols].bitcast(F32R))
                    v.scalar_tensor_tensor(dst, dst.bitcast(F32), sel[:, which:which + 1],
                                           PS[:, n % 6, :], ALU.mult, ALU.add).then_inc(s_prol, 1)
                    for k in range(*EARLY[n]):
                        ins = one_hot(0, k)
                        if k in [part[-1] for part in PARTS]:
                            ins.then_inc(s_oh, 1)

            def picks(t, part):
                v.wait_ge(s_cnt, NP * t - NP + 1 + part)
                for k in PARTS[part]:
                    last = one_hot(t, k)
                last.then_inc(s_oh, 1)

            def read_counts(t):
                v.wait_ge(s_cnt, NP * t + NP)
                if not (isinstance(t, int) and t == 0):
                    v.wait_ge(s_mask, t)
                v.tensor_scalar(count1[:, :], PS[:, 6, 0:KEYS0], 1.0, None, ALU.max).then_inc(s_c1, 1)
                v.tensor_scalar(never[:, :], PS[:, 6, 0:KEYS0], 0.5, NEVER, ALU.is_lt, ALU.mult)\
                    .then_inc(s_nv, 1)

            def make_mask(t, u):
                v.wait_ge(s_log, t + 1)
                v.wait_ge(s_nv, t + 1)
                v.scalar_tensor_tensor(mask[:, u, :], logc[:, :], 1.0 / SCALE0, never[:, :],
                                       ALU.mult, ALU.add).then_inc(s_mask, 1)

            def max0(t, u, hp, more, between=None):
                n = 8 * t + hp
                if hp == 0:
                    v.wait_ge(s_mask, t + 1)
                v.wait_ge(s_s0, n + 1)
                if not (isinstance(n, int) and n < 2):
                    v.wait_ge(s_p0, n - 1)
                if more and hp < NP:
                    picks(t + 1, hp)
                if more and hp == NP:
                    read_counts(t + 1)
                if more and hp == NP + 1:
                    make_mask(t + 1, 1 - u)
                if between is not None:
                    between()
                for r in range(2):
                    last = v.tensor_tensor_reduce(T0[:, hp % 2, r, :],
                                                  PS[:, hp % 2, r * KEYS0:(r + 1) * KEYS0],
                                                  mask[:, u, :], SCALE0, -3e38, ALU.add, ALU.max,
                                                  mx0[:, 2 * hp + r:2 * hp + r + 1])
                last.then_inc(s_t0, 1)
                v.wait_ge(s_t0, n + 1)
                v.tensor_scalar(nb0[:, 2 * hp:2 * hp + 2], mx0[:, 2 * hp:2 * hp + 2], -1.0, None,
                                ALU.mult).then_inc(s_nb, 1)

            def norm0(t, u, half):
                v.wait_ge(s_p0, 8 * t + 4 * half + 4)
                v.reciprocal(rec0[:, 8 * half:8 * half + 8], sum0[:, u, 8 * half:8 * half + 8])\
                    .then_inc(s_rec, 1)
                v.wait_ge(s_rec, 2 * t + half + 1)
                v.wait_ge(s_o0, 8 * t + 4 * half + 4)
                if half == 0 and not (isinstance(t, int) and t == 0):
                    v.wait_ge(s_ot, t)
                own = PS[:, 4:6, :].rearrange("p b n -> p (b n)")
                own = bass.AP(own.tensor, own.offset + 64 * half, [own.ap[0], [P + HD0, 8], [1, HD0]])
                v.tensor_tensor(O0[:, 8 * half:8 * half + 8, :], own,
                                rec0[:, 8 * half:8 * half + 8].rearrange("p (h o) -> p h o", o=1)
                                .to_broadcast([P, 8, HD0]), ALU.mult).then_inc(s_on0, 1)

            def add0(t):
                v.wait_ge(s_y0, t + 1)
                xt = X[:, bass.ds(t, 1), :].rearrange("p o n -> p (o n)")
                v.scalar_tensor_tensor(xt, PS[:, 7, P:2 * P], gate[:, 0:1], xt, ALU.mult, ALU.add)\
                    .then_inc(s_x0, 1)

            def attend0(t, u, first=False, last=False):
                for hp in range(8):
                    if hp == 1 and not first:
                        max0(t, u, hp, not last, lambda: norm0(t - 1, 1 - u, 1))
                    else:
                        max0(t, u, hp, not last)
                    if hp == 3 and not first:
                        add0(t - 1)
                    if hp == 5:
                        norm0(t, u, 0)

            read_counts(0)
            make_mask(0, 0)
            v.wait_ge(s_rrow, 1)
            v.tensor_reduce(flagrow[0:1, 0:1], PS[0:1, 7, 0:P], AX.X, ALU.max).then_inc(g_step, 1)
            v.wait_ge(g_step, 3)
            v.tensor_scalar(flagrow[0:1, 1:2], flagrow[0:1, 0:1], KEYS0 - 0.5, None, ALU.is_gt)\
                .then_inc(g_step, 1)
            v.wait_ge(g_step, 4)
            v.tensor_copy(flag[0:1, 0:1], flagrow[0:1, 1:2]).then_inc(s_flag, 1)
            v.wait_ge(s_tanh, 1)
            attend0(0, 0, first=True)
            attend0(1, 1)
            attend0(2, 0)
            with v.Fori(1, NT // 2 - 1) as j:
                attend0(2 * j + 1, 1)
                attend0(2 * j + 2, 0)
            attend0(NT - 1, 1, last=True)
            norm0(NT - 1, 1, 1)
            add0(NT - 1)

            SO_FAR = 7
            TILE_STEPS, BLOCK_STEPS, END_STEPS = 3, 10, 1
            PER_TILE = TILE_STEPS + BLOCKS * BLOCK_STEPS + END_STEPS

            def done(ins, count):
                ins.then_inc(g_step, 1)
                v.wait_ge(g_step, count)

            def true_picks():
                done(v.tensor_scalar(away[:, :, :], idxf[:, :, :], 0.0, float(SKV), ALU.is_lt,
                                     ALU.mult), 5)
                done(v.tensor_tensor(idxf[:, :, :], idxf[:, :, :], away[:, :, :], ALU.add), 6)
                done(v.tensor_scalar(idxf[:, :, :], idxf[:, :, :], SKV - 1.0, 0.0, ALU.min,
                                     ALU.max), 7)
                v.wait_ge(g_xl, 16)

            def tile_start(t):
                masked_q(v, t, 0).then_inc(g_qm, 1)
                v.tensor_scalar(gbest[:, 1, :], mx0[:, :], 0.0, -3e38, ALU.mult, ALU.add)
                v.memset(gsum[:, :], 0.0).then_inc(g_step, 1)
                v.memset(gacc[:, :, :], 0.0).then_inc(g_step, 1)
                v.tensor_scalar(gidx[:, :], idxf[:, bass.ds(t, 1), :].rearrange("p o k -> p (o k)"),
                                float(KEYS0), None, ALU.add).then_inc(g_step, 1)

            def block(b, t, j, n):
                base = t * PER_TILE + SO_FAR + TILE_STEPS + j * BLOCK_STEPS
                v.wait_ge(g_step, base)
                v.tensor_scalar(gidx[:, :], gidx[:, :], float(KEYS0), None, ALU.subtract)\
                    .then_inc(g_go, 1)
                v.wait_ge(g_go, n + 1)
                for k in range(PICK):
                    last = v.tensor_scalar(onehot[:, k, :], iota[:, :], gidx[:, k:k + 1], None,
                                           ALU.is_equal)
                last.then_inc(g_oh, 1)
                v.wait_ge(g_kvs, n + 1)
                for half in range(2):
                    high = K0[:, 2 * half:2 * half + 2, 0:KEYS0]
                    last = v.scalar_tensor_tensor(high, high.bitcast(F32), sel[:, GH:GH + 1],
                                                  PS[:, 2 + half, :]
                                                  .rearrange("p (g k) -> p g k", g=2),
                                                  ALU.mult, ALU.add)
                last.then_inc(g_kl, 1)
                v.wait_ge(g_cnt, n + 1)
                v.tensor_scalar(count1[:, :], PS[:, 6, 0:KEYS0], 1.0, None, ALU.max).then_inc(g_c1, 1)
                v.tensor_scalar(never[:, :], PS[:, 6, 0:KEYS0], 0.5, NEVER, ALU.is_lt, ALU.mult)\
                    .then_inc(g_nv, 1)
                v.wait_ge(g_log, n + 1)
                v.wait_ge(g_nv, n + 1)
                v.scalar_tensor_tensor(mask[:, 0, :], logc[:, :], 1.0 / SCALE0, never[:, :],
                                       ALU.mult, ALU.add).then_inc(g_mask, 1)
                v.wait_ge(g_mask, n + 1)
                for hp in range(8):
                    v.wait_ge(g_s, 8 * n + hp + 1)
                    v.tensor_tensor(ALLP[:, 2 * hp:2 * hp + 2, :],
                                    PS[:, 0, :].rearrange("p (r k) -> p r k", k=KEYS0),
                                    mask[:, 0:1, :].to_broadcast([P, 2, KEYS0]), ALU.add)\
                        .then_inc(g_t, 1)
                v.wait_ge(g_t, 8 * n + 8)
                done(v.tensor_scalar(ALLP[:, :, :], ALLP[:, :, :], SCALE0, None, ALU.mult), base + 1)
                done(v.tensor_reduce(mx0[:, :], ALLP[:, :, :], AX.X, ALU.max), base + 2)
                done(v.tensor_tensor(gbest[:, 0, :], mx0[:, :], gbest[:, 1, :], ALU.max), base + 3)
                v.tensor_scalar(gneg[:, :], gbest[:, 0, :], -1.0, None, ALU.mult).then_inc(g_step, 1)
                done(v.tensor_tensor(gshrink[:, 0, :], gbest[:, 1, :], gbest[:, 0, :], ALU.subtract),
                     base + 5)
                v.tensor_copy(gbest[:, 1, :], gbest[:, 0, :]).then_inc(g_best, 1)
                v.wait_ge(g_best, n + 1)
                v.wait_ge(g_shr, n + 1)
                v.wait_ge(g_p, n + 1)
                v.wait_ge(g_o, 8 * n + 8)
                for half in range(2):
                    own = PS[:, 2 + 2 * half:4 + 2 * half, :].rearrange("p b n -> p (b n)")
                    own = bass.AP(own.tensor, own.offset + 64 * half,
                                  [own.ap[0], [P + HD0, 8], [1, HD0]])
                    last = v.tensor_copy(gown[:, 8 * half:8 * half + 8, :], own)
                last.then_inc(g_step, 1)
                done(v.tensor_tensor(gacc[:, :, :], gacc[:, :, :],
                                     gshrink[:, 1, :].rearrange("p (h o) -> p h o", o=1)
                                     .to_broadcast([P, H0, HD0]), ALU.mult), base + 7)
                v.tensor_tensor(gacc[:, :, :], gacc[:, :, :], gown[:, :, :], ALU.add)\
                    .then_inc(g_step, 1)
                done(v.tensor_tensor(gsum[:, :], gsum[:, :], gshrink[:, 1, :], ALU.mult), base + 9)
                v.tensor_tensor(gsum[:, :], gsum[:, :], gpart[:, :], ALU.add).then_inc(g_step, 1)

            def tile_end(t):
                base = t * PER_TILE + SO_FAR + PER_TILE
                v.wait_ge(g_step, base - 1)
                done(v.reciprocal(rec0[:, :], gsum[:, :]), base)
                v.tensor_tensor(O0[:, :, :], gacc[:, :, :],
                                rec0[:, :].rearrange("p (h o) -> p h o", o=1)
                                .to_broadcast([P, H0, HD0]), ALU.mult).then_inc(g_norm, 1)
                v.wait_ge(g_y, t + 1)
                xt = X[:, bass.ds(t, 1), :].rearrange("p o n -> p (o n)")
                v.scalar_tensor_tensor(xt, PS[:, 7, P:2 * P], gate[:, 0:1], xt, ALU.mult, ALU.add)\
                    .then_inc(g_x, 1)

            v.wait_ge(s_x0, NT)
            all_blocks(v, true_picks, tile_start, block, tile_end, lambda: v.wait_ge(g_x, NT))

            ln_vector(v, 1, X, XN)
            v.wait_ge(s_ff, 16 * 7)

            links = []

            def chain(ins):
                links.append(1)
                ins.then_inc(s_dv2, 1)
                v.wait_ge(s_dv2, len(links))

            def reduce_angle(dst, src, tmp):
                chain(v.tensor_scalar(tmp, src, 1 / (2 * PI), MAGIC, ALU.mult, ALU.add))
                chain(v.tensor_scalar(tmp, tmp, MAGIC, None, ALU.subtract))
                chain(v.scalar_tensor_tensor(dst, tmp, -TWO_PI_HI, src, ALU.mult, ALU.add))
                chain(v.scalar_tensor_tensor(dst, tmp, -TWO_PI_LO, dst, ALU.mult, ALU.add))

            reduce_angle(trig[:, 1, :], fcol[:, 1, :], trig[:, 0, :])
            chain(v.tensor_scalar(trig[:, 3, :], trig[:, 1, :], PI / 2, None, ALU.add))
            chain(v.tensor_scalar(trig[:, 0, :], trig[:, 3, :], PI, -2 * PI, ALU.is_gt, ALU.mult))
            chain(v.tensor_tensor(trig[:, 3, :], trig[:, 3, :], trig[:, 0, :], ALU.add))
            v.tensor_scalar(trig[:, 3, :], trig[:, 3, :], PI_DOWN, -PI_DOWN, ALU.min, ALU.max)\
                .then_inc(s_th, 1)
            v.tensor_scalar(trig[:, 2, :], trig[:, 1, :], PI_DOWN, -PI_DOWN, ALU.min, ALU.max)\
                .then_inc(s_th, 1)
            v.scalar_tensor_tensor(trig[:, 8, :], fcol[:, 0, :], 0.1, trig[:, 1, :], ALU.mult, ALU.add)\
                .then_inc(s_th, 1)
            v.wait_ge(s_ths, 1)
            chain(v.tensor_tensor(trig[:, 0, :], trig[:, 5, :], fcol[:, 2, :], ALU.mult))
            chain(v.tensor_tensor(trig[:, 7, :], trig[:, 4, :], fcol[:, 3, :], ALU.mult))
            chain(v.tensor_tensor(trig[:, 0, :], trig[:, 0, :], trig[:, 7, :], ALU.add))
            chain(v.tensor_tensor(trig[:, 0, :], trig[:, 0, :], fcol[:, 3, :], ALU.mult))
            chain(v.tensor_scalar(trig[:, 6, :], trig[:, 0, :], 0.1, None, ALU.mult))

            for n in range(9):
                if n < 8:
                    v.wait_ge(s_hid, 2 * n + 2)
                    arg, tmp = ff[:, n % 3, 1, :], ff[:, n % 3, 4, :]
                    chain(v.tensor_scalar(tmp, arg, 1 / (2 * PI), MAGIC, ALU.mult, ALU.add))
                    chain(v.tensor_scalar(tmp, tmp, MAGIC, None, ALU.subtract))
                    chain(v.scalar_tensor_tensor(arg, tmp, -TWO_PI_HI, arg, ALU.mult, ALU.add))
                    v.scalar_tensor_tensor(arg, tmp, -TWO_PI_LO, arg, ALU.mult, ALU.add)\
                        .then_inc(s_red, 1)
                if n:
                    m = n - 1
                    v.wait_ge(s_red, m + 1)
                    v.wait_ge(s_sin, m + 1)
                    v.scalar_tensor_tensor(ff[:, m % 3, 4, :], ff[:, m % 3, 3, :],
                                           trig[:, 6, m // 2:m // 2 + 1], ff[:, m % 3, 0, :],
                                           ALU.mult, ALU.add).then_inc(s_q, 1)
            v.wait_ge(s_wi, 16 * 3)
            v.tensor_scalar(wf[:, :], wi[:, :], 1.0 / 127.0, None, ALU.mult).then_inc(s_wf, 1)

            def add_ffn(n, g, bias, base):
                y = PS[:, base + n % 2, :].rearrange("p (t d) -> p t d", d=P)
                v.wait_ge(s_fy, n + 1)
                if bias:
                    v.tensor_tensor(yb[:, n, :, :], y, B2[:, :].rearrange("p (o d) -> p o d", o=1)
                                    .to_broadcast([P, 4, P]), ALU.add).then_inc(s_yb, 1)
                    v.wait_ge(s_yb, n + 1)
                    y = yb[:, n, :, :]
                xs = X[:, 4 * (n % 2):4 * (n % 2) + 4, :]
                v.scalar_tensor_tensor(xs, y, gate[:, g:g + 1], xs, ALU.mult, ALU.add)\
                    .then_inc(s_x0, 4)

            for n in range(2):
                add_ffn(n, 2, True, 2)
            v.wait_ge(s_x0, 2 * NT)
            ln_vector(v, 2, X, XN)
            v.wait_ge(s_row, 16 * 3)
            v.wait_ge(s_xn, 3 * NT)
            v.tensor_tensor(Y[:, :, :], XN[:, :, :], rowv[:, 0:1, :].to_broadcast([P, NT, P]), ALU.add)\
                .then_inc(s_yi, 1)
            v.wait_ge(s_ones, 5)
            v.wait_ge(s_yi, 1)

            def side(s, u):
                def q():
                    v.wait_ge(s_qh, s + 1)
                    for h in range(2):
                        last = v.scalar_tensor_tensor(
                            QA[HD1:P, u, h, :], PS[HD1 * h:HD1 * h + HD1, 6, 0:SQ],
                            WP[HD1 * h:HD1 * h + HD1, u, 3 * P:3 * P + 1],
                            QA[0:HD1, u, h, :].bitcast(F32), ALU.add, ALU.subtract)
                    last.then_inc(s_ql, 1)

                def k(c):
                    def go():
                        v.wait_ge(s_kh, NC * s + c + 1)
                        k0, n = CHUNK[c]
                        for h in range(2):
                            last = v.scalar_tensor_tensor(
                                KB[0:HD1, u, h, k0:k0 + n], PS[HD1 * h:HD1 * h + HD1, 7 - c % 2, 0:n],
                                WP[HD1 * h:HD1 * h + HD1, u, 3 * P + 1:3 * P + 2],
                                KA[0:HD1, u, h, k0:k0 + n].bitcast(F32), ALU.add, ALU.subtract)
                        last.then_inc(s_kl, 1)
                    return go

                def low(g):
                    def go():
                        v.wait_ge(s_vs, VG * s + g + 1)
                        k0, k1 = 4 * g, min(4 * g + 4, NK)
                        n = TK if k1 < NK else LASTK
                        v.tensor_tensor(VL[0:n, u, k0:k1, :, 0:HD1],
                                        PS[0:n, 6 + g % 2, 0:(k1 - k0) * P]
                                        .rearrange("p (k h d) -> p k h d", h=2, d=HD1),
                                        VH[0:n, u, k0:k1, :, 0:HD1].bitcast(F32), ALU.subtract)\
                            .then_inc(s_vl, 1)
                    return go

                def m(n):
                    def go():
                        if n == 0 and not (isinstance(s, int) and s == 0):
                            v.wait_ge(s_nm, s)
                        v.wait_ge(s_ms, 16 * s + n + 1)
                        cols = CHUNK[n // NC][1]
                        v.tensor_reduce(negpart[:, n % NC, n // NC:n // NC + 1],
                                        PS[:, n % 2, 0:cols], AX.X, ALU.max, negate=True)\
                            .then_inc(s_mr, 1)
                    return go

                def split():
                    v.wait_ge(s_mr, 16 * s + 16)
                    if not (isinstance(s, int) and s == 0):
                        v.wait_ge(s_nl, s)
                        v.wait_ge(s_nt, s)
                    v.tensor_reduce(negmax[:, :], negpart[:, :, :], AX.X, ALU.min).then_inc(s_nm, 1)
                    v.wait_ge(s_nm, s + 1)
                    v.tensor_copy(neghi[:, :], negmax[:, :]).then_inc(s_nh, 1)
                    v.wait_ge(s_nh, s + 1)
                    v.tensor_copy(negsplit[:, :, 0], neghi[:, :].bitcast(F32))
                    v.tensor_tensor(negsplit[:, :, 1], negmax[:, :], neghi[:, :].bitcast(F32),
                                    ALU.subtract).then_inc(s_nl, 1)

                def store():
                    v.wait_ge(s_nt, s + 1)
                    for h in range(2):
                        last = v.tensor_copy(QB[HD1:HD1 + 2, u, h, :], PS[0:2, 0, h * SQ:(h + 1) * SQ])
                    last.then_inc(s_nq, 1)
                return q, k, low, m, split, store

            def copy_sums(i, u):
                v.wait_ge(s_pvl, NK * i + NK)
                if not (isinstance(i, int) and i == 0):
                    v.wait_ge(s_rc, i)
                for h in range(2):
                    last = v.tensor_copy(sums[HD1 * (1 - h):HD1 * (2 - h), :],
                                         PS[HD1:P, 4 + u, h * SQ:(h + 1) * SQ])
                last.then_inc(s_su, 1)

            def recip_sums(i, u):
                v.wait_ge(s_su, i + 1)
                if not (isinstance(i, int) and i == 0):
                    v.wait_ge(s_nr, i)
                v.reciprocal(recip[:, :], sums[:, :]).then_inc(s_rc, 1)

            def normalise(i, u):
                v.wait_ge(s_rc, i + 1)
                if not (isinstance(i, int) and i == 0):
                    v.wait_ge(s_bv, i)
                for h in range(2):
                    last = v.tensor_tensor(ONR[HD1 * h:HD1 * h + HD1, :],
                                           PS[0:HD1, 4 + u, h * SQ:(h + 1) * SQ],
                                           recip[HD1 * (1 - h):HD1 * (2 - h), :], ALU.mult)
                last.then_inc(s_nr, 1)

            def add_pair(i, b):
                v.wait_ge(s_po, i + 1)
                if not (isinstance(i, int) and i == 0):
                    v.wait_ge(s_ya, i)
                y = Y[:, bass.ds(b * QT, QT), :].rearrange("p t d -> p (t d)")
                v.tensor_tensor(y, y, PS[:, 7, 0:QT * P], ALU.add).then_inc(s_ya, 1)

            def step(i, u, b_prev, first=False, last=False):
                work = {}
                if not first:
                    work |= {"sums": lambda: copy_sums(i - 1, 1 - u),
                             "recip": lambda: recip_sums(i - 1, 1 - u),
                             "norm": lambda: normalise(i - 1, 1 - u),
                             "pair": lambda: add_pair(i - 1, b_prev)}
                if not last:
                    q, k, low, m, split, store = side(i + 1, 1 - u)
                    work |= {"q": q, "split": split, "store": store}
                    work |= {f"k{c}": k(c) for c in range(NC)}
                    work |= {f"v{g}": low(g) for g in range(VG)}
                    work |= {f"m{n}": m(n) for n in range(NC * 2 * QT)}
                for name in DVE_ORDER:
                    if name in work:
                        work[name]()

            q, k, low, m, split, store = side(0, 0)
            q()
            for c in range(NC):
                k(c)()
            for g in range(VG):
                low(g)()
            for n in range(16):
                m(n)()
            split()
            store()
            step(0, 0, 0, first=True)
            step(1, 1, 0)
            step(2, 0, 0)
            with v.Fori(1, PAIRS // 2) as j:
                step(2 * j + 1, 1, 0)
                step(2 * j + 2, 0, 0)
            with v.Fori(1, B - 1) as b:
                with v.Fori(0, PAIRS // 2) as j:
                    step(PAIRS * b + 2 * j + 1, 1, b)
                    step(PAIRS * b + 2 * j + 2, 0, b)
            with v.Fori(0, PAIRS // 2 - 1) as j:
                step(PAIRS * (B - 1) + 2 * j + 1, 1, B - 1)
                step(PAIRS * (B - 1) + 2 * j + 2, 0, B - 1)
            v.wait_ge(s_ya, IT // 2)
            ln_moments(v, 3, Y)
            step(IT - 1, 1, B - 1, last=True)
            copy_sums(IT - 1, 1)
            recip_sums(IT - 1, 1)
            normalise(IT - 1, 1)

            def gated(half):
                ts, h = HALVES[half], half + 1
                y, xs = Y[:, ts[0]:ts[-1] + 1, :], X[:, ts[0]:ts[-1] + 1, :]
                ln_apply(v, 3 + 2 * half, Y, Y)
                v.wait_ge(s_xn, LN_BEFORE[4 + 2 * half])
                v.tensor_tensor(y, y, rowv[:, 1:2, :].to_broadcast([P, len(ts), P]), ALU.mult)\
                    .then_inc(s_yl, 1)
                v.wait_ge(s_yl, h)
                v.tensor_tensor(y, y, rowv[:, 2:3, :].to_broadcast([P, len(ts), P]), ALU.add)\
                    .then_inc(s_yg, 1)
                v.wait_ge(s_yg, h)
                v.scalar_tensor_tensor(xs, y, gate[:, 1:2], xs, ALU.mult, ALU.add)\
                    .then_inc(s_x0, len(ts))
                v.wait_ge(s_x0, 2 * NT + len(ts) * h)

            gated(0)
            ln_moments(v, 4, X)
            add_pair(IT - 1, B - 1)
            ln_apply(v, 4, X, XN)
            v.wait_ge(s_ya, IT)
            ln_moments(v, 5, Y)
            gated(1)
            ln_vector(v, 6, X, XN)
            for n in range(2 * FC1):
                v.wait_ge(s_gs, n + 1)
                half, c = n // FC1, n % FC1
                v.tensor_tensor(AT[:, c, 512 * half:512 * half + 512], ff[:, n % 2, 0, :],
                                PS[:, 2 + n % 2, :], ALU.mult).then_inc(s_ht, 1)
            for n in range(2, 4):
                add_ffn(n, 3, False, 4)


def kernel(**inputs):
    import numpy as _np
    import concourse.bacc as _bacc
    from concourse import mybir as _mybir
    from concourse.bass_utils import run_bass_kernel_spmd as _run

    g = {k: _np.asarray(v) for k, v in inputs.items()}
    ctxT = g["ctx_1024"].transpose(0, 2, 1)
    pair = lambda w: w.reshape(P, PAIRS, P).transpose(1, 0, 2)
    cols = lambda v: v.reshape(PAIRS, P, 1)
    four = lambda w: _np.tile(w.reshape(P, GROUPS, 1, GW), (1, 1, P // GW, 1)).reshape(P, GROUPS, P)
    row = _np.arange(P)
    select = _np.stack([*(row % GW // HD0 == h for h in range(GH)),
                        -1.0 * (row >= P // 2), -1.0 * (row // GW % 2)], axis=1).astype(_np.float32)
    arrays = {
        "x": g["x"].reshape(ROWS, P),
        "ctxT": _np.concatenate([ctxT, ctxT[:, :, -1:]], axis=2),
        "ctx0": _np.concatenate([ctxT, _np.zeros((B, P, BLOCKS * KEYS0 - SKV), ctxT.dtype)], axis=2),
        "idx": g["itok_BxSx64_0_2047"].reshape(ROWS, PICK),
        "gates": _np.concatenate([g["g_xattn"], g["g_ffn"]]),
        "wq4": four(g["L0_xattn_W_q"].T), "wk4": four(g["L0_xattn_W_kv_up"][:P].T),
        "select": select, "wdT": g["L0_xattn_W_kv_down"].T,
        "wvT": g["L0_xattn_W_kv_up"][P:].T, "woT": g["L0_xattn_W_out"].T,
        "w1": g["L0_ffn_W1"], "b1": g["L0_ffn_b1"].reshape(FC0, P).T,
        "theta": g["L0_ffn_quantum_phases"].reshape(FC0, P).T,
        "wre": g["L0_ffn_quantum_weights_real"].reshape(FC0, P).T,
        "wim": g["L0_ffn_quantum_weights_imag"].reshape(FC0, P).T,
        "w2": g["L0_ffn_W2"], "b2": g["L0_ffn_b2"],
        "wqkv": _np.concatenate([pair(g["L1_xattn_Wq"]), pair(g["L1_xattn_Wk"]),
                                 pair(g["L1_xattn_Wv"]), cols(g["L1_xattn_bq"]),
                                 cols(g["L1_xattn_bk"])], axis=2),
        "wout": _np.concatenate([g["L1_xattn_Wo"].reshape(PAIRS, P, P), cols(g["L1_xattn_bv"])],
                                axis=2),
        "bo": g["L1_xattn_bo"], "gamma": g["L1_xattn_ln_gamma"], "beta": g["L1_xattn_ln_beta"],
        "wgT": g["L1_ffn_w_gate"].T, "wupT": g["L1_ffn_w_up"].T,
        "wdnT": g["L1_ffn_w_down"].reshape(P, FC1, P).transpose(2, 1, 0).reshape(P, FC1 * P),
    }
    arrays = {k: _np.ascontiguousarray(v) for k, v in arrays.items()}
    nc = _bacc.Bacc("TRN2", target_bir_lowering=False, num_devices=1)
    args = [nc.dram_tensor(f"in_{k}", a.shape, _mybir.dt.from_np(a.dtype), kind="ExternalInput").ap()
            for k, a in arrays.items()]
    out = nc.dram_tensor("out_0", (ROWS, P), F32, kind="ExternalOutput").ap()
    program(nc, *args, out)
    r = _run(nc, [{f"in_{k}": a for k, a in arrays.items()}], core_ids=[0])
    return r.results[0]["out_0"].reshape(B, SQ, P)
```
